# Optimizing a Trainium2 kernel written in Bass

```python
import numpy as np
import jax
import jax.numpy as jnp

def _softmax(x, axis=-1):
    return jax.nn.softmax(x, axis=axis)

def _gelu(x):
    return jax.nn.gelu(x, approximate=True)

def _silu(x):
    return jax.nn.silu(x)

def _sigmoid(x):
    return jax.nn.sigmoid(x)

def _layernorm(x, axis=-1, eps=1e-05):
    m = jnp.mean(x, axis=axis, keepdims=True)
    v = jnp.var(x, axis=axis, keepdims=True)
    return (x - m) / jnp.sqrt(v + eps)

def _scatter_add(tgt, idx, src, axis=0):
    return tgt.at[idx].add(src)

def _segment_sum(src, seg, n):
    return jax.ops.segment_sum(src, seg, n)
kernel_name = 'mk_cond_seq_d4_seqx_r4_a05c5b'

def setup_inputs(seed: int=0):
    np.random.seed(seed)
    _w = jnp.asarray

    def _rec_inputs():
        import jax
        import jax.numpy as jnp
        _rk = jax.random.key(seed)
        x = 7.22e-05 + 1 * jax.random.normal(jax.random.fold_in(_rk, 1), (4, 512, 512), jnp.float32)
        _lenS = 512 - jax.random.randint(jax.random.fold_in(_rk, 7), (4,), 0, max(1, 512 // 4) + 1, jnp.int32)
        _lenS2 = 512 - jax.random.randint(jax.random.fold_in(_rk, 8), (4,), 0, max(1, 512 // 4) + 1, jnp.int32)
        cond_2048 = 0.0061147 + 1.02565 * jax.random.normal(jax.random.fold_in(_rk, 11), (4, 512), jnp.float32)
        pos_BxS = jnp.broadcast_to(jnp.arange(512, dtype=jnp.int32), (4, 512))
        _validS = jnp.arange(512)[None, :] < _lenS[:, None]
        _validS2 = jnp.arange(512)[None, :] < _lenS2[:, None]
        _causal = jnp.tril(jnp.ones((512, 512), dtype=bool))
        mask_1x1xSxS_ff0 = jnp.where(jnp.ones((1, 1, 512, 512), dtype=bool), 0.0, -1000000000.0).astype(jnp.float32)
        return (x, cond_2048, pos_BxS, mask_1x1xSxS_ff0)
    x, cond_2048, pos_BxS, mask_1x1xSxS_ff0 = _rec_inputs()

    def _L0_cond_setup():
        import jax, jax.numpy as jnp
        import numpy as np
        D_MODEL = 512
        N_HEADS = 16
        N_KV_HEADS = 4
        HEAD_DIM = D_MODEL // N_HEADS
        N_GROUPS = N_HEADS // N_KV_HEADS
        BLOCK_SIZE = 128
        WINDOW = 64
        GLOBAL_EVERY = 64
        LATENT = 128
        ROPE_THETA = 10000.0
        LN_EPS = 1e-05

        def _rope_tables(T, dtype):
            freqs = 1.0 / ROPE_THETA ** (jnp.arange(0, HEAD_DIM, 2, dtype=jnp.float32) / HEAD_DIM)
            emb = jnp.arange(T, dtype=jnp.float32)[:, None] * freqs[None, :]
            cos = jnp.concatenate([jnp.cos(emb), jnp.cos(emb)], axis=-1).astype(dtype)
            sin = jnp.concatenate([jnp.sin(emb), jnp.sin(emb)], axis=-1).astype(dtype)
            return (cos, sin)

        def _rotate_half(x):
            h = x.shape[-1] // 2
            return jnp.concatenate([-x[..., h:], x[..., :h]], axis=-1)

        def _sparse_mask(T):
            idx = jnp.arange(T)
            blk = idx // BLOCK_SIZE
            future_block = blk[None, :] > blk[:, None]
            outside_window = jnp.abs(idx[None, :] - idx[:, None]) > WINDOW
            global_visible = jnp.broadcast_to((idx % GLOBAL_EVERY == 0)[None, :], (T, T))
            return outside_window & ~global_visible | future_block
        key = jax.random.key(seed)
        ks = jax.random.split(key, 9)
        B, T = (2, 512)
        s = 0.02
        return {'x': jax.random.normal(ks[0], (B, T, D_MODEL), jnp.float32), 't_emb': jax.random.normal(ks[1], (B, D_MODEL), jnp.float32), 'W_ada': jax.random.normal(ks[2], (2 * D_MODEL, D_MODEL), jnp.float32) * s, 'b_ada': jnp.zeros((2 * D_MODEL,), jnp.float32), 'Wq': jax.random.normal(ks[3], (N_HEADS * HEAD_DIM, D_MODEL), jnp.float32) * s, 'Wkd': jax.random.normal(ks[4], (LATENT, D_MODEL), jnp.float32) * s, 'Wku': jax.random.normal(ks[5], (N_KV_HEADS * HEAD_DIM, LATENT), jnp.float32) * s, 'Wvu': jax.random.normal(ks[6], (N_KV_HEADS * HEAD_DIM, LATENT), jnp.float32) * s, 'Wo': jax.random.normal(ks[7], (D_MODEL, N_HEADS * HEAD_DIM), jnp.float32) * s}
    _L0_cond_all = _L0_cond_setup()
    _L0_cond_in = {k: v for k, v in _L0_cond_all.items() if k in ('W_ada', 'b_ada', 'Wq', 'Wkd', 'Wku', 'Wvu', 'Wo')}
    del _L0_cond_all

    def _L1_cond_setup():
        import jax, jax.numpy as jnp
        import numpy as np
        HIDDEN, NQ, NKV, HD, INTER = (512, 8, 1, 64, 2048)
        B, S = (4, 512)
        EPS = 1e-06
        ROPE_BASE = 10000.0

        def ada_rms(x, t, w, tw):
            n = x * jax.lax.rsqrt(jnp.mean(jnp.square(x), axis=-1, keepdims=True) + EPS)
            scale = t @ tw.T
            return n * (w * (1.0 + scale))[:, None, :]

        def apply_rope(x, pos_ids):
            half = HD // 2
            inv_freq = 1.0 / ROPE_BASE ** (jnp.arange(0, HD, 2, dtype=jnp.float32) / HD)
            ang = pos_ids.astype(jnp.float32)[:, :, None] * inv_freq
            cos = jnp.concatenate([jnp.cos(ang), jnp.cos(ang)], axis=-1)[:, None]
            sin = jnp.concatenate([jnp.sin(ang), jnp.sin(ang)], axis=-1)[:, None]
            x1, x2 = (x[..., :half], x[..., half:])
            rot = jnp.concatenate([-x2, x1], axis=-1)
            return x * cos + rot * sin
        key = jax.random.key(seed)
        ks = jax.random.split(key, 12)
        f32 = jnp.float32
        inp = {'x': jax.random.normal(ks[0], (B, S, HIDDEN), f32), 'pos_ids': jnp.broadcast_to(jnp.arange(S, dtype=jnp.int32), (B, S)), 'time_emb': jax.random.normal(ks[1], (B, HIDDEN), f32), 'ln1_w': jnp.ones((HIDDEN,), f32), 'ln1_tw': jax.random.normal(ks[2], (HIDDEN, HIDDEN), f32) * 0.02, 'ln2_w': jnp.ones((HIDDEN,), f32), 'ln2_tw': jax.random.normal(ks[3], (HIDDEN, HIDDEN), f32) * 0.02, 'Wq': jax.random.normal(ks[4], (NQ * HD, HIDDEN), f32) * 0.02, 'Wk': jax.random.normal(ks[5], (NKV * HD, HIDDEN), f32) * 0.02, 'Wv': jax.random.normal(ks[6], (NKV * HD, HIDDEN), f32) * 0.02, 'Wo': jax.random.normal(ks[7], (HIDDEN, NQ * HD), f32) * 0.02, 'Wg': jax.random.normal(ks[8], (INTER, HIDDEN), f32) * 0.02, 'Wu': jax.random.normal(ks[9], (INTER, HIDDEN), f32) * 0.02, 'Wd': jax.random.normal(ks[10], (HIDDEN, INTER), f32) * 0.02}
        return inp
    _L1_cond_all = _L1_cond_setup()
    _L1_cond_in = {k: v for k, v in _L1_cond_all.items() if k in ('ln1_w', 'ln1_tw', 'ln2_w', 'ln2_tw', 'Wq', 'Wk', 'Wv', 'Wo', 'Wg', 'Wu', 'Wd')}
    del _L1_cond_all

    def _L2_cond_setup():
        import jax, jax.numpy as jnp
        import numpy as np
        B, L, C, H = (2, 512, 512, 16)
        COND = 512
        HID = 4 * C
        LN_EPS = 1e-06

        def _ln(x):
            m = jnp.mean(x, axis=-1, keepdims=True)
            v = jnp.mean((x - m) ** 2, axis=-1, keepdims=True)
            return (x - m) / jnp.sqrt(v + LN_EPS)

        def _gelu_tanh(u):
            c = np.sqrt(2.0 / np.pi).astype(np.float32)
            return 0.5 * u * (1.0 + jnp.tanh(c * (u + 0.044715 * u ** 3)))
        key = jax.random.key(seed)
        ks = jax.random.split(key, 8)
        s = 0.02
        return {'x': jax.random.normal(ks[0], (B, L, C), jnp.float32), 'cond_BD': jax.random.normal(ks[1], (B, COND), jnp.float32), 'attn_bias': jnp.zeros((1, 1, L, L), jnp.float32), 'Wqkv': jax.random.normal(ks[2], (3 * C, C), jnp.float32) * s, 'q_bias': jnp.zeros((C,), jnp.float32), 'v_bias': jnp.zeros((C,), jnp.float32), 'scale_mul_log': jnp.full((1, H, 1, 1), np.log(4.0), jnp.float32), 'Wproj': jax.random.normal(ks[3], (C, C), jnp.float32) * s, 'bproj': jnp.zeros((C,), jnp.float32), 'Wada': jax.random.normal(ks[4], (6 * C, COND), jnp.float32) * s, 'bada': jnp.zeros((6 * C,), jnp.float32), 'Wfc1': jax.random.normal(ks[5], (HID, C), jnp.float32) * s, 'bfc1': jnp.zeros((HID,), jnp.float32), 'Wfc2': jax.random.normal(ks[6], (C, HID), jnp.float32) * s, 'bfc2': jnp.zeros((C,), jnp.float32)}
    _L2_cond_all = _L2_cond_setup()
    _L2_cond_in = {k: v for k, v in _L2_cond_all.items() if k in ('Wqkv', 'q_bias', 'v_bias', 'scale_mul_log', 'Wproj', 'bproj', 'Wada', 'bada', 'Wfc1', 'bfc1', 'Wfc2', 'bfc2')}
    del _L2_cond_all

    def _L3_cond_setup():
        import jax, jax.numpy as jnp
        import numpy as np
        B, T, LATENT, FFN, TEMB = (4, 1024, 64, 256, 512)
        D = 8 * LATENT
        LN_EPS = 1e-05

        def _layernorm(h, g, b):
            mu = jnp.mean(h, axis=-1, keepdims=True)
            var = jnp.mean(jnp.square(h - mu), axis=-1, keepdims=True)
            return (h - mu) * jax.lax.rsqrt(var + LN_EPS) * g + b
        key = jax.random.key(seed)
        ks = jax.random.split(key, 12)
        s1 = 1.0 / np.sqrt(LATENT)
        s2 = 1.0 / np.sqrt(FFN)
        sd = 1.0 / np.sqrt(D)
        st = 1.0 / np.sqrt(TEMB)
        return {'x': jax.random.normal(ks[0], (B, T, D), dtype=jnp.float32), 'emb': jax.random.normal(ks[1], (B, TEMB), dtype=jnp.float32), 'W1': jax.random.uniform(ks[2], (8, LATENT, FFN), jnp.float32, -s1, s1), 'b1': jax.random.uniform(ks[3], (8, FFN), jnp.float32, -s1, s1), 'W2': jax.random.uniform(ks[4], (8, FFN, LATENT), jnp.float32, -s2, s2), 'b2': jax.random.uniform(ks[5], (8, LATENT), jnp.float32, -s2, s2), 'emb_W': jax.random.uniform(ks[6], (TEMB, 2 * D), jnp.float32, -st, st), 'emb_b': jax.random.uniform(ks[7], (2 * D,), jnp.float32, -st, st), 'ln_g': jnp.ones((D,), jnp.float32), 'ln_b': jnp.zeros((D,), jnp.float32), 'out_W': jax.random.uniform(ks[8], (D, D), jnp.float32, -sd, sd), 'out_b': jax.random.uniform(ks[9], (D,), jnp.float32, -sd, sd)}
    _L3_cond_all = _L3_cond_setup()
    _L3_cond_in = {k: v for k, v in _L3_cond_all.items() if k in ('W1', 'b1', 'W2', 'b2', 'emb_W', 'emb_b', 'ln_g', 'ln_b', 'out_W', 'out_b')}
    del _L3_cond_all
    return {'x': x, 'cond_2048': cond_2048, 'pos_BxS': pos_BxS, 'mask_1x1xSxS_ff0': mask_1x1xSxS_ff0, 'L0_cond_W_ada': _L0_cond_in['W_ada'], 'L0_cond_b_ada': _L0_cond_in['b_ada'], 'L0_cond_Wq': _L0_cond_in['Wq'], 'L0_cond_Wkd': _L0_cond_in['Wkd'], 'L0_cond_Wku': _L0_cond_in['Wku'], 'L0_cond_Wvu': _L0_cond_in['Wvu'], 'L0_cond_Wo': _L0_cond_in['Wo'], 'L1_cond_ln1_w': _L1_cond_in['ln1_w'], 'L1_cond_ln1_tw': _L1_cond_in['ln1_tw'], 'L1_cond_ln2_w': _L1_cond_in['ln2_w'], 'L1_cond_ln2_tw': _L1_cond_in['ln2_tw'], 'L1_cond_Wq': _L1_cond_in['Wq'], 'L1_cond_Wk': _L1_cond_in['Wk'], 'L1_cond_Wv': _L1_cond_in['Wv'], 'L1_cond_Wo': _L1_cond_in['Wo'], 'L1_cond_Wg': _L1_cond_in['Wg'], 'L1_cond_Wu': _L1_cond_in['Wu'], 'L1_cond_Wd': _L1_cond_in['Wd'], 'L2_cond_Wqkv': _L2_cond_in['Wqkv'], 'L2_cond_q_bias': _L2_cond_in['q_bias'], 'L2_cond_v_bias': _L2_cond_in['v_bias'], 'L2_cond_scale_mul_log': _L2_cond_in['scale_mul_log'], 'L2_cond_Wproj': _L2_cond_in['Wproj'], 'L2_cond_bproj': _L2_cond_in['bproj'], 'L2_cond_Wada': _L2_cond_in['Wada'], 'L2_cond_bada': _L2_cond_in['bada'], 'L2_cond_Wfc1': _L2_cond_in['Wfc1'], 'L2_cond_bfc1': _L2_cond_in['bfc1'], 'L2_cond_Wfc2': _L2_cond_in['Wfc2'], 'L2_cond_bfc2': _L2_cond_in['bfc2'], 'L3_cond_W1': _L3_cond_in['W1'], 'L3_cond_b1': _L3_cond_in['b1'], 'L3_cond_W2': _L3_cond_in['W2'], 'L3_cond_b2': _L3_cond_in['b2'], 'L3_cond_emb_W': _L3_cond_in['emb_W'], 'L3_cond_emb_b': _L3_cond_in['emb_b'], 'L3_cond_ln_g': _L3_cond_in['ln_g'], 'L3_cond_ln_b': _L3_cond_in['ln_b'], 'L3_cond_out_W': _L3_cond_in['out_W'], 'L3_cond_out_b': _L3_cond_in['out_b']}

def reference(x, cond_2048, pos_BxS, mask_1x1xSxS_ff0, L0_cond_W_ada, L0_cond_b_ada, L0_cond_Wq, L0_cond_Wkd, L0_cond_Wku, L0_cond_Wvu, L0_cond_Wo, L1_cond_ln1_w, L1_cond_ln1_tw, L1_cond_ln2_w, L1_cond_ln2_tw, L1_cond_Wq, L1_cond_Wk, L1_cond_Wv, L1_cond_Wo, L1_cond_Wg, L1_cond_Wu, L1_cond_Wd, L2_cond_Wqkv, L2_cond_q_bias, L2_cond_v_bias, L2_cond_scale_mul_log, L2_cond_Wproj, L2_cond_bproj, L2_cond_Wada, L2_cond_bada, L2_cond_Wfc1, L2_cond_bfc1, L2_cond_Wfc2, L2_cond_bfc2, L3_cond_W1, L3_cond_b1, L3_cond_W2, L3_cond_b2, L3_cond_emb_W, L3_cond_emb_b, L3_cond_ln_g, L3_cond_ln_b, L3_cond_out_W, L3_cond_out_b):
    import jax
    import jax.numpy as jnp

    def _L0_cond_ref(x, t_emb, W_ada, b_ada, Wq, Wkd, Wku, Wvu, Wo):
        import jax, jax.numpy as jnp
        import numpy as np
        D_MODEL = 512
        N_HEADS = 16
        N_KV_HEADS = 4
        HEAD_DIM = D_MODEL // N_HEADS
        N_GROUPS = N_HEADS // N_KV_HEADS
        BLOCK_SIZE = 128
        WINDOW = 64
        GLOBAL_EVERY = 64
        LATENT = 128
        ROPE_THETA = 10000.0
        LN_EPS = 1e-05

        def _rope_tables(T, dtype):
            freqs = 1.0 / ROPE_THETA ** (jnp.arange(0, HEAD_DIM, 2, dtype=jnp.float32) / HEAD_DIM)
            emb = jnp.arange(T, dtype=jnp.float32)[:, None] * freqs[None, :]
            cos = jnp.concatenate([jnp.cos(emb), jnp.cos(emb)], axis=-1).astype(dtype)
            sin = jnp.concatenate([jnp.sin(emb), jnp.sin(emb)], axis=-1).astype(dtype)
            return (cos, sin)

        def _rotate_half(x):
            h = x.shape[-1] // 2
            return jnp.concatenate([-x[..., h:], x[..., :h]], axis=-1)

        def _sparse_mask(T):
            idx = jnp.arange(T)
            blk = idx // BLOCK_SIZE
            future_block = blk[None, :] > blk[:, None]
            outside_window = jnp.abs(idx[None, :] - idx[:, None]) > WINDOW
            global_visible = jnp.broadcast_to((idx % GLOBAL_EVERY == 0)[None, :], (T, T))
            return outside_window & ~global_visible | future_block
        B, T, C = x.shape
        proj = t_emb @ W_ada.T + b_ada
        scale, shift = (proj[:, :C], proj[:, C:])
        mu = jnp.mean(x, axis=-1, keepdims=True)
        var = jnp.mean(jnp.square(x - mu), axis=-1, keepdims=True)
        h = (x - mu) * jax.lax.rsqrt(var + LN_EPS)
        h = h * (1.0 + scale[:, None, :]) + shift[:, None, :]
        q = (h @ Wq.T).reshape(B, T, N_HEADS, HEAD_DIM).transpose(0, 2, 1, 3)
        c_kv = h @ Wkd.T
        k = (c_kv @ Wku.T).reshape(B, T, N_KV_HEADS, HEAD_DIM).transpose(0, 2, 1, 3)
        v = (c_kv @ Wvu.T).reshape(B, T, N_KV_HEADS, HEAD_DIM).transpose(0, 2, 1, 3)
        cos, sin = _rope_tables(T, x.dtype)
        cos, sin = (cos[None, None], sin[None, None])
        q = q * cos + _rotate_half(q) * sin
        k = k * cos + _rotate_half(k) * sin
        k_exp = jnp.repeat(k, N_GROUPS, axis=1)
        v_exp = jnp.repeat(v, N_GROUPS, axis=1)
        mask = _sparse_mask(T)
        scores = jnp.einsum('bhtd,bhsd->bhts', q, k_exp) / jnp.sqrt(jnp.asarray(HEAD_DIM, x.dtype))
        scores = jnp.where(mask[None, None], jnp.asarray(-jnp.inf, x.dtype), scores)
        attn = jax.nn.softmax(scores, axis=-1)
        y = jnp.einsum('bhts,bhsd->bhtd', attn, v_exp)
        out = y.transpose(0, 2, 1, 3).reshape(B, T, C) @ Wo.T
        return x + out

    def _L1_cond_ref(x, pos_ids, time_emb, ln1_w, ln1_tw, ln2_w, ln2_tw, Wq, Wk, Wv, Wo, Wg, Wu, Wd):
        import jax, jax.numpy as jnp
        import numpy as np
        HIDDEN, NQ, NKV, HD, INTER = (512, 8, 1, 64, 2048)
        B, S = (4, 512)
        EPS = 1e-06
        ROPE_BASE = 10000.0

        def ada_rms(x, t, w, tw):
            n = x * jax.lax.rsqrt(jnp.mean(jnp.square(x), axis=-1, keepdims=True) + EPS)
            scale = t @ tw.T
            return n * (w * (1.0 + scale))[:, None, :]

        def apply_rope(x, pos_ids):
            half = HD // 2
            inv_freq = 1.0 / ROPE_BASE ** (jnp.arange(0, HD, 2, dtype=jnp.float32) / HD)
            ang = pos_ids.astype(jnp.float32)[:, :, None] * inv_freq
            cos = jnp.concatenate([jnp.cos(ang), jnp.cos(ang)], axis=-1)[:, None]
            sin = jnp.concatenate([jnp.sin(ang), jnp.sin(ang)], axis=-1)[:, None]
            x1, x2 = (x[..., :half], x[..., half:])
            rot = jnp.concatenate([-x2, x1], axis=-1)
            return x * cos + rot * sin
        b, s, _ = x.shape
        g = NQ // NKV
        res = x
        h = ada_rms(x, time_emb, ln1_w, ln1_tw)
        q = (h @ Wq.T).reshape(b, s, NQ, HD).transpose(0, 2, 1, 3)
        k = (h @ Wk.T).reshape(b, s, NKV, HD).transpose(0, 2, 1, 3)
        v = (h @ Wv.T).reshape(b, s, NKV, HD).transpose(0, 2, 1, 3)
        q = apply_rope(q, pos_ids)
        k = apply_rope(k, pos_ids)
        qg = q.reshape(b, NKV, g, s, HD)
        scores = jnp.einsum('bkgsd,bktd->bkgst', qg, k) / jnp.sqrt(jnp.float32(HD))
        attn = jax.nn.softmax(scores, axis=-1)
        ctx = jnp.einsum('bkgst,bktd->bkgsd', attn, v)
        ctx = ctx.reshape(b, NQ, s, HD).transpose(0, 2, 1, 3).reshape(b, s, NQ * HD)
        x = res + ctx @ Wo.T
        res = x
        h = ada_rms(x, time_emb, ln2_w, ln2_tw)
        mlp = jax.nn.silu(h @ Wg.T) * (h @ Wu.T) @ Wd.T
        return res + mlp

    def _L2_cond_ref(x, cond_BD, attn_bias, Wqkv, q_bias, v_bias, scale_mul_log, Wproj, bproj, Wada, bada, Wfc1, bfc1, Wfc2, bfc2):
        import jax, jax.numpy as jnp
        import numpy as np
        B, L, C, H = (2, 512, 512, 16)
        COND = 512
        HID = 4 * C
        LN_EPS = 1e-06

        def _ln(x):
            m = jnp.mean(x, axis=-1, keepdims=True)
            v = jnp.mean((x - m) ** 2, axis=-1, keepdims=True)
            return (x - m) / jnp.sqrt(v + LN_EPS)

        def _gelu_tanh(u):
            c = np.sqrt(2.0 / np.pi).astype(np.float32)
            return 0.5 * u * (1.0 + jnp.tanh(c * (u + 0.044715 * u ** 3)))
        Bs, Lx, Cx = x.shape
        D = Cx // H
        ada = (jax.nn.silu(cond_BD) @ Wada.T + bada).reshape(Bs, 1, 6, Cx)
        gamma1, gamma2, scale1, scale2, shift1, shift2 = [ada[:, :, i, :] for i in range(6)]

        def attn(xin):
            qkv_bias = jnp.concatenate([q_bias, jnp.zeros_like(q_bias), v_bias])
            qkv = (xin @ Wqkv.T + qkv_bias).reshape(Bs, Lx, 3, H, D)
            qkv = jnp.transpose(qkv, (2, 0, 3, 1, 4))
            q, k, v = (qkv[0], qkv[1], qkv[2])
            sm = jnp.exp(jnp.minimum(scale_mul_log, jnp.log(jnp.float32(100.0))))
            qn = q / jnp.maximum(jnp.linalg.norm(q, axis=-1, keepdims=True), 1e-12) * sm
            kn = k / jnp.maximum(jnp.linalg.norm(k, axis=-1, keepdims=True), 1e-12)
            scores = jnp.einsum('bhqd,bhkd->bhqk', qn, kn) + attn_bias
            p = jax.nn.softmax(scores, axis=-1)
            o = jnp.einsum('bhqk,bhkd->bhqd', p, v)
            o = jnp.transpose(o, (0, 2, 1, 3)).reshape(Bs, Lx, Cx)
            return o @ Wproj.T + bproj
        x = x + attn(_ln(x) * (scale1 + 1.0) + shift1) * gamma1
        h = _gelu_tanh((_ln(x) * (scale2 + 1.0) + shift2) @ Wfc1.T + bfc1)
        x = x + (h @ Wfc2.T + bfc2) * gamma2
        return x

    def _L3_cond_ref(x, emb, W1, b1, W2, b2, emb_W, emb_b, ln_g, ln_b, out_W, out_b):
        import jax, jax.numpy as jnp
        import numpy as np
        B, T, LATENT, FFN, TEMB = (4, 1024, 64, 256, 512)
        D = 8 * LATENT
        LN_EPS = 1e-05

        def _layernorm(h, g, b):
            mu = jnp.mean(h, axis=-1, keepdims=True)
            var = jnp.mean(jnp.square(h - mu), axis=-1, keepdims=True)
            return (h - mu) * jax.lax.rsqrt(var + LN_EPS) * g + b
        Bx, Tx, Dx = x.shape
        xr = x.reshape(Bx, Tx, 8, LATENT)
        h = jnp.einsum('btel,elf->btef', xr, W1) + b1
        h = jax.nn.gelu(h, approximate=False)
        y = jnp.einsum('btef,efl->btel', h, W2) + b2
        y = y.reshape(Bx, Tx, Dx)
        eo = jax.nn.silu(emb) @ emb_W + emb_b
        scale, shift = jnp.split(eo[:, None, :], 2, axis=-1)
        hn = _layernorm(y, ln_g, ln_b) * (1.0 + scale) + shift
        proj = jax.nn.silu(hn) @ out_W + out_b
        return x + proj
    x = _L0_cond_ref(x, cond_2048, L0_cond_W_ada, L0_cond_b_ada, L0_cond_Wq, L0_cond_Wkd, L0_cond_Wku, L0_cond_Wvu, L0_cond_Wo)
    x = _L1_cond_ref(x, pos_BxS, cond_2048, L1_cond_ln1_w, L1_cond_ln1_tw, L1_cond_ln2_w, L1_cond_ln2_tw, L1_cond_Wq, L1_cond_Wk, L1_cond_Wv, L1_cond_Wo, L1_cond_Wg, L1_cond_Wu, L1_cond_Wd)
    x = _L2_cond_ref(x, cond_2048, mask_1x1xSxS_ff0, L2_cond_Wqkv, L2_cond_q_bias, L2_cond_v_bias, L2_cond_scale_mul_log, L2_cond_Wproj, L2_cond_bproj, L2_cond_Wada, L2_cond_bada, L2_cond_Wfc1, L2_cond_bfc1, L2_cond_Wfc2, L2_cond_bfc2)
    x = _L3_cond_ref(x, cond_2048, L3_cond_W1, L3_cond_b1, L3_cond_W2, L3_cond_b2, L3_cond_emb_W, L3_cond_emb_b, L3_cond_ln_g, L3_cond_ln_b, L3_cond_out_W, L3_cond_out_b)
    return x

_drawn_inputs = setup_inputs


def setup_inputs(seed=0):
    import zlib

    import numpy as np

    out = dict(_drawn_inputs(seed))
    spreads = {'L0_cond_b_ada': (0.0, 0.1),
     'L1_cond_ln1_w': (1.0, 0.2),
     'L1_cond_ln2_w': (1.0, 0.2),
     'L2_cond_q_bias': (0.0, 0.1),
     'L2_cond_v_bias': (0.0, 0.1),
     'L2_cond_scale_mul_log': (1.3862943649291992, 0.2),
     'L2_cond_bproj': (0.0, 0.1),
     'L2_cond_bada': (0.0, 0.1),
     'L2_cond_bfc1': (0.0, 0.1),
     'L2_cond_bfc2': (0.0, 0.1),
     'L3_cond_ln_g': (1.0, 0.2),
     'L3_cond_ln_b': (0.0, 0.1)}
    factors = {}
    for name, (base, spread) in spreads.items():
        noise = np.random.default_rng([zlib.crc32(name.encode()), seed]).standard_normal(out[name].shape)
        drawn = base * np.exp(spread * noise) if base else spread * noise
        out[name] = jnp.asarray(drawn.astype(out[name].dtype))
    for name, factor in factors.items():
        out[name] = (out[name] * factor).astype(out[name].dtype)
    return out
```

```python
from contextlib import ExitStack

import numpy as np
import concourse.bass as bass
from concourse import mybir

F32 = mybir.dt.float32
I32 = mybir.dt.int32
ALU = mybir.AluOpType
ACT = mybir.ActivationFunctionType
AX_X = mybir.AxisListType.X

P = 128
B, T, D = 4, 512, 512
C = D // P
TT = T // P
HID = 2048
HC = 256
NCH = HID // HC
EXP, LAT, FFN = 8, 64, 256
ET = EXP * FFN // P
NAMES = ("pe", "act", "dve", "pool")


class Step:

    n = {}

    def pe(self, k, e, b, at): pass
    def act(self, k, e, b, at): pass
    def dve(self, k, e, b, at): pass
    def pool(self, k, e, b, at): pass


def start_wait(k, e, at, *names):
    for name in names:
        if not (isinstance(at[name], int) and at[name] == 0):
            e.wait_ge(k.done[name], at[name])


class Norm(Step):

    def __init__(s, src, out, A, Bias, eps, rms=False, func=None, extra=None):
        s.src, s.out, s.A, s.Bias, s.eps, s.rms, s.extra = src, out, A, Bias, eps, rms, extra
        s.func = func or ACT.Identity
        m = 0 if rms else 1
        s.n = {"pe": 1 + m, "dve": m * C + 1 + C, "act": C + 1 + m * C + (C if extra is not None else 0)}

    def centred(s, k, b, c):
        return s.src(b, c) if s.rms else k.hN[:, c, :]

    def pe(s, k, e, b, at):
        start_wait(k, e, at, "act", "dve", "pool")
        if not s.rms:
            for c in range(C):
                mm = e.matmul(k.bank(0), k.ones[:], s.src(b, c), start=c == 0, stop=c == C - 1)
            mm.then_inc(k.done["pe"], 1)
        for c in range(C):
            e.wait_ge(k.done["act"], at["act"] + c + 1)
            mm = e.matmul(k.bank(1), k.ones[:], k.t1[:, c, :], start=c == 0, stop=c == C - 1)
        mm.then_inc(k.done["pe"], 1)

    def dve(s, k, e, b, at):
        start_wait(k, e, at, "act", "dve", "pe", "pool")
        n = 0
        if not s.rms:
            e.wait_ge(k.done["pe"], at["pe"] + 1)
            for c in range(C):
                e.tensor_tensor(k.hN[:, c, :], s.src(b, c), k.bank(0), ALU.subtract)\
                    .then_inc(k.done["dve"], 1)
            n = C
        e.wait_ge(k.done["act"], at["act"] + C + 1)
        e.reciprocal(k.rstd[:], k.sd[:]).then_inc(k.done["dve"], 1)
        e.wait_ge(k.done["dve"], at["dve"] + n + 1)
        for c in range(C):
            out = s.out(b, c) if s.rms else k.hN[:, c, :]
            e.scalar_tensor_tensor(out=out, in0=s.centred(k, b, c), scalar=s.A(b, c),
                                   in1=k.rstd[:], op0=ALU.mult, op1=ALU.mult)\
                .then_inc(k.done["dve"], 1)

    def act(s, k, e, b, at):
        start_wait(k, e, at, "act", "dve", "pe", "pool")
        for c in range(C):
            if not s.rms:
                e.wait_ge(k.done["dve"], at["dve"] + c + 1)
            e.activation(k.t1[:, c, :], s.centred(k, b, c), ACT.Square).then_inc(k.done["act"], 1)
        e.wait_ge(k.done["pe"], at["pe"] + s.n["pe"])
        e.activation(k.sd[:], k.bank(1), ACT.Sqrt, bias=s.eps, scale=1.0)\
            .then_inc(k.done["act"], 1)
        if not s.rms:
            for c in range(C):
                e.wait_ge(k.done["dve"], at["dve"] + C + 1 + c + 1)
                e.activation(s.out(b, c), k.hN[:, c, :], s.func, bias=s.Bias(b, c), scale=1.0)\
                    .then_inc(k.done["act"], 1)
        if s.extra is not None:
            for c in range(C):
                if c == 0:
                    e.wait_ge(k.done["dve"], at["dve"] + s.n["dve"])
                e.activation(s.src(b, c), s.src(b, c), ACT.Identity, bias=s.extra(b, c), scale=1.0)\
                    .then_inc(k.done["act"], 1)


class Linear(Step):

    def __init__(s, groups, mats, put_act, put_dve, width=T, only=None, load=None):
        s.groups, s.mats, s.put_act, s.put_dve, s.width, s.only = groups, mats, put_act, put_dve, width, only
        s.load = load
        to_act = [s.by(g) == "act" for g in range(groups)]
        s.n = {"pe": groups, "act": sum(to_act), "dve": groups - sum(to_act)}

    def by(s, g):
        return s.only or ("act" if g % 2 == 0 else "dve")

    def count(s, g):
        return sum(s.by(i) == s.by(g) for i in range(g + 1))

    def pe(s, k, e, b, at):
        start_wait(k, e, at, "act", "dve", "pool")
        if s.load is not None:
            e.wait_ge(*s.load)
        for g in range(s.groups):
            if g >= 4:
                f = g - 4
                e.wait_ge(k.done[s.by(f)], at[s.by(f)] + s.count(f))
            mats = s.mats(b, g)
            for i, (lhsT, rhs) in enumerate(mats):
                mm = e.matmul(k.bank(g % 4)[:, 0:s.width], lhsT, rhs,
                              start=i == 0, stop=i == len(mats) - 1)
            mm.then_inc(k.done["pe"], 1)

    def act(s, k, e, b, at):
        if s.n["act"]:
            start_wait(k, e, at, "act", "dve", "pe", "pool")
        for g in range(s.groups):
            if s.by(g) == "act":
                e.wait_ge(k.done["pe"], at["pe"] + g + 1)
                s.put_act(e, b, g, k.bank(g % 4)[:, 0:s.width]).then_inc(k.done["act"], 1)

    def dve(s, k, e, b, at):
        if s.n["dve"]:
            start_wait(k, e, at, "act", "dve", "pe", "pool")
        for g in range(s.groups):
            if s.by(g) == "dve":
                e.wait_ge(k.done["pe"], at["pe"] + g + 1)
                s.put_dve(e, b, g, k.bank(g % 4)[:, 0:s.width]).then_inc(k.done["dve"], 1)


class Rope(Step):

    def __init__(s, tiles, perm, cos, sin):
        s.tiles, s.perm, s.cos, s.sin = tiles, perm, cos, sin
        s.n = {"pe": len(tiles), "dve": 2 * len(tiles), "pool": len(tiles)}

    def pe(s, k, e, b, at):
        start_wait(k, e, at, "act", "dve", "pool")
        for g, z in enumerate(s.tiles):
            if g >= 4:
                e.wait_ge(k.done["dve"], at["dve"] + g - 3)
            e.matmul(k.bank(g % 4), s.perm, z, start=True, stop=True).then_inc(k.done["pe"], 1)

    def dve(s, k, e, b, at):
        start_wait(k, e, at, "act", "dve", "pe", "pool")
        for g in range(len(s.tiles)):
            e.wait_ge(k.done["pe"], at["pe"] + g + 1)
            e.tensor_tensor(k.ropet[:, g, :], k.bank(g % 4), s.sin, ALU.mult).then_inc(k.done["dve"], 1)
        for g, z in enumerate(s.tiles):
            e.wait_ge(k.done["dve"], at["dve"] + g + 1)
            e.wait_ge(k.done["pool"], at["pool"] + g + 1)
            e.tensor_tensor(z, z, k.ropet[:, g, :], ALU.add).then_inc(k.done["dve"], 1)

    def pool(s, k, e, b, at):
        start_wait(k, e, at, "act", "dve", "pe", "pool")
        for g, z in enumerate(s.tiles):
            e.wait_ge(k.done["pe"], at["pe"] + g + 1)
            e.tensor_tensor(z, z, s.cos, ALU.mult).then_inc(k.done["pool"], 1)


class Angles(Step):

    n = {"dve": 14, "act": 2}
    C1 = 6.28125
    C2 = float(np.float32(2 * np.pi - 6.28125))
    C3 = float(2 * np.pi - 6.28125 - float(np.float32(2 * np.pi - 6.28125)))
    MAGIC = 12582912.0
    TOP = 3.1415925

    def dve(s, k, e, b, at):
        start_wait(k, e, at, "act", "dve", "pe", "pool")
        done = [0]

        def inc(ins):
            done[0] += 1
            ins.then_inc(k.done["dve"], 1)
            e.wait_ge(k.done["dve"], at["dve"] + done[0])

        e.wait_ge(k.l_pos, 16)
        ang, kk, r = k.Pb[:, 0, :], k.Pb[:, 1, :], k.Pb[:, 2, :]
        inc(e.tensor_copy(kk, k.pos[:, bass.ds(b, 1), :].rearrange("p o t -> p (o t)")))
        inc(e.tensor_scalar(ang, kk, k.freq[:, 0:1], None, ALU.mult))
        for src, parts, out in ((ang, (s.C1, s.C2, s.C3), k.sint), (r, (s.C1, s.C2), k.cost)):
            inc(e.tensor_scalar(kk, src, 1 / (2 * np.pi), s.MAGIC, ALU.mult, ALU.add))
            inc(e.tensor_scalar(kk, kk, s.MAGIC, None, ALU.subtract))
            for part in parts:
                inc(e.scalar_tensor_tensor(out=r, in0=kk, scalar=-part, in1=src, op0=ALU.mult, op1=ALU.add))
                src = r
            inc(e.tensor_scalar(out, r, s.TOP, -s.TOP, ALU.min, ALU.max))
            if out is k.sint:
                inc(e.tensor_scalar(r, r, float(np.pi / 2), None, ALU.add))
        assert done[0] == s.n["dve"], done

    def act(s, k, e, b, at):
        start_wait(k, e, at, "act", "dve", "pe", "pool")
        e.wait_ge(k.done["dve"], at["dve"] + s.n["dve"])
        e.activation(k.sinr[:], k.sint, ACT.Sin).then_inc(k.done["act"], 1)
        e.activation(k.cosr[:], k.cost, ACT.Sin).then_inc(k.done["act"], 1)


class Sign(Step):

    n = {"dve": 1}

    def dve(s, k, e, b, at):
        start_wait(k, e, at, "act", "dve", "pe", "pool")
        e.tensor_scalar(k.sinr[:], k.sinr[:], k.sign[:, 0:1], None, ALU.mult).then_inc(k.done["dve"], 1)


class QKNorm(Step):

    n = {"act": 2 * 2 * C, "pe": 2 * C, "dve": 3 * 2 * C}

    def tile(s, k, g):
        return k.R[:, g // C, g % C, :]

    def pe(s, k, e, b, at):
        start_wait(k, e, at, "act", "dve", "pool")
        for g in range(2 * C):
            e.wait_ge(k.done["act"], at["act"] + s.sq(g))
            e.matmul(k.bank(g % 4), k.blockones[:], k.t1[:, g % 4, :], start=True, stop=True)\
                .then_inc(k.done["pe"], 1)

    def sq(s, g):
        return 1 if g == 0 else 2 * g

    def rt(s, g):
        return 2 * g + 3 if g < 2 * C - 1 else 4 * C

    def act(s, k, e, b, at):
        start_wait(k, e, at, "act", "dve", "pe", "pool")
        for g in range(2 * C + 1):
            if g < 2 * C:
                if g >= 4:
                    e.wait_ge(k.done["pe"], at["pe"] + g - 3)
                e.activation(k.t1[:, g % 4, :], s.tile(k, g), ACT.Square).then_inc(k.done["act"], 1)
            if g >= 1:
                f = g - 1
                e.wait_ge(k.done["pe"], at["pe"] + f + 1)
                if f >= 4:
                    e.wait_ge(k.done["dve"], at["dve"] + 3 * (f - 3))
                e.activation(k.ropet[:, f % 4, :], k.bank(f % 4), ACT.Sqrt).then_inc(k.done["act"], 1)

    def dve(s, k, e, b, at):
        start_wait(k, e, at, "act", "dve", "pe", "pool")
        for g in range(2 * C):
            e.wait_ge(k.done["act"], at["act"] + s.rt(g))
            r = k.ropet[:, g % 4, :]
            e.tensor_scalar(r, r, 1e-12, None, ALU.max).then_inc(k.done["dve"], 1)
            e.wait_ge(k.done["dve"], at["dve"] + 3 * g + 1)
            e.reciprocal(r, r).then_inc(k.done["dve"], 1)
            e.wait_ge(k.done["dve"], at["dve"] + 3 * g + 2)
            z = s.tile(k, g)
            scale = k.smul[:, g:g + 1] if g < C else 1.0
            e.scalar_tensor_tensor(out=z, in0=z, scalar=scale, in1=r, op0=ALU.mult, op1=ALU.mult)\
                .then_inc(k.done["dve"], 1)


class Attention(Step):

    def __init__(s, H, q_of, k_of, v_of, dv, bias_loaded, tiles_of):
        s.bias_loaded, biased = bias_loaded, bias_loaded is not None
        s.H, s.q_of, s.k_of, s.v_of, s.dv, s.biased, s.tiles_of = H, q_of, k_of, v_of, dv, biased, tiles_of
        s.U = TT * H
        s.pe_order, s.act_order, s.dve_order = [], [], []
        for t in range(s.U + 8):
            if t < s.U:
                s.pe_order.append(("scores", t))
                s.dve_order.append(("max", t))
                s.act_order.append(("exp", t))
            if 0 <= t - 2 < s.U:
                s.pe_order.append(("turn", t - 2))
                (s.act_order if t % 2 == 0 else s.dve_order).append(("copy", t - 2))
            if 0 <= t - 3 < s.U:
                s.pe_order.append(("values", t - 3))
            if t >= 4 and (t - 4) % H == H - 1 and t - 4 < s.U:
                s.dve_order += [("recip", (t - 4) // H), ("norm", (t - 4) // H)]
            if t >= 6 and (t - 6) % H == H - 1 and t - 6 < s.U:
                s.pe_order.append(("outturn", (t - 6) // H))
                s.act_order.append(("outcopy", (t - 6) // H))
        s.i = {}
        for name, order in (("pe", s.pe_order), ("act", s.act_order), ("dve", s.dve_order)):
            for n, op in enumerate(order):
                s.i[op] = (name, n + 1)
        s.n = {"pe": len(s.pe_order), "act": len(s.act_order), "dve": len(s.dve_order)}

    def wait(s, k, e, at, kind, index):
        name, n = s.i[(kind, index)]
        e.wait_ge(k.done[name], at[name] + n)

    def S(s, k, u):
        return k.bank(u % 3)[:, 0:P * s.tiles_of(u // s.H)]

    def O(s, k, i):
        return k.bank(5 + i % 2)[:, 0:s.H * s.dv]

    def pe(s, k, e, b, at):
        start_wait(k, e, at, "act", "dve", "pool")
        for kind, u in s.pe_order:
            if kind == "scores":
                if u >= 3:
                    s.wait(k, e, at, "max" if s.biased else "exp", u - 3)
                i, h = u // s.H, u % s.H
                mm = e.matmul(s.S(k, u), s.q_of(h, i), s.k_of(h, s.tiles_of(i)), start=True, stop=True)
            elif kind == "turn":
                s.wait(k, e, at, "exp", u)
                if u >= 2:
                    s.wait(k, e, at, "copy", u - 2)
                for j in range(s.tiles_of(u // s.H)):
                    mm = e.transpose(k.bank(3 + u % 2)[:, j * P:(j + 1) * P],
                                     k.Pb[:, u % 3, j * P:(j + 1) * P], k.ident[:])
            elif kind == "values":
                i, h = u // s.H, u % s.H
                s.wait(k, e, at, "copy", u)
                if h == 0 and i >= 2:
                    s.wait(k, e, at, "norm", i - 2)
                n = s.tiles_of(i)
                for j in range(n):
                    mm = e.matmul(s.O(k, i)[:, h * s.dv:(h + 1) * s.dv],
                                  k.PT[:, u % 3, j * P:(j + 1) * P], s.v_of(h, j),
                                  start=j == 0, stop=j == n - 1)
            else:
                s.wait(k, e, at, "norm", u)
                if u >= 1:
                    s.wait(k, e, at, "outcopy", u - 1)
                for c in range(C):
                    mm = e.transpose(k.bank(7)[:, c * P:(c + 1) * P],
                                     k.hN[:, u, c * P:(c + 1) * P], k.ident[:])
            mm.then_inc(k.done["pe"], 1)

    def dve(s, k, e, b, at):
        start_wait(k, e, at, "act", "dve", "pe", "pool")
        for kind, u in s.dve_order:
            if kind == "max":
                s.wait(k, e, at, "scores", u)
                if u >= 3:
                    s.wait(k, e, at, "turn", u - 3)
                    s.wait(k, e, at, "exp", u - 3)
                w = P * s.tiles_of(u // s.H)
                if s.biased:
                    e.wait_ge(s.bias_loaded, 16)
                    ins = e.tensor_tensor_reduce(k.Pb[:, u % 3, 0:w], s.S(k, u), k.bias[:, u // s.H, 0:w],
                                                 -1.0, 3.0e38, ALU.add, ALU.min, k.nmax[:, u:u + 1])
                else:
                    ins = e.tensor_reduce(k.nmax[:, u:u + 1], s.S(k, u), AX_X, ALU.max, negate=True)
            elif kind == "copy":
                s.wait(k, e, at, "turn", u)
                if u >= 3:
                    s.wait(k, e, at, "values", u - 3)
                w = P * s.tiles_of(u // s.H)
                ins = e.tensor_copy(k.PT[:, u % 3, 0:w], k.bank(3 + u % 2)[:, 0:w])
            elif kind == "recip":
                s.wait(k, e, at, "exp", u * s.H + s.H - 1)
                ins = e.reciprocal(k.rsum[:, u * s.H:(u + 1) * s.H], k.sums[:, u * s.H:(u + 1) * s.H])
            else:
                s.wait(k, e, at, "recip", u)
                s.wait(k, e, at, "values", u * s.H + s.H - 1)
                ins = e.tensor_tensor(
                    k.hN[:, u, :].rearrange("p (h d) -> p h d", h=s.H),
                    s.O(k, u).rearrange("p (h d) -> p h d", h=s.H),
                    k.rsum[:, u * s.H:(u + 1) * s.H].unsqueeze(2).to_broadcast([P, s.H, s.dv]), ALU.mult)
            ins.then_inc(k.done["dve"], 1)

    def act(s, k, e, b, at):
        start_wait(k, e, at, "act", "dve", "pe", "pool")
        for kind, u in s.act_order:
            if kind == "exp":
                s.wait(k, e, at, "max", u)
                w = P * s.tiles_of(u // s.H)
                src = k.Pb[:, u % 3, 0:w] if s.biased else s.S(k, u)
                if not s.biased and u >= 3:
                    s.wait(k, e, at, "turn", u - 3)
                ins = e.activation(k.Pb[:, u % 3, 0:w], src, ACT.Exp, bias=k.nmax[:, u:u + 1],
                                   scale=-1.0 if s.biased else 1.0, accum_out=k.sums[:, u:u + 1])
            elif kind == "copy":
                s.wait(k, e, at, "turn", u)
                if u >= 3:
                    s.wait(k, e, at, "values", u - 3)
                w = P * s.tiles_of(u // s.H)
                ins = e.activation(k.PT[:, u % 3, 0:w], k.bank(3 + u % 2)[:, 0:w], ACT.Copy)
            else:
                s.wait(k, e, at, "outturn", u)
                ins = e.activation(k.t1[:, :, u * P:(u + 1) * P],
                                   k.bank(7).rearrange("p (c q) -> p c q", c=C), ACT.Copy)
            ins.then_inc(k.done["act"], 1)


class MlpChunk(Step):

    def __init__(s, j, slot, gated, load, hbias=None, gamma=None):
        s.j, s.slot, s.gated, s.load, s.hbias, s.gamma = j, slot, gated, load, hbias, gamma
        s.ups = 2 if gated else 1
        s.n = {"pe": 2 * s.ups + C, "act": 2, "dve": (2 if gated else 0) + C}

    def pe(s, k, e, b, at):
        start_wait(k, e, at, "act", "dve", "pool")
        e.wait_ge(*s.load)
        up = k.WM[:, s.slot, 0:C * s.ups * HC].rearrange("p (c m) -> p c m", c=C)
        down = k.WM[:, s.slot, 2 * C * HC:2 * C * HC + 2 * D].rearrange("p (t m) -> p t m", t=2)
        for t in range(2):
            for w in range(s.ups):
                for c in range(C):
                    mm = e.matmul(k.bank(s.ups * t + w), up[:, c, w * HC + t * P:w * HC + (t + 1) * P],
                                  k.h2(b, c), start=c == 0, stop=c == C - 1)
                mm.then_inc(k.done["pe"], 1)
        for t in range(2):
            if s.gated:
                e.wait_ge(k.done["dve"], at["dve"] + t + 1)
            else:
                e.wait_ge(k.done["act"], at["act"] + t + 1)
            for m in range(C):
                mm = e.matmul(k.bank(4 + m), down[:, t, m * P:(m + 1) * P], k.hid[:, t, :],
                              start=t == 0, stop=t == 1)
                if t == 1:
                    mm.then_inc(k.done["pe"], 1)

    def act(s, k, e, b, at):
        start_wait(k, e, at, "act", "dve", "pe", "pool")
        for t in range(2):
            e.wait_ge(k.done["pe"], at["pe"] + s.ups * t + 1)
            if s.gated:
                e.activation(k.sg[:, t, :], k.bank(2 * t), ACT.Silu).then_inc(k.done["act"], 1)
            else:
                e.activation(k.hid[:, t, :], k.bank(t), ACT.Gelu_apprx_tanh,
                             bias=s.hbias[:, 2 * s.j + t:2 * s.j + t + 1], scale=1.0)\
                    .then_inc(k.done["act"], 1)

    def dve(s, k, e, b, at):
        start_wait(k, e, at, "act", "dve", "pe", "pool")
        if s.gated:
            for t in range(2):
                e.wait_ge(k.done["act"], at["act"] + t + 1)
                e.wait_ge(k.done["pe"], at["pe"] + 2 * t + 2)
                e.tensor_tensor(k.hid[:, t, :], k.sg[:, t, :], k.bank(2 * t + 1), ALU.mult)\
                    .then_inc(k.done["dve"], 1)
        for m in range(C):
            e.wait_ge(k.done["pe"], at["pe"] + 2 * s.ups + m + 1)
            e.scalar_tensor_tensor(out=k.xs(b, m), in0=k.bank(4 + m),
                                   scalar=1.0 if s.gamma is None else s.gamma(b, m),
                                   in1=k.xs(b, m), op0=ALU.mult, op1=ALU.add).then_inc(k.done["dve"], 1)


class Kit:
    pass


def conditioned_stack(nc, a, out):
    ctx = ExitStack()
    with ctx:
        def sb(name, shape, dt=F32):
            return ctx.enter_context(nc.sbuf_tensor("sb_" + name, shape, dt))

        def sem(name):
            return ctx.enter_context(nc.semaphore(name))

        k = Kit()
        psum = ctx.enter_context(nc.psum_tensor("banks", [P, 8, 512], F32))
        k.bank = lambda i: psum[:, i, :]
        x = sb("x", [P, C, B, T])
        k.R = sb("R", [P, 4, C, T])
        k.hN = sb("hN", [P, C, T])
        k.t1 = sb("t1", [P, C, T])
        k.sd = sb("sd", [P, T])
        k.rstd = sb("rstd", [P, T])
        k.Pb = sb("Pb", [P, 3, T])
        k.PT = sb("PT", [P, 3, T])
        W0 = sb("W0", [P, C * 2048])
        W1 = sb("W1", [P, C * 1536])
        k.WM = sb("WM", [P, 2, 3072])
        k.hid = sb("hid", [P, 2, T])
        k.sg = sb("sg", [P, 2, T])
        k.bias = sb("bias", [P, TT, T])
        k.cosr = sb("cos", [P, T])
        k.sinr = sb("sin", [P, T])
        k.cost, k.sint = k.PT[:, 0, :], k.PT[:, 1, :]
        k.pos = k.bias[:, :, :].bitcast(I32)
        k.ident = sb("ident", [P, P])
        k.ones = sb("ones", [P, P])
        perm = sb("perm", [P, 2, P])
        k.blockones = sb("blockones", [P, P])
        k.freq = sb("freq", [P, 1])
        k.sign = sb("sign", [P, 1])
        k.nmax = sb("nmax", [P, 64])
        k.sums = sb("sums", [P, 64])
        k.rsum = sb("rsum", [P, 64])
        k.smul = sb("smul", [P, C])
        cond = sb("cond", [P, 2, C, B])
        ADA = 48
        mod = sb("mod", [P, ADA, B])
        modb = sb("modb", [P, ADA])
        cols = sb("cols", [P, 80])
        eps5 = sb("eps5", [P, 1])
        eps6 = sb("eps6", [P, 1])
        comb = sb("comb", [P, 6, C, B])
        vbias = k.sg[:, 0, :]
        k.ropet = k.R[:, 3, :, :]

        k.done = {n: sem(n + "_done") for n in NAMES}
        l_x, l_const, l_cond = sem("l_x"), sem("l_const"), sem("l_cond")
        l_w = [sem(f"l_w{i}") for i in range(4)]
        l_bias = [sem(f"l_bias{i}") for i in range(2)]
        k.l_pos = sem("l_pos")
        l_vb = sem("l_vb")
        l_m = [sem(f"l_m{i}") for i in range(2)]
        s_zero = sem("s_zero")
        s_out = sem("s_out")

        one = lambda b: bass.ds(b, 1)
        k.xs = lambda b, c: x[:, c, one(b), :].rearrange("p o t -> p (o t)")
        k.h2 = lambda b, c: k.R[:, c, one(b), :].rearrange("p o t -> p (o t)")
        modc = lambda tile: (lambda b, c: mod[:, tile + c, one(b)])
        combc = lambda i: (lambda b, c: comb[:, i, c, one(b)])
        hN = lambda b, c: k.hN[:, c, :]
        R = lambda i, c: k.R[:, i, c, :]

        COLS = [("L1_cond_ln1_w", 4), ("L1_cond_ln2_w", 4), ("L2_cond_q_bias", 4), ("L2_cond_bproj", 4),
                ("L2_cond_bfc1", 16), ("L2_cond_bfc2", 4), ("L3_cond_b1", 16), ("L3_cond_b2", 4),
                ("L3_cond_ln_g", 4), ("L3_cond_ln_b", 4), ("L3_cond_out_b", 4)]
        col, o = {}, 0
        for name, n in COLS:
            col[name] = cols[:, o:o + n]
            o += n
        mods = {"L0": 0, "L1a": 8, "L1b": 12, "L2": 16, "L3": 40}
        MODB = [("L0_cond_b_ada", 0, 8), ("L2_cond_bada", 16, 24), ("L3_cond_emb_b", 40, 8)]

        def view(w, base, width, n=C):
            return w[:, base:base + n * width].rearrange("p (c m) -> p c m", c=n)

        wq0, wkd, wo0 = view(W0, 0, D), view(W0, 2048, P), view(W0, 2560, D)
        wku, wvu = W0[:, 4608:5120], W0[:, 5120:5248]
        wq1, wk1, wv1, wo1 = view(W1, 0, D), view(W1, 2048, P), view(W1, 2560, 64), view(W1, 2816, D)
        wqkv2, wo2 = view(W0, 0, 3 * D), view(W0, 6144, D)
        w1e, w2e = view(W1, 0, P, ET), view(W1, 2048, P, ET)
        wout3 = view(W1, 4096, D)

        def rows(name):
            return a[name].rearrange("(c p) m -> p c m", p=P)

        def copies(dst, scale=lambda g: 1.0, bias=None):
            def put_act(e, b, g, bank):
                if bias is None:
                    return e.activation(dst(b, g), bank, ACT.Copy, scale=scale(g))
                return e.activation(dst(b, g), bank, ACT.Identity, bias=bias(g), scale=scale(g))

            def put_dve(e, b, g, bank):
                return e.tensor_scalar(dst(b, g), bank, scale(g), None if bias is None else bias(g), ALU.mult,
                                       ALU.bypass if bias is None else ALU.add)
            return put_act, put_dve

        def residual(bias=None, gamma=None):
            def put_dve(e, b, g, bank):
                if gamma is not None:
                    return e.scalar_tensor_tensor(out=k.xs(b, g), in0=bank, scalar=gamma(b, g),
                                                  in1=k.xs(b, g), op0=ALU.mult, op1=ALU.add)
                return e.scalar_tensor_tensor(out=k.xs(b, g), in0=bank, scalar=0.0 if bias is None else bias(g),
                                              in1=k.xs(b, g), op0=ALU.add, op1=ALU.add)
            return None, put_dve

        def dense(w, src):
            return lambda b, g: [(w[:, c, g * P:(g + 1) * P], src(c)) for c in range(C)]

        hsrc = lambda c: k.hN[:, c, :]
        asrc = lambda c: k.t1[:, c, :]

        class Ada(Step):
            n = {"pe": 12}

            def pe(s, k, e, b, at):
                e.wait_ge(l_cond, 16)
                for j in range(12):
                    if j == 4:
                        e.wait_ge(k.done["dve"], 2)
                    e.wait_ge(l_m[j % 2], 16 * (j // 2 + 1))
                    w = k.WM[:, j % 2, 0:C * D].rearrange("p (c m) -> p c m", c=C)
                    for t in range(4):
                        for c in range(C):
                            mm = e.matmul(k.bank(0)[:, 4 * (4 * j + t):4 * (4 * j + t) + 4],
                                          w[:, c, t * P:(t + 1) * P], cond[:, int(j >= 4), c, :],
                                          start=c == 0, stop=c == C - 1)
                    mm.then_inc(k.done["pe"], 1)

            def act(s, k, e, b, at):
                e.wait_ge(l_cond, 16)
                e.activation(cond[:, 1, :, :], cond[:, 0, :, :], ACT.Silu).then_inc(k.done["act"], 1)
                e.wait_ge(l_const, 16 * n_const)
                e.activation(k.smul[:], k.smul[:], ACT.Exp).then_inc(k.done["act"], 1)

            def dve(s, k, e, b, at):
                e.memset(eps5[:], 1e-5).then_inc(k.done["dve"], 1)
                e.wait_ge(k.done["act"], 1)
                e.memset(eps6[:], 1e-6).then_inc(k.done["dve"], 1)
        Ada.n = {"pe": 12, "act": 2, "dve": 2}

        class Mods(Step):
            n = {"dve": 13}

            def dve(s, k, e, b, at):
                done = [0]

                def inc(ins):
                    done[0] += 1
                    ins.then_inc(k.done["dve"], 1)
                    e.wait_ge(k.done["dve"], at["dve"] + done[0])

                def wide(ap):
                    return ap.unsqueeze(2).to_broadcast([P, C, B])

                start_wait(k, e, at, "pe", "dve", "act")
                e.wait_ge(l_const, 16 * n_const)
                inc(e.tensor_copy(mod[:].rearrange("p t b -> p (t b)"), k.bank(0)[:, 0:ADA * B]))
                inc(e.tensor_tensor(mod[:], mod[:], modb[:].unsqueeze(2).to_broadcast([P, ADA, B]), ALU.add))
                for t0, n in ((0, 4), (8, 8), (24, 8), (40, 4)):
                    m = mod[:, t0:t0 + n, :]
                    inc(e.tensor_scalar(m, m, 1.0, None, ALU.add))
                inc(e.tensor_tensor(comb[:, 0], mod[:, 8:12, :], wide(col["L1_cond_ln1_w"]), ALU.mult))
                inc(e.tensor_tensor(comb[:, 1], mod[:, 12:16, :], wide(col["L1_cond_ln2_w"]), ALU.mult))
                inc(e.tensor_tensor(comb[:, 2], mod[:, 20:24, :], wide(col["L2_cond_bfc2"]), ALU.mult))
                inc(e.tensor_tensor(comb[:, 5], mod[:, 16:20, :], wide(col["L2_cond_bproj"]), ALU.mult))
                inc(e.tensor_tensor(comb[:, 3], mod[:, 40:44, :], wide(col["L3_cond_ln_g"]), ALU.mult))
                inc(e.tensor_tensor(comb[:, 4], mod[:, 40:44, :], wide(col["L3_cond_ln_b"]), ALU.mult))
                inc(e.tensor_tensor(comb[:, 4], comb[:, 4], mod[:, 44:48, :], ALU.add))
                assert done[0] == s.n["dve"], done

        v0 = k.R[:, 2, :, 0:P]
        v1 = k.R[:, 2, :, 0:64]
        v2 = k.R[:, 2, :, :]

        def attention(H, dv, khead, vhead, v, bias_loaded, tiles_of):
            d = D // H
            per = P // d
            return Attention(
                H,
                lambda h, i: k.R[d * (h % per):d * (h % per + 1), 0, h // per, i * P:(i + 1) * P],
                lambda h, n: k.R[d * (h % per):d * (h % per + 1), 1, khead(h), 0:n * P],
                lambda h, j: v[:, j, dv * vhead(h):dv * (vhead(h) + 1)], dv, bias_loaded, tiles_of)

        all_tiles = lambda i: TT
        def kv0(b, g):
            if g < C:
                return [(wku[:, g * P:(g + 1) * P], R(3, 0))]
            return [(R(3, 0)[:, (g - C) * P:(g - C + 1) * P], wvu)]

        layer0 = [
            Norm(k.xs, hN, modc(0), modc(4), eps5[:, 0:1]),
            Linear(C + 1, lambda b, g: dense(wq0, hsrc)(b, g) if g < C else
                   [(wkd[:, c, :], hsrc(c)) for c in range(C)],
                   *copies(lambda b, g: R(0, g) if g < C else R(3, 0),
                           lambda g: float(1 / np.sqrt(np.float32(32))) if g < C else 1.0), load=(l_w[0], 80)),
            Linear(C, kv0, *copies(lambda b, g: R(1, g))),
            Linear(TT, lambda b, g: kv0(b, g + C), *copies(lambda b, g: v0[:, g, :]), width=P),
            Rope([R(0, c) for c in range(C)], perm[:, 0, :], k.cosr[:], k.sinr[:]),
            Rope([R(1, c) for c in range(C)], perm[:, 0, :], k.cosr[:], k.sinr[:]),
            attention(16, 32, lambda h: h // 4, lambda h: h // 4, v0, l_bias[0], lambda i: i + 1),
            Linear(C, dense(wo0, asrc), *residual(), only="dve"),
        ]

        layer1a = [
            Norm(k.xs, hN, combc(0), None, eps6[:, 0:1], rms=True),
            Angles(), Sign(),
            Linear(C, dense(wq1, hsrc), *copies(lambda b, g: R(0, g), lambda g: 0.125), load=(l_w[1], 64)),
            Linear(1, lambda b, g: [(wk1[:, c, :], hsrc(c)) for c in range(C)],
                   *copies(lambda b, g: R(1, 0))),
            Linear(TT, lambda b, g: [(k.hN[:, c, g * P:(g + 1) * P], wv1[:, c, :]) for c in range(C)],
                   *copies(lambda b, g: v1[:, g, :]), width=64),
            Rope([R(0, c) for c in range(C)], perm[:, 1, :], k.cosr[:], k.sinr[:]),
            Rope([R(1, 0)], perm[:, 1, :], k.cosr[:], k.sinr[:]),
            attention(8, 64, lambda h: 0, lambda h: 0, v1, None, all_tiles),
            Linear(C, dense(wo1, asrc), *residual(), only="dve"),
        ]
        norm1b = [Norm(k.xs, k.h2, combc(1), None, eps6[:, 0:1], rms=True)]

        class ValueBias(Step):
            n = {"pool": TT}

            def pool(s, k, e, b, at):
                start_wait(k, e, at, "act", "dve", "pe", "pool")
                e.wait_ge(l_vb, 16)
                for j in range(TT):
                    e.tensor_tensor(v2[:, j, :], v2[:, j, :], vbias, ALU.add).then_inc(k.done["pool"], 1)

        class ProjBias(Step):
            n = {"act": C}

            def act(s, k, e, b, at):
                start_wait(k, e, at, "act", "dve", "pe", "pool")
                for c in range(C):
                    e.activation(k.xs(b, c), k.xs(b, c), ACT.Identity, bias=combc(5)(b, c), scale=1.0)\
                        .then_inc(k.done["act"], 1)

        layer2a = [
            Norm(k.xs, hN, modc(24), modc(32), eps6[:, 0:1]),
            Linear(C, dense(wqkv2, hsrc), *copies(lambda b, g: R(0, g),
                                                  bias=lambda g: col["L2_cond_q_bias"][:, g:g + 1]),
                   load=(l_w[2], 32)),
            Linear(C, lambda b, g: dense(wqkv2, hsrc)(b, g + C), *copies(lambda b, g: R(1, g))),
            Linear(TT, lambda b, g: [(k.hN[:, c, g * P:(g + 1) * P], wqkv2[:, c, 2 * D:3 * D])
                                     for c in range(C)],
                   *copies(lambda b, g: v2[:, g, :])),
            ValueBias(),
            QKNorm(),
            attention(16, 32, lambda h: h // 4, lambda h: h, v2, l_bias[1], all_tiles),
            Linear(C, dense(wo2, asrc), *residual(gamma=modc(16)), only="dve"),
            ProjBias(),
        ]
        norm2b = [Norm(k.xs, k.h2, modc(28), modc(36), eps6[:, 0:1], extra=combc(2))]

        hide = k.R[:, :, :, :].rearrange("p a c t -> p (a c) t")
        gelu_bias = col["L3_cond_b1"]

        def gelu_put(e, b, g, bank):
            return e.activation(hide[:, g, :], bank, ACT.Gelu, bias=gelu_bias[:, g:g + 1], scale=1.0)

        layer3 = [
            Linear(ET, lambda b, g: [(w1e[:, g, :], k.xs(b, g // 4))], gelu_put, None, only="act",
                   load=(l_w[3], 16 * 17)),
            Linear(C, lambda b, g: [(w2e[:, 4 * g + i, :], hide[:, 4 * g + i, :]) for i in range(4)],
                   *copies(hN, bias=lambda g: col["L3_cond_b2"][:, g:g + 1])),
            Norm(hN, hN, combc(3), combc(4), eps5[:, 0:1], func=ACT.Silu),
            Linear(C, dense(wout3, hsrc), *residual(lambda g: col["L3_cond_out_b"][:, g:g + 1]), only="dve"),
        ]

        phases = [([Ada(), Mods()], False), (layer0, True), (layer1a, True), (norm1b, True)]
        for j in range(NCH):
            n = 12 + j
            phases.append(([MlpChunk(j, n % 2, True, (l_m[n % 2], 16 * (n // 2 + 1) if n < 12 else
                                                     16 * 6 + 48 * ((n - 12) // 2 + 1)))], True))
        phases += [(layer2a, True), (norm2b, True)]
        base2 = 16 * 6 + 48 * (NCH // 2)
        for j in range(NCH):
            phases.append(([MlpChunk(j, j % 2, False, (l_m[j % 2], base2 + 32 * (j // 2 + 1)),
                                     col["L2_cond_bfc1"], modc(20))], True))
        phases.append((layer3, True))

        starts, total = [], dict.fromkeys(NAMES, 0)
        for stages, looped in phases:
            starts.append(dict(total))
            for n in NAMES:
                total[n] += (B if looped else 1) * sum(st.n.get(n, 0) for st in stages)
        starts.append(dict(total))
        FIRST1, FIRST2 = 4, 4 + NCH + 2
        L0P, L1P, L2P, L3P = 1, 2, 4 + NCH, len(phases) - 1

        PICK = {"pe": lambda st: st.pe, "act": lambda st: st.act, "dve": lambda st: st.dve,
                "pool": lambda st: st.pool}

        n_const = 8 + len(COLS) + len(MODB) + 1

        def wait_all(e, p):
            for name in NAMES:
                if starts[p][name]:
                    e.wait_ge(k.done[name], starts[p][name])

        def engine(e, name, first, last):
            for (stages, looped), start in list(zip(phases, starts))[first:last]:
                if not any(st.n.get(name, 0) or st.n == {} for st in stages):
                    continue
                per = {n: sum(st.n.get(n, 0) for st in stages) for n in NAMES}

                def body(b):
                    at = {n: start[n] + (b * per[n] if looped else 0) for n in NAMES}
                    for st in stages:
                        PICK[name](st)(k, e, b, at)
                        at = {n: at[n] + st.n.get(n, 0) for n in NAMES}
                if looped:
                    for b in range(B):
                        body(b)
                else:
                    body(0)

        def run_pool(e, first, last):
            engine(e, "pool", first, last)

        block = ctx.enter_context(nc.Block())

        @block.sync
        def _(e):
            e.dma_start(cond[:, 0, :, :], a["condT"].rearrange("(c p) b -> p c b", p=P)).then_inc(l_cond, 16)
            blocks = [("L0_cond_W_ada", 2), ("L1_cond_ln1_tw", 1), ("L1_cond_ln2_tw", 1), ("L2_cond_Wada", 6),
                      ("L3_cond_emb_W", 2)]
            n = 0
            for name, count in blocks:
                for j in range(count):
                    if n >= 2:
                        e.wait_ge(k.done["pe"], n - 1)
                    e.dma_start(k.WM[:, n % 2, 0:C * D].rearrange("p (c m) -> p c m", c=C),
                                rows(name)[:, :, j * D:(j + 1) * D]).then_inc(l_m[n % 2], 16)
                    n += 1
                    if n == 1:
                        for c in range(C):
                            e.dma_start(x[:, c, :, :], a["x"][c * P:(c + 1) * P]).then_inc(l_x, 16)

            def wait_phase(p):
                for name in NAMES:
                    if starts[p][name]:
                        e.wait_ge(k.done[name], starts[p][name])

            for j in range(NCH):
                e.wait_ge(k.done["pe"], 12 if j < 2 else starts[FIRST1 + j - 1]["pe"])
                up = k.WM[:, j % 2, 0:2 * C * HC].rearrange("p (c w m) -> p c w m", c=C, w=2)
                for w, name in enumerate(("L1_cond_Wg", "L1_cond_Wu")):
                    e.dma_start(up[:, :, w, :], rows(name)[:, :, j * HC:(j + 1) * HC]).then_inc(l_m[j % 2], 16)
                e.dma_start(k.WM[:, j % 2, 2 * C * HC:2 * C * HC + 2 * D].rearrange("p (t m) -> p t m", t=2),
                            rows("L1_cond_Wd")[:, 2 * j:2 * j + 2, :]).then_inc(l_m[j % 2], 16)
            for j in range(NCH):
                e.wait_ge(k.done["pe"], starts[FIRST1 + NCH - 1 + j]["pe"] if j < 2 else
                          starts[FIRST2 + j - 1]["pe"])
                e.dma_start(k.WM[:, j % 2, 0:C * HC].rearrange("p (c m) -> p c m", c=C),
                            rows("L2_cond_Wfc1")[:, :, j * HC:(j + 1) * HC]).then_inc(l_m[j % 2], 16)
                e.dma_start(k.WM[:, j % 2, 2 * C * HC:2 * C * HC + 2 * D].rearrange("p (t m) -> p t m", t=2),
                            rows("L2_cond_Wfc2")[:, 2 * j:2 * j + 2, :]).then_inc(l_m[j % 2], 16)
            wait_phase(L3P)
            with e.Fori(0, B) as b:
                per = {n: sum(st.n.get(n, 0) for st in layer3) for n in NAMES}
                e.wait_ge(k.done["dve"], starts[L3P]["dve"] + (b + 1) * per["dve"])
                e.dma_start(out[:, :, one(b), :], x[:, :, one(b), :]).then_inc(s_out, 16)
            e.wait_ge(s_out, 16 * B)

        @block.gpsimd
        def _(e):
            e.dma_start(k.ident[:], a["ident"]).then_inc(l_const, 16)
            e.dma_start(k.ones[:], a["ones"]).then_inc(l_const, 16)
            e.dma_start(k.blockones[:], a["blockones"]).then_inc(l_const, 16)
            e.dma_start(perm[:], a["perm"].rearrange("w p m -> p w m")).then_inc(l_const, 16)
            e.dma_start(k.cosr[:], a["cos0"]).then_inc(l_const, 16)
            e.dma_start(k.sinr[:], a["sin0"]).then_inc(l_const, 16)
            e.dma_start(k.freq[:], a["freq"]).then_inc(l_const, 16)
            e.dma_start(k.sign[:], a["sign"]).then_inc(l_const, 16)
            for name, _ in COLS:
                e.dma_start(col[name], a[name]).then_inc(l_const, 16)
            e.dma_start(k.smul[:], a["L2_cond_scale_mul_log"]).then_inc(l_const, 16)
            e.memset(modb[:], 0.0).then_inc(s_zero, 1)
            e.wait_ge(s_zero, 1)
            for name, t0, n in MODB:
                e.dma_start(modb[:, t0:t0 + n], a[name]).then_inc(l_const, 16)
            e.dma_start(k.bias[:], a["mask0"].rearrange("(i p) t -> p i t", p=P)).then_inc(l_bias[0], 16)
            for dst, name in ((wq0, "L0_cond_Wq"), (wkd, "L0_cond_Wkd"), (wo0, "L0_cond_Wo")):
                e.dma_start(dst, rows(name)).then_inc(l_w[0], 16)
            e.dma_start(wku, a["L0_cond_Wku"]).then_inc(l_w[0], 16)
            e.dma_start(wvu, a["L0_cond_Wvu"]).then_inc(l_w[0], 16)
            for dst, name in ((wq1, "L1_cond_Wq"), (wk1, "L1_cond_Wk"), (wv1, "L1_cond_Wv"), (wo1, "L1_cond_Wo")):
                e.dma_start(dst, rows(name)).then_inc(l_w[1], 16)
            run_pool(e, 0, L1P)
            wait_all(e, L1P)
            e.dma_start(k.pos, a["pos"].rearrange("b t -> (b t)").partition_broadcast(P)
                        .rearrange("p (b t) -> p b t", b=B)).then_inc(k.l_pos, 16)
            e.dma_start(wqkv2, rows("L2_cond_Wqkv")).then_inc(l_w[2], 16)
            e.dma_start(wo2, rows("L2_cond_Wproj")).then_inc(l_w[2], 16)
            run_pool(e, L1P, L1P + 1)
            wait_all(e, L1P + 1)
            e.memset(W1[:, 0:4096], 0.0).then_inc(s_zero, 1)
            e.wait_ge(s_zero, 2)
            for half in range(2):
                src1 = a["L3_cond_W1"].rearrange("(q h) l (t f) -> h l q t f", h=2, t=2)[half]
                dst1 = w1e[64 * half:64 * half + 64].rearrange("l (q h t) f -> l q h t f", h=2, t=2)[:, :, half]
                src2 = a["L3_cond_W2"].rearrange("(q h) (t p) l -> h p q t l", h=2, t=2)[half]
                dst2 = w2e.rearrange("p (q h t) l -> p q h t l", h=2, t=2)[:, :, half, :,
                                                                          64 * half:64 * half + 64]
                for q in range(4):
                    e.dma_start(dst1[:, q], src1[:, q]).then_inc(l_w[3], 16)
                    e.dma_start(dst2[:, q], src2[:, q]).then_inc(l_w[3], 16)
            e.dma_start(wout3, rows("L3_cond_out_W")).then_inc(l_w[3], 16)
            e.dma_start(k.bias[:], a["mask"].rearrange("(i p) t -> p i t", p=P)).then_inc(l_bias[1], 16)
            wait_all(e, L2P)
            e.dma_start(vbias, a["L2_cond_v_bias"].rearrange("o d -> (o d)").partition_broadcast(P))\
                .then_inc(l_vb, 16)
            run_pool(e, L1P + 1, len(phases))

        @block.tensor
        def _(e):
            engine(e, "pe", 0, 1)
            e.wait_ge(l_x, 16 * C)
            e.wait_ge(l_const, 16 * n_const)
            engine(e, "pe", 1, len(phases))

        @block.vector
        def _(e):
            engine(e, "dve", 0, 1)
            e.wait_ge(l_x, 16 * C)
            engine(e, "dve", 1, len(phases))

        @block.scalar
        def _(e):
            engine(e, "act", 0, 1)
            e.wait_ge(l_x, 16 * C)
            engine(e, "act", 1, len(phases))


def _layout(inputs):
    g = {n: np.asarray(v) for n, v in inputs.items()}
    T_ = lambda w: np.ascontiguousarray(w.T)
    column = lambda v: np.ascontiguousarray(v.reshape(-1, P).T)
    o = {"x": np.ascontiguousarray(g["x"].transpose(2, 0, 1)), "condT": T_(g["cond_2048"]),
         "pos": g["pos_BxS"], "mask": np.ascontiguousarray(g["mask_1x1xSxS_ff0"][0, 0])}
    for n in ("L0_cond_W_ada", "L0_cond_Wq", "L0_cond_Wkd", "L0_cond_Wvu", "L0_cond_Wo", "L1_cond_ln1_tw",
              "L1_cond_ln2_tw", "L1_cond_Wq", "L1_cond_Wv", "L1_cond_Wo", "L1_cond_Wg", "L1_cond_Wu",
              "L1_cond_Wd", "L2_cond_Wqkv", "L2_cond_Wproj", "L2_cond_Wada", "L2_cond_Wfc1", "L2_cond_Wfc2"):
        o[n] = T_(g[n])
    o["L0_cond_Wku"] = T_(np.repeat(g["L0_cond_Wku"].reshape(4, 1, 32, P), 4, axis=1).reshape(D, P))
    o["L1_cond_Wk"] = T_(np.concatenate([g["L1_cond_Wk"]] * 2))
    for n in ("L3_cond_emb_W", "L3_cond_W1", "L3_cond_W2", "L3_cond_out_W"):
        o[n] = g[n]
    for n in ("L1_cond_ln1_w", "L1_cond_ln2_w", "L2_cond_q_bias", "L2_cond_bproj", "L2_cond_bfc1",
              "L2_cond_bfc2", "L3_cond_b1", "L3_cond_b2", "L3_cond_ln_g", "L3_cond_ln_b", "L3_cond_out_b",
              "L0_cond_b_ada", "L2_cond_bada", "L3_cond_emb_b"):
        o[n] = column(g[n])
    o["L2_cond_v_bias"] = g["L2_cond_v_bias"].reshape(1, D)
    o["L2_cond_scale_mul_log"] = column(np.repeat(g["L2_cond_scale_mul_log"].reshape(16), 32))
    return {n: np.ascontiguousarray(v) for n, v in o.items()}


def _constants():
    f = np.float32
    eye = np.eye(P, dtype=f)
    o = {"ident": eye, "ones": np.full((P, P), 1 / D, f),
         "blockones": np.kron(np.eye(4, dtype=f), np.ones((32, 32), f))}
    o["perm"] = np.stack([np.kron(np.eye(P // d), np.roll(np.eye(d), d // 2, axis=0)).astype(f)
                          for d in (32, 64)])
    row = np.arange(P)
    f32 = (1.0 / f(10000.0) ** (np.arange(0, 32, 2, dtype=f) / f(32))).astype(f)
    ang = (np.arange(T, dtype=f)[None, :] * f32[row % 16][:, None]).astype(f)
    sgn = np.where(row % 32 < 16, -1, 1).astype(f)[:, None]
    o["cos0"], o["sin0"] = np.cos(ang), np.sin(ang) * sgn
    f64 = (1.0 / f(10000.0) ** (np.arange(0, 64, 2, dtype=f) / f(64))).astype(f)
    o["freq"] = f64[row % 32][:, None]
    o["sign"] = np.where(row % 64 < 32, -1, 1).astype(f)[:, None]
    i = np.arange(T)
    hidden = (np.abs(i[None] - i[:, None]) > 64) & ~(i % 64 == 0)[None] | (i[None] // P > i[:, None] // P)
    o["mask0"] = np.where(hidden, f(-1e30), f(0))
    return {n: np.ascontiguousarray(v, dtype=f) for n, v in o.items()}


def kernel(**inputs):
    import concourse.bacc as _bacc
    from concourse.bass_utils import run_bass_kernel_spmd as _run

    nc = _bacc.Bacc("TRN2", target_bir_lowering=False, num_devices=1)
    arrays, aps = {}, {}
    for name, v in {**_layout(inputs), **_constants()}.items():
        arrays["in_" + name] = v
        aps[name] = nc.dram_tensor("in_" + name, v.shape, mybir.dt.from_np(v.dtype), kind="ExternalInput").ap()
    out = nc.dram_tensor("out_x", (P, C, B, T), F32, kind="ExternalOutput").ap()
    conditioned_stack(nc, aps, out)
    r = _run(nc, [arrays], core_ids=[0])
    return np.ascontiguousarray(r.results[0]["out_x"].transpose(2, 3, 1, 0)).reshape(B, T, D)
```

```python
from contextlib import ExitStack

import numpy as np
import concourse.bass as bass
from concourse import mybir

F32 = mybir.dt.float32
F32R = mybir.dt.float32r
I32 = mybir.dt.int32
ALU = mybir.AluOpType
ACT = mybir.ActivationFunctionType
AX_X = mybir.AxisListType.X

P = 128
B, T, D = 4, 512, 512
C = D // P
TT = T // P
HID = 2048
HC = 256
NCH = HID // HC
EXP, LAT, FFN = 8, 64, 256
ET = EXP * FFN // P
NAMES = ("pe", "act", "dve", "pool")


class Step:

    n = {}

    def pe(self, k, e, b, at): pass
    def act(self, k, e, b, at): pass
    def dve(self, k, e, b, at): pass
    def pool(self, k, e, b, at): pass


def start_wait(k, e, at, *names):
    for name in names:
        if not (isinstance(at[name], int) and at[name] == 0):
            e.wait_ge(k.done[name], at[name])


class Norm(Step):

    def __init__(s, src, A, Bias, eps, rms=False, func=None, pair=None, extra=None):
        s.src, s.A, s.Bias, s.eps, s.rms, s.pair, s.extra = src, A, Bias, eps, rms, pair, extra
        s.func = func or ACT.Identity
        s.m = 0 if rms else 1
        s.n = {"pe": 1 + s.m, "dve": s.m * C + 1 + C + (C if pair else 0),
               "act": C + 1 + s.m * C + (C if pair else 0) + (C if extra else 0)}

    def centred(s, k, b, c):
        return s.src(b, c) if s.rms else k.hN[:, c, :]

    def pe(s, k, e, b, at):
        start_wait(k, e, at, "act", "dve", "pool")
        if not s.rms:
            for c in range(C):
                mm = e.matmul(k.bank(0), k.ones[:], s.src(b, c), start=c == 0, stop=c == C - 1)
            mm.then_inc(k.done["pe"], 1)
        for c in range(C):
            e.wait_ge(k.done["act"], at["act"] + c + 1)
            mm = e.matmul(k.bank(1), k.ones[:], k.t1[:, c, :], start=c == 0, stop=c == C - 1)
        mm.then_inc(k.done["pe"], 1)

    def dve(s, k, e, b, at):
        start_wait(k, e, at, "act", "dve", "pe", "pool")
        n = s.m * C
        if not s.rms:
            e.wait_ge(k.done["pe"], at["pe"] + 1)
            for c in range(C):
                e.tensor_tensor(k.hN[:, c, :], s.src(b, c), k.bank(0), ALU.subtract)\
                    .then_inc(k.done["dve"], 1)
        e.wait_ge(k.done["act"], at["act"] + C + 1)
        e.reciprocal(k.rstd, k.sd).then_inc(k.done["dve"], 1)
        e.wait_ge(k.done["dve"], at["dve"] + n + 1)
        for c in range(C):
            e.scalar_tensor_tensor(out=k.hN[:, c, :], in0=s.centred(k, b, c), scalar=s.A(b, c),
                                   in1=k.rstd, op0=ALU.mult, op1=ALU.mult)\
                .then_inc(k.done["dve"], 1)
        if s.pair:
            for c in range(C):
                e.wait_ge(k.done["act"], at["act"] + C + 1 + s.m * C + c + 1)
                high = s.pair[0](b, c).bitcast(F32)
                e.tensor_tensor(s.pair[1](b, c), k.hN[:, c, :], high, ALU.subtract)\
                    .then_inc(k.done["dve"], 1)

    def act(s, k, e, b, at):
        start_wait(k, e, at, "act", "dve", "pe", "pool")
        for c in range(C):
            if not s.rms:
                e.wait_ge(k.done["dve"], at["dve"] + c + 1)
            e.activation(k.t1[:, c, :], s.centred(k, b, c), ACT.Square).then_inc(k.done["act"], 1)
        e.wait_ge(k.done["pe"], at["pe"] + s.n["pe"])
        e.activation(k.sd, k.bank(1), ACT.Sqrt, bias=s.eps, scale=1.0)\
            .then_inc(k.done["act"], 1)
        if not s.rms:
            for c in range(C):
                e.wait_ge(k.done["dve"], at["dve"] + C + 1 + c + 1)
                e.activation(k.hN[:, c, :], k.hN[:, c, :], s.func, bias=s.Bias(b, c), scale=1.0)\
                    .then_inc(k.done["act"], 1)
        if s.pair:
            for c in range(C):
                if s.rms:
                    e.wait_ge(k.done["dve"], at["dve"] + 1 + c + 1)
                else:
                    e.wait_ge(k.done["act"], at["act"] + C + 1 + c + 1)
                e.activation(s.pair[0](b, c), k.hN[:, c, :], ACT.Copy).then_inc(k.done["act"], 1)
        if s.extra is not None:
            e.wait_ge(k.done["dve"], at["dve"] + s.m * C + 1 + C)
            for c in range(C):
                e.activation(s.src(b, c), s.src(b, c), ACT.Identity, bias=s.extra(b, c), scale=1.0)\
                    .then_inc(k.done["act"], 1)


class Linear(Step):

    def __init__(s, groups, mats, put_act, put_dve, width=T, only=None, load=None):
        s.groups, s.mats, s.put_act, s.put_dve, s.width, s.only = groups, mats, put_act, put_dve, width, only
        s.load = load
        to_act = [s.by(g) == "act" for g in range(groups)]
        s.n = {"pe": groups, "act": sum(to_act), "dve": groups - sum(to_act)}

    def by(s, g):
        return s.only or ("act" if g % 2 == 0 else "dve")

    def count(s, g):
        return sum(s.by(i) == s.by(g) for i in range(g + 1))

    def pe(s, k, e, b, at):
        start_wait(k, e, at, "act", "dve", "pool")
        if s.load is not None:
            e.wait_ge(*s.load)
        for g in range(s.groups):
            if g >= 4:
                f = g - 4
                e.wait_ge(k.done[s.by(f)], at[s.by(f)] + s.count(f))
            mats = s.mats(b, g)
            for i, (lhsT, rhs) in enumerate(mats):
                mm = e.matmul(k.bank(g % 4)[:, 0:s.width], lhsT, rhs,
                              start=i == 0, stop=i == len(mats) - 1)
            mm.then_inc(k.done["pe"], 1)

    def act(s, k, e, b, at):
        if s.n["act"]:
            start_wait(k, e, at, "act", "dve", "pe", "pool")
        for g in range(s.groups):
            if s.by(g) == "act":
                e.wait_ge(k.done["pe"], at["pe"] + g + 1)
                s.put_act(e, b, g, k.bank(g % 4)[:, 0:s.width]).then_inc(k.done["act"], 1)

    def dve(s, k, e, b, at):
        if s.n["dve"]:
            start_wait(k, e, at, "act", "dve", "pe", "pool")
        for g in range(s.groups):
            if s.by(g) == "dve":
                e.wait_ge(k.done["pe"], at["pe"] + g + 1)
                s.put_dve(e, b, g, k.bank(g % 4)[:, 0:s.width]).then_inc(k.done["dve"], 1)


class Rope(Step):

    def __init__(s, tiles, perm, cos, sin):
        s.tiles, s.perm, s.cos, s.sin = tiles, perm, cos, sin
        s.n = {"pe": len(tiles), "dve": 2 * len(tiles), "pool": len(tiles)}

    def pe(s, k, e, b, at):
        start_wait(k, e, at, "act", "dve", "pool")
        for g, z in enumerate(s.tiles):
            if g >= 4:
                e.wait_ge(k.done["dve"], at["dve"] + g - 3)
            e.matmul(k.bank(g % 4), s.perm, z, start=True, stop=True).then_inc(k.done["pe"], 1)

    def dve(s, k, e, b, at):
        start_wait(k, e, at, "act", "dve", "pe", "pool")
        for g in range(len(s.tiles)):
            e.wait_ge(k.done["pe"], at["pe"] + g + 1)
            e.tensor_tensor(k.ropet[:, g, :], k.bank(g % 4), s.sin, ALU.mult).then_inc(k.done["dve"], 1)
        for g, z in enumerate(s.tiles):
            e.wait_ge(k.done["dve"], at["dve"] + g + 1)
            e.wait_ge(k.done["pool"], at["pool"] + g + 1)
            e.tensor_tensor(z, z, k.ropet[:, g, :], ALU.add).then_inc(k.done["dve"], 1)

    def pool(s, k, e, b, at):
        start_wait(k, e, at, "act", "dve", "pe", "pool")
        for g, z in enumerate(s.tiles):
            e.wait_ge(k.done["pe"], at["pe"] + g + 1)
            e.tensor_tensor(z, z, s.cos, ALU.mult).then_inc(k.done["pool"], 1)


class Angles(Step):

    n = {"dve": 14, "act": 2}
    C1 = 6.28125
    C2 = float(np.float32(2 * np.pi - 6.28125))
    C3 = float(2 * np.pi - 6.28125 - float(np.float32(2 * np.pi - 6.28125)))
    MAGIC = 12582912.0
    TOP = 3.1415925

    def dve(s, k, e, b, at):
        start_wait(k, e, at, "act", "dve", "pe", "pool")
        done = [0]

        def inc(ins):
            done[0] += 1
            ins.then_inc(k.done["dve"], 1)
            e.wait_ge(k.done["dve"], at["dve"] + done[0])

        e.wait_ge(k.l_pos, 16)
        ang, kk, r = k.Pb[:, 0, :], k.Pb[:, 1, :], k.scratch[:, 2, :]
        inc(e.tensor_copy(kk, k.pos[:, bass.ds(b, 1), :].rearrange("p o t -> p (o t)")))
        inc(e.tensor_scalar(ang, kk, k.freq[:, 0:1], None, ALU.mult))
        for src, parts, out in ((ang, (s.C1, s.C2, s.C3), k.sint), (r, (s.C1, s.C2), k.cost)):
            inc(e.tensor_scalar(kk, src, 1 / (2 * np.pi), s.MAGIC, ALU.mult, ALU.add))
            inc(e.tensor_scalar(kk, kk, s.MAGIC, None, ALU.subtract))
            for part in parts:
                inc(e.scalar_tensor_tensor(out=r, in0=kk, scalar=-part, in1=src, op0=ALU.mult, op1=ALU.add))
                src = r
            inc(e.tensor_scalar(out, r, s.TOP, -s.TOP, ALU.min, ALU.max))
            if out is k.sint:
                inc(e.tensor_scalar(r, r, float(np.pi / 2), None, ALU.add))
        assert done[0] == s.n["dve"], done

    def act(s, k, e, b, at):
        start_wait(k, e, at, "act", "dve", "pe", "pool")
        e.wait_ge(k.done["dve"], at["dve"] + s.n["dve"])
        e.activation(k.sinr[:], k.sint, ACT.Sin).then_inc(k.done["act"], 1)
        e.activation(k.cosr[:], k.cost, ACT.Sin).then_inc(k.done["act"], 1)


class Sign(Step):

    n = {"dve": 1}

    def dve(s, k, e, b, at):
        start_wait(k, e, at, "act", "dve", "pe", "pool")
        e.tensor_scalar(k.sinr[:], k.sinr[:], k.sign[:, 0:1], None, ALU.mult).then_inc(k.done["dve"], 1)


class QKNorm(Step):

    n = {"act": 2 * 2 * C, "pe": 2 * C, "dve": 3 * 2 * C}

    def tile(s, k, g):
        return k.R[:, g // C, g % C, :]

    def pe(s, k, e, b, at):
        start_wait(k, e, at, "act", "dve", "pool")
        for g in range(2 * C):
            e.wait_ge(k.done["act"], at["act"] + s.sq(g))
            e.matmul(k.bank(g % 4), k.blockones[:], k.t1[:, g % 4, :], start=True, stop=True)\
                .then_inc(k.done["pe"], 1)

    def sq(s, g):
        return 1 if g == 0 else 2 * g

    def rt(s, g):
        return 2 * g + 3 if g < 2 * C - 1 else 4 * C

    def act(s, k, e, b, at):
        start_wait(k, e, at, "act", "dve", "pe", "pool")
        for g in range(2 * C + 1):
            if g < 2 * C:
                if g >= 4:
                    e.wait_ge(k.done["pe"], at["pe"] + g - 3)
                e.activation(k.t1[:, g % 4, :], s.tile(k, g), ACT.Square).then_inc(k.done["act"], 1)
            if g >= 1:
                f = g - 1
                e.wait_ge(k.done["pe"], at["pe"] + f + 1)
                if f >= 4:
                    e.wait_ge(k.done["dve"], at["dve"] + 3 * (f - 3))
                e.activation(k.ropet[:, f % 4, :], k.bank(f % 4), ACT.Sqrt).then_inc(k.done["act"], 1)

    def dve(s, k, e, b, at):
        start_wait(k, e, at, "act", "dve", "pe", "pool")
        for g in range(2 * C):
            e.wait_ge(k.done["act"], at["act"] + s.rt(g))
            r = k.ropet[:, g % 4, :]
            e.tensor_scalar(r, r, 1e-12, None, ALU.max).then_inc(k.done["dve"], 1)
            e.wait_ge(k.done["dve"], at["dve"] + 3 * g + 1)
            e.reciprocal(r, r).then_inc(k.done["dve"], 1)
            e.wait_ge(k.done["dve"], at["dve"] + 3 * g + 2)
            z = s.tile(k, g)
            scale = k.smul[:, g:g + 1] if g < C else 1.0
            e.scalar_tensor_tensor(out=z, in0=z, scalar=scale, in1=r, op0=ALU.mult, op1=ALU.mult)\
                .then_inc(k.done["dve"], 1)


def three(wh, wl, xh, xl):
    return [(wh, xh), (wh, xl), (wl, xh)]


class Split(Step):

    def __init__(s, tiles):
        s.tiles = tiles
        s.n = {"act": len(tiles), "dve": len(tiles)}

    def act(s, k, e, b, at):
        start_wait(k, e, at, "act", "dve", "pe", "pool")
        for src, high, low in s.tiles:
            e.activation(high, src, ACT.Copy).then_inc(k.done["act"], 1)

    def dve(s, k, e, b, at):
        start_wait(k, e, at, "act", "dve", "pe", "pool")
        for g, (src, high, low) in enumerate(s.tiles):
            e.wait_ge(k.done["act"], at["act"] + g + 1)
            e.tensor_tensor(low, src, high.bitcast(F32), ALU.subtract).then_inc(k.done["dve"], 1)


class Ordered(Step):

    def number(s, orders):
        s.orders = orders
        s.i = {op: (name, n + 1) for name, order in orders.items() for n, op in enumerate(order)}
        s.n = {name: len(order) for name, order in orders.items()}

    def wait(s, k, e, at, kind, index):
        name, n = s.i[(kind, index)]
        e.wait_ge(k.done[name], at[name] + n)


class Attention(Ordered):

    PARTS = 3

    def __init__(s, H, khead, vhead, bias_loaded, tiles_of, V, Vz):
        s.V, s.Vz = V, Vz
        s.H, s.khead, s.vhead, s.bias_loaded, s.tiles_of = H, khead, vhead, bias_loaded, tiles_of
        s.biased = bias_loaded is not None
        s.dv = D // H
        s.per = H // C
        s.U = TT * H
        pe, act, dve = [], [], []
        pool = [("pad q", (0, p)) for p in range(2)]
        for h in range(H):
            pool += [("pad q", (h + 1, p)) for p in range(2) if h + 1 < H]
            pool += [("pad v", (h, p)) for p in range(2)]
        last = s.U - 1
        for t in range(s.U + 12):
            if t == 0:
                pe.append(("scores", 0))
            if t < last:
                pe.append(("scores", t + 1))
            if t - 1 in range(s.U):
                dve.append(("recip", t - 1))
            if t <= last:
                dve.append(("max", t))
                act.append(("exp", t))
            if t - 2 in range(s.U):
                dve.append(("low", t - 2))
            if t - 1 in range(s.U):
                dve.append(("high", t - 1))
            if t - 2 in range(s.U):
                pe.append(("turn high", t - 2))
                act.append(("copy high", t - 2))
            if t - 3 in range(s.U):
                pe.append(("turn low", t - 3))
                act.append(("copy low", t - 3))
            h, part = divmod(t - 7, TT)
            if h in range(H) and part < s.PARTS:
                pe.append(("values", (h, part)))
                if h % s.per == s.per - 1 and part == s.PARTS - 1:
                    act.append(("outcopy", h // s.per))
        s.number({"pe": pe, "act": act, "dve": dve, "pool": pool})

    def S(s, k, u):
        return k.bank((0, 1, 7)[u % 3])

    def width(s, u):
        return P * s.tiles_of(u % TT)

    def turned(s, k, u, p):
        return k.bank(2 + 2 * (u % 2) + p)[:, 0:s.width(u)]

    def pool(s, k, e, b, at):
        start_wait(k, e, at, "act", "dve", "pe", "pool")
        for kind, (h, p) in s.orders["pool"]:
            if kind == "pad q":
                if h >= 2:
                    s.wait(k, e, at, "scores", (h - 2) * TT + TT - 1)
                ins = e.tensor_tensor(k.Qz[p][:, h % 2, :], k.Q[p][:, h // s.per, :].bitcast(F32),
                                      k.heads[s.per][:, h % s.per:h % s.per + 1].to_broadcast([P, T]), ALU.mult)
            else:
                if h >= 2:
                    s.wait(k, e, at, "values", (h - 2, s.PARTS - 1))
                v = s.V[p][:, :, s.vhead(h) * s.dv:(s.vhead(h) + 1) * s.dv].bitcast(F32)
                shape = [P, TT, s.per, s.dv]
                ins = e.tensor_tensor(s.Vz[p][:, h % 2].rearrange("p j (a d) -> p j a d", a=s.per),
                                      v.unsqueeze(2).to_broadcast(shape),
                                      k.places[s.per][:, h % s.per].unsqueeze(1).unsqueeze(3).to_broadcast(shape),
                                      ALU.mult)
            ins.then_inc(k.done["pool"], 1)

    def pe(s, k, e, b, at):
        start_wait(k, e, at, "act", "dve", "pool")
        for kind, u in s.orders["pe"]:
            if kind != "values":
                h, i = divmod(u, TT)
                n = s.tiles_of(i)
            if kind == "scores":
                s.wait(k, e, at, "pad q", (h, 1))
                if u >= 3:
                    s.wait(k, e, at, "max" if s.biased else "exp", u - 3)
                w = P * max(n, 2)
                mats = three(*[k.Qz[p][:, h % 2, i * P:(i + 1) * P] for p in range(2)],
                             *[k.K[p][:, s.khead(h), 0:w] for p in range(2)])
                for m, (lhsT, rhs) in enumerate(mats):
                    mm = e.matmul(s.S(k, u)[:, 0:w], lhsT, rhs, start=m == 0, stop=m == 2)
            elif kind.startswith("turn"):
                p = int(kind == "turn low")
                s.wait(k, e, at, ("high", "low")[p], u)
                if u >= 2:
                    s.wait(k, e, at, ("copy high", "copy low")[p], u - 2)
                for j in range(n):
                    mm = e.transpose(s.turned(k, u, p)[:, j * P:(j + 1) * P].bitcast(F32R),
                                     k.Pr[p][:, u % 2, j * P:(j + 1) * P], k.identr[:])
            else:
                h, part = u
                if part == 0:
                    s.wait(k, e, at, "pad v", (h, 1))
                    s.wait(k, e, at, "copy low", h * TT + TT - 1)
                    if h % s.per == 0 and h >= s.per:
                        s.wait(k, e, at, "outcopy", h // s.per - 1)
                mats = []
                for j in range(TT):
                    first = min(q for q in range(TT) if s.tiles_of(q) > j) * P
                    mats += [(v, pt, first) for v, pt in
                             three(*[s.Vz[p][:, h % 2, j, :] for p in range(2)],
                                   *[k.PT[p][:, h % 2, j, first:T] for p in range(2)])]
                each = len(mats) // s.PARTS
                for m in range(part * each, (part + 1) * each):
                    lhsT, rhs, first = mats[m]
                    mm = e.matmul(k.bank(6)[:, first:T], lhsT, rhs,
                                  start=h % s.per == 0 and m == 0,
                                  stop=h % s.per == s.per - 1 and m == len(mats) - 1)
            mm.then_inc(k.done["pe"], 1)

    def dve(s, k, e, b, at):
        start_wait(k, e, at, "act", "dve", "pe", "pool")
        for kind, u in s.orders["dve"]:
            src = k.hN[:, u % C, 0:s.width(u)]
            high = k.Pr[0][:, u % 2, 0:s.width(u)]
            rsum = k.rsum[:, u:u + 1]
            if kind == "max":
                s.wait(k, e, at, "scores", u)
                if s.biased:
                    if u >= C:
                        s.wait(k, e, at, "low", u - C)
                    e.wait_ge(s.bias_loaded, 16)
                    ins = e.tensor_tensor_reduce(src, s.S(k, u)[:, 0:s.width(u)], k.bias[:, u % TT, 0:s.width(u)],
                                                 -1.0, 3.0e38, ALU.add, ALU.min, k.nmax[:, u:u + 1])
                else:
                    ins = e.tensor_reduce(k.nmax[:, u:u + 1], s.S(k, u)[:, 0:s.width(u)], AX_X, ALU.max, negate=True)
            elif kind == "recip":
                s.wait(k, e, at, "exp", u)
                ins = e.reciprocal(rsum, k.sums[:, u:u + 1])
            elif kind == "high":
                s.wait(k, e, at, "recip", u)
                if u >= 2:
                    s.wait(k, e, at, "turn high", u - 2)
                ins = e.tensor_scalar(high, src, rsum, None, ALU.mult)
            else:
                s.wait(k, e, at, "high", u)
                if u >= 2:
                    s.wait(k, e, at, "turn low", u - 2)
                ins = e.scalar_tensor_tensor(out=k.Pr[1][:, u % 2, 0:s.width(u)], in0=src, scalar=rsum,
                                             in1=high.bitcast(F32), op0=ALU.mult, op1=ALU.subtract)
            ins.then_inc(k.done["dve"], 1)

    def act(s, k, e, b, at):
        start_wait(k, e, at, "act", "dve", "pe", "pool")
        for kind, u in s.orders["act"]:
            h, i = divmod(u, TT)
            if kind == "exp":
                s.wait(k, e, at, "max", u)
                dst = k.hN[:, u % C, 0:s.width(u)]
                if not s.biased and u >= C:
                    s.wait(k, e, at, "low", u - C)
                ins = e.activation(dst, dst if s.biased else s.S(k, u)[:, 0:s.width(u)], ACT.Exp, bias=k.nmax[:, u:u + 1],
                                   scale=-1.0 if s.biased else 1.0, accum_out=k.sums[:, u:u + 1])
            elif kind.startswith("copy"):
                p = int(kind == "copy low")
                s.wait(k, e, at, ("turn high", "turn low")[p], u)
                if h >= 2:
                    s.wait(k, e, at, "values", (h - 2, s.PARTS - 1))
                ins = e.activation(k.PT[p][:, h % 2, 0:s.tiles_of(i), i * P:(i + 1) * P],
                                   s.turned(k, u, p).rearrange("p (j q) -> p j q", q=P), ACT.Copy)
            else:
                s.wait(k, e, at, "values", ((u + 1) * s.per - 1, s.PARTS - 1))
                ins = e.activation(k.t1[:, u, :], k.bank(6), ACT.Copy)
            ins.then_inc(k.done["act"], 1)


class Mlp(Ordered):

    def __init__(s, gated, pieces, loaded, hbias=None, gamma=None):
        s.gated, s.pieces, s.loaded, s.hbias, s.gamma = gated, pieces, loaded, hbias, gamma
        s.S = NCH * B
        s.ups = 2 if gated else 1
        pe, act, dve = [], [], []
        for p in range(len(pieces)):
            dve += [("high", p), ("low", p)]
        for st in range(s.S + 1):
            if st < s.S:
                pe += [("up", (st, t, w)) for t in range(2) for w in range(s.ups)]
                for t in range(2):
                    act.append(("act", (st, t)))
                    if gated:
                        dve.append(("gate", (st, t)))
                    act.append(("hidden high", (st, t)))
                    dve.append(("hidden low", (st, t)))
                j, b = divmod(st, B)
                if j + 1 < NCH and b in (1, 2):
                    for p in range(len(pieces)):
                        if b == 1 + p % 2:
                            dve += [("high", (j + 1) * len(pieces) + p), ("low", (j + 1) * len(pieces) + p)]
            if st >= 1:
                pe += [("down", (st - 1, m)) for m in range(C)]
                dve += [("add", (st - 1, m)) for m in range(C)]
        s.number({"pe": pe, "act": act, "dve": dve})

    def split_free(s, k, e, at, n):
        j = n // len(s.pieces)
        if j >= 2:
            s.wait(k, e, at, "down", ((j - 1) * B - 1, C - 1))

    def pe(s, k, e, b, at):
        start_wait(k, e, at, "act", "dve", "pool")
        for kind, index in s.orders["pe"]:
            if kind == "up":
                st, t, w = index
                j, q = divmod(st, B)
                if q == 0 and t == 0 and w == 0:
                    s.wait(k, e, at, "low", (j + 1) * len(s.pieces) - 1)
                if st >= 1:
                    s.wait(k, e, at, "gate" if s.gated else "act", (st - 1, t))
                    if not s.gated:
                        s.wait(k, e, at, "hidden high", (st - 1, t))
                mats = [m for c in range(C) for m in
                        three(*[s.up(v, j % 2, c, w, t) for v in range(2)], k.HH(q, c), k.HL(q, c))]
                for i, (lhsT, rhs) in enumerate(mats):
                    mm = e.matmul(k.bank(s.ups * t + w), lhsT, rhs, start=i == 0, stop=i == len(mats) - 1)
                mm.then_inc(k.done["pe"], 1)
            else:
                st, m = index
                j = st // B
                if m == 0:
                    s.wait(k, e, at, "hidden low", (st, 1))
                if st >= 1:
                    s.wait(k, e, at, "add", (st - 1, m))
                mats = [mt for t in range(2) for mt in
                        three(*[s.down(v, j % 2, t, m) for v in range(2)],
                              k.hidH[:, st % 2, t, :], k.hidL[:, st % 2, t, :])]
                for i, (lhsT, rhs) in enumerate(mats):
                    mm = e.matmul(k.bank(4 + m), lhsT, rhs, start=i == 0, stop=i == len(mats) - 1)
                mm.then_inc(k.done["pe"], 1)

    def act(s, k, e, b, at):
        start_wait(k, e, at, "act", "dve", "pe", "pool")
        for kind, (st, t) in s.orders["act"]:
            if kind == "act":
                s.wait(k, e, at, "up", (st, t, 0))
                if st >= 2:
                    s.wait(k, e, at, "hidden low", (st - 2, t))
                if s.gated:
                    if st >= 1:
                        s.wait(k, e, at, "gate", (st - 1, t))
                    ins = e.activation(k.t1[:, t, :], k.bank(2 * t), ACT.Silu)
                else:
                    ins = e.activation(k.hN[:, 2 * (st % 2) + t, :], k.bank(t), ACT.Gelu_apprx_tanh,
                                       bias=s.hbias[:, 2 * (st // B) + t:2 * (st // B) + t + 1], scale=1.0)
            else:
                s.wait(k, e, at, "gate" if s.gated else "act", (st, t))
                if st >= 2:
                    s.wait(k, e, at, "down", (st - 2, C - 1))
                ins = e.activation(k.hidH[:, st % 2, t, :], k.hN[:, 2 * (st % 2) + t, :], ACT.Copy)
            ins.then_inc(k.done["act"], 1)

    def dve(s, k, e, b, at):
        start_wait(k, e, at, "act", "dve", "pe", "pool")
        for kind, index in s.orders["dve"]:
            if kind == "high":
                sem, value = s.loaded(index)
                e.wait_ge(sem, value)
                s.split_free(k, e, at, index)
                j, p = divmod(index, len(s.pieces))
                o, w = s.pieces[p]
                ins = e.tensor_copy(k.Wsplit[0][:, j % 2, o:o + w], k.staged(index, w))
            elif kind == "low":
                s.wait(k, e, at, "high", index)
                j, p = divmod(index, len(s.pieces))
                o, w = s.pieces[p]
                ins = e.tensor_tensor(k.Wsplit[1][:, j % 2, o:o + w], k.staged(index, w),
                                      k.Wsplit[0][:, j % 2, o:o + w].bitcast(F32), ALU.subtract)
            elif kind == "gate":
                st, t = index
                s.wait(k, e, at, "act", index)
                s.wait(k, e, at, "up", (st, t, 1))
                if st >= 2:
                    s.wait(k, e, at, "hidden high", (st - 2, t))
                ins = e.tensor_tensor(k.hN[:, 2 * (st % 2) + t, :], k.t1[:, t, :], k.bank(2 * t + 1), ALU.mult)
            elif kind == "hidden low":
                st, t = index
                s.wait(k, e, at, "hidden high", index)
                if st >= 2:
                    s.wait(k, e, at, "down", (st - 2, C - 1))
                ins = e.tensor_tensor(k.hidL[:, st % 2, t, :], k.hN[:, 2 * (st % 2) + t, :],
                                      k.hidH[:, st % 2, t, :].bitcast(F32), ALU.subtract)
            else:
                st, m = index
                q = st % B
                s.wait(k, e, at, "down", index)
                if st >= B:
                    s.wait(k, e, at, "add", (st - B, m))
                ins = e.scalar_tensor_tensor(out=k.xs(q, m), in0=k.bank(4 + m),
                                             scalar=1.0 if s.gamma is None else s.gamma(q, m),
                                             in1=k.xs(q, m), op0=ALU.mult, op1=ALU.add)
            ins.then_inc(k.done["dve"], 1)


class Kit:
    pass


def conditioned_stack(nc, a, out):
    ctx = ExitStack()
    with ctx:
        def sb(name, shape, dt=F32):
            return ctx.enter_context(nc.sbuf_tensor("sb_" + name, shape, dt))

        def sem(name):
            return ctx.enter_context(nc.semaphore(name))

        k = Kit()
        psum = ctx.enter_context(nc.psum_tensor("banks", [P, 8, 512], F32))
        k.bank = lambda i: psum[:, i, :]
        x = sb("x", [P, C, B, T])
        k.hN = sb("hN", [P, C, T])
        k.t1 = sb("t1", [P, C, T])
        k.Pb = sb("Pb", [P, 2, T])
        k.sd, k.rstd = k.Pb[:, 0, :], k.Pb[:, 1, :]
        k.cosr = sb("cos", [P, T])
        k.sinr = sb("sin", [P, T])
        k.ident = sb("ident", [P, P])
        k.ones = sb("ones", [P, P])
        perm = sb("perm", [P, 2, P])
        k.heads = {2: sb("heads2", [P, 2])[:], 4: sb("heads4", [P, 4])[:]}
        k.places = {n: sb(f"places{n}", [P, n, n])[:] for n in (2, 4)}
        k.identr = sb("identr", [P, P], F32R)
        k.blockones = sb("blockones", [P, P])
        k.freq = sb("freq", [P, 1])
        k.sign = sb("sign", [P, 1])
        k.nmax = sb("nmax", [P, 64])
        k.sums = sb("sums", [P, 64])
        k.rsum = sb("rsum", [P, 64])
        k.smul = sb("smul", [P, C])
        cond = sb("cond", [P, 2, C, B])
        ADA = 48
        mod = sb("mod", [P, ADA, B])
        modb = sb("modb", [P, ADA])
        cols = sb("cols", [P, 80])
        eps5 = sb("eps5", [P, 1])
        eps6 = sb("eps6", [P, 1])
        comb = sb("comb", [P, 6, C, B])
        def over(scope, name, shape, dt=F32):
            return scope.enter_context(nc.sbuf_tensor("sb_" + name, shape, dt))

        with ExitStack() as inner:
            hide = over(inner, "experts", [P, ET, T])
        with ExitStack() as attention_scope:
            with ExitStack() as inner:
                k.Pr = [over(inner, f"Pr{i}", [P, 2, T], F32R) for i in range(2)]
                k.Qz = [over(inner, f"Qz{i}", [P, 2, T], F32R) for i in range(2)]
            k.R = over(attention_scope, "R", [P, 2, C, T])
            k.V = [over(attention_scope, f"V{i}", [P, TT, D], F32R) for i in range(2)]
            k.Q = [over(attention_scope, f"Q{i}", [P, C, T], F32R) for i in range(2)]
            k.K = [over(attention_scope, f"K{i}", [P, C, T], F32R) for i in range(2)]
            with ExitStack() as inner:
                over(inner, "W_used", [P, 8192])
                Vz2 = [over(inner, f"Vz{i}", [P, 2, TT, P], F32R) for i in range(2)]
            W = over(attention_scope, "W", [P, 10240])
            k.bias = over(attention_scope, "bias", [P, TT, T])
            with ExitStack() as inner:
                k.scratch = over(inner, "scratch", [P, 4, T])
            k.PT = [over(attention_scope, f"PT{i}", [P, 2, TT, T], F32R) for i in range(2)]
        with ExitStack() as scope:
            Hs = [over(scope, f"H{i}", [P, C, B, T], F32R) for i in range(2)]
            k.Wsplit = [over(scope, f"Ws{i}", [P, 2, 3072], F32R) for i in range(2)]
            k.hidH = over(scope, "hidH", [P, 2, 2, T], F32R)
            k.hidL = over(scope, "hidL", [P, 2, 2, T], F32R)
            k.WM = over(scope, "WM", [P, 2, 2048])
        Vflat = [v[:].rearrange("p j d -> p (j d)") for v in k.V]
        narrow = [v[:, 0:TT * P].rearrange("p (j d) -> p j d", j=TT) for v in Vflat]
        Vz = [v[:, TT * P:3 * TT * P].rearrange("p (s j d) -> p s j d", s=2, j=TT) for v in Vflat]
        W0, W1 = W[:, 0:8192], W[:, 5248:10240]
        k.HH = lambda b, c: Hs[0][:, c, b, :]
        k.HL = lambda b, c: Hs[1][:, c, b, :]
        k.staged = lambda n, w: k.WM[:, n % 2, 0:w]
        k.cost, k.sint = k.scratch[:, 0, :], k.scratch[:, 1, :]
        vbias = k.cosr[:]
        k.pos = k.bias[:, :, :].bitcast(I32)
        k.ropet = k.scratch[:, :, :]

        k.done = {n: sem(n + "_done") for n in NAMES}
        l_x, l_const, l_cond = sem("l_x"), sem("l_const"), sem("l_cond")
        l_w = [sem(f"l_w{i}") for i in range(4)]
        l_bias = [sem(f"l_bias{i}") for i in range(2)]
        k.l_pos = sem("l_pos")
        l_vb = sem("l_vb")
        l_m = [sem(f"l_m{i}") for i in range(2)]
        s_zero = sem("s_zero")
        s_out = sem("s_out")

        one = lambda b: bass.ds(b, 1)
        k.xs = lambda b, c: x[:, c, one(b), :].rearrange("p o t -> p (o t)")
        modc = lambda tile: (lambda b, c: mod[:, tile + c, one(b)])
        combc = lambda i: (lambda b, c: comb[:, i, c, one(b)])
        hN = lambda b, c: k.hN[:, c, :]
        R = lambda i, c: k.R[:, i, c, :]

        COLS = [("L1_cond_ln1_w", 4), ("L1_cond_ln2_w", 4), ("L2_cond_q_bias", 4), ("L2_cond_bproj", 4),
                ("L2_cond_bfc1", 16), ("L2_cond_bfc2", 4), ("L3_cond_b1", 16), ("L3_cond_b2", 4),
                ("L3_cond_ln_g", 4), ("L3_cond_ln_b", 4), ("L3_cond_out_b", 4)]
        col, o = {}, 0
        for name, n in COLS:
            col[name] = cols[:, o:o + n]
            o += n
        mods = {"L0": 0, "L1a": 8, "L1b": 12, "L2": 16, "L3": 40}
        MODB = [("L0_cond_b_ada", 0, 8), ("L2_cond_bada", 16, 24), ("L3_cond_emb_b", 40, 8)]

        def view(w, base, width, n=C):
            return w[:, base:base + n * width].rearrange("p (c m) -> p c m", c=n)

        wq0, wkd, wo0 = view(W0, 0, D), view(W0, 2048, P), view(W0, 2560, D)
        wku, wvu = W0[:, 4608:5120], W0[:, 5120:5248]
        wq1, wk1, wv1, wo1 = view(W1, 0, D), view(W1, 2048, P), view(W1, 2560, 64), view(W1, 2816, D)
        wqkv2, wo2 = view(W0, 0, 3 * D), view(W0, 6144, D)
        w1e, w2e = view(W, 0, P, ET), view(W, 2048, P, ET)
        wout3 = view(W, 4096, D)

        def rows(name):
            return a[name].rearrange("(c p) m -> p c m", p=P)

        def copies(dst, scale=lambda g: 1.0, bias=None):
            def put_act(e, b, g, bank):
                if bias is None:
                    return e.activation(dst(b, g), bank, ACT.Copy, scale=scale(g))
                return e.activation(dst(b, g), bank, ACT.Identity, bias=bias(g), scale=scale(g))

            def put_dve(e, b, g, bank):
                return e.tensor_scalar(dst(b, g), bank, scale(g), None if bias is None else bias(g), ALU.mult,
                                       ALU.bypass if bias is None else ALU.add)
            return put_act, put_dve

        def residual(bias=None, gamma=None):
            def put_dve(e, b, g, bank):
                if gamma is not None:
                    return e.scalar_tensor_tensor(out=k.xs(b, g), in0=bank, scalar=gamma(b, g),
                                                  in1=k.xs(b, g), op0=ALU.mult, op1=ALU.add)
                return e.scalar_tensor_tensor(out=k.xs(b, g), in0=bank, scalar=0.0 if bias is None else bias(g),
                                              in1=k.xs(b, g), op0=ALU.add, op1=ALU.add)
            return None, put_dve

        def dense(w, src):
            return lambda b, g: [(w[:, c, g * P:(g + 1) * P], src(c)) for c in range(C)]

        hsrc = lambda c: k.hN[:, c, :]
        asrc = lambda c: k.t1[:, c, :]

        class Ada(Step):
            n = {"pe": 12}

            def pe(s, k, e, b, at):
                e.wait_ge(l_cond, 16)
                for j in range(12):
                    if j == 4:
                        e.wait_ge(k.done["dve"], 2)
                    e.wait_ge(l_m[j % 2], 16 * (j // 2 + 1))
                    w = k.WM[:, j % 2, 0:C * D].rearrange("p (c m) -> p c m", c=C)
                    for t in range(4):
                        for c in range(C):
                            mm = e.matmul(k.bank(0)[:, 4 * (4 * j + t):4 * (4 * j + t) + 4],
                                          w[:, c, t * P:(t + 1) * P], cond[:, int(j >= 4), c, :],
                                          start=c == 0, stop=c == C - 1)
                    mm.then_inc(k.done["pe"], 1)

            def act(s, k, e, b, at):
                e.wait_ge(l_cond, 16)
                e.activation(cond[:, 1, :, :], cond[:, 0, :, :], ACT.Silu).then_inc(k.done["act"], 1)
                e.wait_ge(l_const, 16 * n_const)
                e.activation(k.smul[:], k.smul[:], ACT.Exp).then_inc(k.done["act"], 1)

            def dve(s, k, e, b, at):
                e.memset(eps5[:], 1e-5).then_inc(k.done["dve"], 1)
                e.wait_ge(k.done["act"], 1)
                e.memset(eps6[:], 1e-6).then_inc(k.done["dve"], 1)
        Ada.n = {"pe": 12, "act": 2, "dve": 2}

        class Mods(Step):
            n = {"dve": 14}

            def dve(s, k, e, b, at):
                done = [0]

                def inc(ins):
                    done[0] += 1
                    ins.then_inc(k.done["dve"], 1)
                    e.wait_ge(k.done["dve"], at["dve"] + done[0])

                def wide(ap):
                    return ap.unsqueeze(2).to_broadcast([P, C, B])

                start_wait(k, e, at, "pe", "dve", "act")
                e.wait_ge(l_const, 16 * n_const)
                inc(e.tensor_copy(k.identr[:], k.ident[:]))
                inc(e.tensor_copy(mod[:].rearrange("p t b -> p (t b)"), k.bank(0)[:, 0:ADA * B]))
                inc(e.tensor_tensor(mod[:], mod[:], modb[:].unsqueeze(2).to_broadcast([P, ADA, B]), ALU.add))
                for t0, n in ((0, 4), (8, 8), (24, 8), (40, 4)):
                    m = mod[:, t0:t0 + n, :]
                    inc(e.tensor_scalar(m, m, 1.0, None, ALU.add))
                inc(e.tensor_tensor(comb[:, 0], mod[:, 8:12, :], wide(col["L1_cond_ln1_w"]), ALU.mult))
                inc(e.tensor_tensor(comb[:, 1], mod[:, 12:16, :], wide(col["L1_cond_ln2_w"]), ALU.mult))
                inc(e.tensor_tensor(comb[:, 2], mod[:, 20:24, :], wide(col["L2_cond_bfc2"]), ALU.mult))
                inc(e.tensor_tensor(comb[:, 5], mod[:, 16:20, :], wide(col["L2_cond_bproj"]), ALU.mult))
                inc(e.tensor_tensor(comb[:, 3], mod[:, 40:44, :], wide(col["L3_cond_ln_g"]), ALU.mult))
                inc(e.tensor_tensor(comb[:, 4], mod[:, 40:44, :], wide(col["L3_cond_ln_b"]), ALU.mult))
                inc(e.tensor_tensor(comb[:, 4], comb[:, 4], mod[:, 44:48, :], ALU.add))
                assert done[0] == s.n["dve"], done

        split_q = [(R(0, c), k.Q[0][:, c], k.Q[1][:, c]) for c in range(C)]
        split_k = [(R(1, c), k.K[0][:, c], k.K[1][:, c]) for c in range(C)]

        def split_v(width):
            V = k.V if width > P else narrow
            return [(k.R[:, 0, j, 0:width], V[0][:, j, 0:width], V[1][:, j, 0:width]) for j in range(TT)]

        put_v = lambda width: copies(lambda b, g: k.R[:, 0, g, 0:width])

        all_tiles = lambda i: TT
        latent = k.t1[:, 0, :]
        inv_root = float(1 / np.sqrt(np.float32(32)))

        layer0 = [
            Norm(k.xs, modc(0), modc(4), eps5[:, 0:1]),
            Linear(1, lambda b, g: [(wkd[:, c, :], hsrc(c)) for c in range(C)],
                   *copies(lambda b, g: latent), load=(l_w[0], 80)),
            Linear(TT, lambda b, g: [(latent[:, g * P:(g + 1) * P], wvu)], *put_v(P), width=P),
            Split(split_v(P)),
            Linear(C, dense(wq0, hsrc), *copies(lambda b, g: R(0, g), lambda g: inv_root)),
            Linear(C, lambda b, g: [(wku[:, g * P:(g + 1) * P], latent)], *copies(lambda b, g: R(1, g))),
            Rope([R(0, c) for c in range(C)], perm[:, 0, :], k.cosr[:], k.sinr[:]),
            Rope([R(1, c) for c in range(C)], perm[:, 0, :], k.cosr[:], k.sinr[:]),
            Split(split_q + split_k),
            Attention(16, lambda h: h // 4, lambda h: h // 4, l_bias[0], lambda i: i + 1, narrow, Vz),
            Linear(C, dense(wo0, asrc), *residual(), only="dve"),
        ]

        layer1a = [
            Norm(k.xs, combc(0), None, eps6[:, 0:1], rms=True),
            Angles(), Sign(),
            Linear(TT, lambda b, g: [(k.hN[:, c, g * P:(g + 1) * P], wv1[:, c, :]) for c in range(C)],
                   *put_v(64), width=64, load=(l_w[1], 64)),
            Split(split_v(64)),
            Linear(C, dense(wq1, hsrc), *copies(lambda b, g: R(0, g), lambda g: 0.125)),
            Linear(1, lambda b, g: [(wk1[:, c, :], hsrc(c)) for c in range(C)],
                   *copies(lambda b, g: R(1, 0))),
            Rope([R(0, c) for c in range(C)], perm[:, 1, :], k.cosr[:], k.sinr[:]),
            Rope([R(1, 0)], perm[:, 1, :], k.cosr[:], k.sinr[:]),
            Split(split_q + split_k[:1]),
            Attention(8, lambda h: 0, lambda h: 0, None, all_tiles, narrow, Vz),
            Linear(C, dense(wo1, asrc), *residual(), only="dve"),
        ]
        norm1b = [Norm(k.xs, combc(1), None, eps6[:, 0:1], rms=True, pair=(k.HH, k.HL))]

        class ValueBias(Step):
            n = {"pool": TT}

            def pool(s, k, e, b, at):
                start_wait(k, e, at, "act", "dve", "pe", "pool")
                e.wait_ge(l_vb, 16)
                for j in range(TT):
                    e.tensor_tensor(k.R[:, 0, j, :], k.R[:, 0, j, :], vbias, ALU.add).then_inc(k.done["pool"], 1)

        class ProjBias(Step):
            n = {"act": C}

            def act(s, k, e, b, at):
                start_wait(k, e, at, "act", "dve", "pe", "pool")
                for c in range(C):
                    e.activation(k.xs(b, c), k.xs(b, c), ACT.Identity, bias=combc(5)(b, c), scale=1.0)\
                        .then_inc(k.done["act"], 1)

        layer2a = [
            Norm(k.xs, modc(24), modc(32), eps6[:, 0:1]),
            Linear(TT, lambda b, g: [(k.hN[:, c, g * P:(g + 1) * P], wqkv2[:, c, 2 * D:3 * D])
                                     for c in range(C)], *put_v(D), load=(l_w[2], 32)),
            ValueBias(),
            Split(split_v(D)),
            Linear(C, dense(wqkv2, hsrc), *copies(lambda b, g: R(0, g),
                                                  bias=lambda g: col["L2_cond_q_bias"][:, g:g + 1])),
            Linear(C, lambda b, g: dense(wqkv2, hsrc)(b, g + C), *copies(lambda b, g: R(1, g))),
            QKNorm(),
            Split(split_q + split_k),
            Attention(16, lambda h: h // 4, lambda h: h, l_bias[1], all_tiles, k.V, Vz2),
            Linear(C, dense(wo2, asrc), *residual(gamma=modc(16)), only="dve"),
            ProjBias(),
        ]
        norm2b = [Norm(k.xs, modc(28), modc(36), eps6[:, 0:1], pair=(k.HH, k.HL), extra=combc(2))]

        gelu_bias = col["L3_cond_b1"]

        def gelu_put(e, b, g, bank):
            return e.activation(hide[:, g, :], bank, ACT.Gelu, bias=gelu_bias[:, g:g + 1], scale=1.0)

        layer3 = [
            Linear(ET, lambda b, g: [(w1e[:, g, :], k.xs(b, g // 4))], gelu_put, None, only="act",
                   load=(l_w[3], 16 * 17)),
            Linear(C, lambda b, g: [(w2e[:, 4 * g + i, :], hide[:, 4 * g + i, :]) for i in range(4)],
                   *copies(hN, bias=lambda g: col["L3_cond_b2"][:, g:g + 1])),
            Norm(hN, combc(3), combc(4), eps5[:, 0:1], func=ACT.Silu),
            Linear(C, dense(wout3, hsrc), *residual(lambda g: col["L3_cond_out_b"][:, g:g + 1]), only="dve"),
        ]

        l_m_at, seen = {1: [], 2: []}, [16 * 6, 16 * 6]
        for layer, loads in ((1, [2, 1] * NCH), (2, [2] * NCH)):
            for n, m in enumerate(loads):
                seen[n % 2] += 16 * m
                l_m_at[layer].append(seen[n % 2])

        def up(layer_ups):
            return lambda v, slot, c, w, t: k.Wsplit[v][:, slot, (c * layer_ups + w) * HC + t * P:
                                                        (c * layer_ups + w) * HC + (t + 1) * P]

        def down(base):
            return lambda v, slot, t, m: k.Wsplit[v][:, slot, base + t * D + m * P:base + t * D + (m + 1) * P]

        phases = [([Ada(), Mods()], False), (layer0, True), (layer1a, True), (norm1b, True)]
        mlp1 = Mlp(True, [(0, 2 * C * HC), (2 * C * HC, 2 * D)], loaded=lambda n: (l_m[n % 2], l_m_at[1][n]))
        mlp2 = Mlp(False, [(0, 2 * C * HC)], loaded=lambda n: (l_m[n % 2], l_m_at[2][n]),
                   hbias=col["L2_cond_bfc1"], gamma=modc(20))
        mlp1.up, mlp1.down = up(2), down(2 * C * HC)
        mlp2.up, mlp2.down = up(1), down(C * HC)
        phases.append(([mlp1], False))
        phases += [(layer2a, True), (norm2b, True)]
        phases.append(([mlp2], False))
        phases.append((layer3, True))

        starts, total = [], dict.fromkeys(NAMES, 0)
        for stages, looped in phases:
            starts.append(dict(total))
            for n in NAMES:
                total[n] += (B if looped else 1) * sum(st.n.get(n, 0) for st in stages)
        starts.append(dict(total))
        L1P, M1P, L2P, M2P, L3P = 2, 4, 5, 7, 8

        PICK = {"pe": lambda st: st.pe, "act": lambda st: st.act, "dve": lambda st: st.dve,
                "pool": lambda st: st.pool}

        n_const = 12 + len(COLS) + len(MODB) + 1

        def wait_all(e, p):
            for name in NAMES:
                if starts[p][name]:
                    e.wait_ge(k.done[name], starts[p][name])

        def engine(e, name, first, last):
            for (stages, looped), start in list(zip(phases, starts))[first:last]:
                if not any(st.n.get(name, 0) or st.n == {} for st in stages):
                    continue
                per = {n: sum(st.n.get(n, 0) for st in stages) for n in NAMES}

                def body(b):
                    at = {n: start[n] + (b * per[n] if looped else 0) for n in NAMES}
                    for st in stages:
                        PICK[name](st)(k, e, b, at)
                        at = {n: at[n] + st.n.get(n, 0) for n in NAMES}
                if looped:
                    for b in range(B):
                        body(b)
                else:
                    body(0)

        def run_pool(e, first, last):
            engine(e, "pool", first, last)

        block = ctx.enter_context(nc.Block())

        @block.sync
        def _(e):
            e.dma_start(cond[:, 0, :, :], a["condT"].rearrange("(c p) b -> p c b", p=P)).then_inc(l_cond, 16)
            blocks = [("L0_cond_W_ada", 2), ("L1_cond_ln1_tw", 1), ("L1_cond_ln2_tw", 1), ("L2_cond_Wada", 6),
                      ("L3_cond_emb_W", 2)]
            n = 0
            for name, count in blocks:
                for j in range(count):
                    if n >= 2:
                        e.wait_ge(k.done["pe"], n - 1)
                    e.dma_start(k.WM[:, n % 2, 0:C * D].rearrange("p (c m) -> p c m", c=C),
                                rows(name)[:, :, j * D:(j + 1) * D]).then_inc(l_m[n % 2], 16)
                    n += 1
                    if n == 1:
                        for c in range(C):
                            e.dma_start(x[:, c, :, :], a["x"][c * P:(c + 1) * P]).then_inc(l_x, 16)

            def wait_phase(p):
                for name in NAMES:
                    if starts[p][name]:
                        e.wait_ge(k.done[name], starts[p][name])

            def slot_free(stage, phase, n):
                name, i = stage.i[("low", n - 2)]
                e.wait_ge(k.done[name], starts[phase][name] + i)

            for j in range(NCH):
                if j == 0:
                    wait_phase(L1P + 1)
                else:
                    slot_free(mlp1, M1P, 2 * j)
                wup = k.WM[:, 0, :].rearrange("p (c w m) -> p c w m", c=C, w=2)
                for w, name in enumerate(("L1_cond_Wg", "L1_cond_Wu")):
                    e.dma_start(wup[:, :, w, :], rows(name)[:, :, j * HC:(j + 1) * HC]).then_inc(l_m[0], 16)
                if j:
                    slot_free(mlp1, M1P, 2 * j + 1)
                e.dma_start(k.WM[:, 1, 0:2 * D].rearrange("p (t m) -> p t m", t=2),
                            rows("L1_cond_Wd")[:, 2 * j:2 * j + 2, :]).then_inc(l_m[1], 16)
            for j in range(NCH):
                if j < 2:
                    wait_phase(M2P - 1)
                else:
                    slot_free(mlp2, M2P, j)
                e.dma_start(k.WM[:, j % 2, 0:C * HC].rearrange("p (c m) -> p c m", c=C),
                            rows("L2_cond_Wfc1")[:, :, j * HC:(j + 1) * HC]).then_inc(l_m[j % 2], 16)
                e.dma_start(k.WM[:, j % 2, C * HC:C * HC + 2 * D].rearrange("p (t m) -> p t m", t=2),
                            rows("L2_cond_Wfc2")[:, 2 * j:2 * j + 2, :]).then_inc(l_m[j % 2], 16)
            wait_phase(L3P)
            with e.Fori(0, B) as b:
                per = {n: sum(st.n.get(n, 0) for st in layer3) for n in NAMES}
                e.wait_ge(k.done["dve"], starts[L3P]["dve"] + (b + 1) * per["dve"])
                e.dma_start(out[:, :, one(b), :], x[:, :, one(b), :]).then_inc(s_out, 16)
            e.wait_ge(s_out, 16 * B)

        @block.gpsimd
        def _(e):
            e.dma_start(k.ident[:], a["ident"]).then_inc(l_const, 16)
            e.dma_start(k.ones[:], a["ones"]).then_inc(l_const, 16)
            e.dma_start(k.blockones[:], a["blockones"]).then_inc(l_const, 16)
            e.dma_start(perm[:], a["perm"].rearrange("w p m -> p w m")).then_inc(l_const, 16)
            e.dma_start(k.cosr[:], a["cos0"]).then_inc(l_const, 16)
            e.dma_start(k.sinr[:], a["sin0"]).then_inc(l_const, 16)
            e.dma_start(k.freq[:], a["freq"]).then_inc(l_const, 16)
            e.dma_start(k.sign[:], a["sign"]).then_inc(l_const, 16)
            e.dma_start(k.heads[2], a["heads2"]).then_inc(l_const, 16)
            e.dma_start(k.heads[4], a["heads4"]).then_inc(l_const, 16)
            for n in (2, 4):
                e.dma_start(k.places[n], a[f"places{n}"]).then_inc(l_const, 16)
            for name, _ in COLS:
                e.dma_start(col[name], a[name]).then_inc(l_const, 16)
            e.dma_start(k.smul[:], a["L2_cond_scale_mul_log"]).then_inc(l_const, 16)
            e.memset(modb[:], 0.0).then_inc(s_zero, 1)
            e.wait_ge(s_zero, 1)
            for name, t0, n in MODB:
                e.dma_start(modb[:, t0:t0 + n], a[name]).then_inc(l_const, 16)
            e.dma_start(k.bias[:], a["mask0"].rearrange("(i p) t -> p i t", p=P)).then_inc(l_bias[0], 16)
            for dst, name in ((wq0, "L0_cond_Wq"), (wkd, "L0_cond_Wkd"), (wo0, "L0_cond_Wo")):
                e.dma_start(dst, rows(name)).then_inc(l_w[0], 16)
            e.dma_start(wku, a["L0_cond_Wku"]).then_inc(l_w[0], 16)
            e.dma_start(wvu, a["L0_cond_Wvu"]).then_inc(l_w[0], 16)
            for dst, name in ((wq1, "L1_cond_Wq"), (wk1, "L1_cond_Wk"), (wv1, "L1_cond_Wv"), (wo1, "L1_cond_Wo")):
                e.dma_start(dst, rows(name)).then_inc(l_w[1], 16)
            run_pool(e, 0, L1P)
            wait_all(e, L1P)
            e.dma_start(k.pos, a["pos"].rearrange("b t -> (b t)").partition_broadcast(P)
                        .rearrange("p (b t) -> p b t", b=B)).then_inc(k.l_pos, 16)
            run_pool(e, L1P, L2P)
            wait_all(e, L2P)
            e.dma_start(wqkv2, rows("L2_cond_Wqkv")).then_inc(l_w[2], 16)
            e.dma_start(wo2, rows("L2_cond_Wproj")).then_inc(l_w[2], 16)
            e.dma_start(k.bias[:], a["mask"].rearrange("(i p) t -> p i t", p=P)).then_inc(l_bias[1], 16)
            e.dma_start(vbias, a["L2_cond_v_bias"].rearrange("o d -> (o d)").partition_broadcast(P))\
                .then_inc(l_vb, 16)
            run_pool(e, L2P, L3P)
            wait_all(e, L3P)
            e.memset(W[:, 0:4096], 0.0).then_inc(s_zero, 1)
            e.wait_ge(s_zero, 2)
            for half in range(2):
                src1 = a["L3_cond_W1"].rearrange("(q h) l (t f) -> h l q t f", h=2, t=2)[half]
                dst1 = w1e[64 * half:64 * half + 64].rearrange("l (q h t) f -> l q h t f", h=2, t=2)[:, :, half]
                src2 = a["L3_cond_W2"].rearrange("(q h) (t p) l -> h p q t l", h=2, t=2)[half]
                dst2 = w2e.rearrange("p (q h t) l -> p q h t l", h=2, t=2)[:, :, half, :,
                                                                          64 * half:64 * half + 64]
                for q in range(4):
                    e.dma_start(dst1[:, q], src1[:, q]).then_inc(l_w[3], 16)
                    e.dma_start(dst2[:, q], src2[:, q]).then_inc(l_w[3], 16)
            e.dma_start(wout3, rows("L3_cond_out_W")).then_inc(l_w[3], 16)
            run_pool(e, L3P, len(phases))

        @block.tensor
        def _(e):
            engine(e, "pe", 0, 1)
            e.wait_ge(l_x, 16 * C)
            e.wait_ge(l_const, 16 * n_const)
            engine(e, "pe", 1, len(phases))

        @block.vector
        def _(e):
            engine(e, "dve", 0, 1)
            e.wait_ge(l_x, 16 * C)
            engine(e, "dve", 1, len(phases))

        @block.scalar
        def _(e):
            engine(e, "act", 0, 1)
            e.wait_ge(l_x, 16 * C)
            engine(e, "act", 1, len(phases))


def _layout(inputs):
    g = {n: np.asarray(v) for n, v in inputs.items()}
    T_ = lambda w: np.ascontiguousarray(w.T)
    column = lambda v: np.ascontiguousarray(v.reshape(-1, P).T)
    o = {"x": np.ascontiguousarray(g["x"].transpose(2, 0, 1)), "condT": T_(g["cond_2048"]),
         "pos": g["pos_BxS"], "mask": np.ascontiguousarray(g["mask_1x1xSxS_ff0"][0, 0])}
    for n in ("L0_cond_W_ada", "L0_cond_Wq", "L0_cond_Wkd", "L0_cond_Wvu", "L0_cond_Wo", "L1_cond_ln1_tw",
              "L1_cond_ln2_tw", "L1_cond_Wq", "L1_cond_Wv", "L1_cond_Wo", "L1_cond_Wg", "L1_cond_Wu",
              "L1_cond_Wd", "L2_cond_Wqkv", "L2_cond_Wproj", "L2_cond_Wada", "L2_cond_Wfc1", "L2_cond_Wfc2"):
        o[n] = T_(g[n])
    o["L0_cond_Wku"] = T_(np.repeat(g["L0_cond_Wku"].reshape(4, 1, 32, P), 4, axis=1).reshape(D, P))
    o["L1_cond_Wk"] = T_(np.concatenate([g["L1_cond_Wk"]] * 2))
    for n in ("L3_cond_emb_W", "L3_cond_W1", "L3_cond_W2", "L3_cond_out_W"):
        o[n] = g[n]
    for n in ("L1_cond_ln1_w", "L1_cond_ln2_w", "L2_cond_q_bias", "L2_cond_bproj", "L2_cond_bfc1",
              "L2_cond_bfc2", "L3_cond_b1", "L3_cond_b2", "L3_cond_ln_g", "L3_cond_ln_b", "L3_cond_out_b",
              "L0_cond_b_ada", "L2_cond_bada", "L3_cond_emb_b"):
        o[n] = column(g[n])
    o["L2_cond_v_bias"] = g["L2_cond_v_bias"].reshape(1, D)
    o["L2_cond_scale_mul_log"] = column(np.repeat(g["L2_cond_scale_mul_log"].reshape(16), 32))
    return {n: np.ascontiguousarray(v) for n, v in o.items()}


def _constants():
    f = np.float32
    eye = np.eye(P, dtype=f)
    o = {"ident": eye, "ones": np.full((P, P), 1 / D, f),
         "blockones": np.kron(np.eye(4, dtype=f), np.ones((32, 32), f))}
    o["perm"] = np.stack([np.kron(np.eye(P // d), np.roll(np.eye(d), d // 2, axis=0)).astype(f)
                          for d in (32, 64)])
    row = np.arange(P)
    f32 = (1.0 / f(10000.0) ** (np.arange(0, 32, 2, dtype=f) / f(32))).astype(f)
    ang = (np.arange(T, dtype=f)[None, :] * f32[row % 16][:, None]).astype(f)
    sgn = np.where(row % 32 < 16, -1, 1).astype(f)[:, None]
    o["cos0"], o["sin0"] = np.cos(ang), np.sin(ang) * sgn
    f64 = (1.0 / f(10000.0) ** (np.arange(0, 64, 2, dtype=f) / f(64))).astype(f)
    o["freq"] = f64[row % 32][:, None]
    o["sign"] = np.where(row % 64 < 32, -1, 1).astype(f)[:, None]
    o["heads2"], o["heads4"] = np.kron(np.eye(2), np.ones((64, 1))), np.kron(np.eye(4), np.ones((32, 1)))
    for n in (2, 4):
        o[f"places{n}"] = np.broadcast_to(np.eye(n), (P, n, n))
    i = np.arange(T)
    hidden = (np.abs(i[None] - i[:, None]) > 64) & ~(i % 64 == 0)[None] | (i[None] // P > i[:, None] // P)
    o["mask0"] = np.where(hidden, f(-1e30), f(0))
    return {n: np.ascontiguousarray(v, dtype=f) for n, v in o.items()}


def kernel(**inputs):
    import concourse.bacc as _bacc
    from concourse.bass_utils import run_bass_kernel_spmd as _run

    nc = _bacc.Bacc("TRN2", target_bir_lowering=False, num_devices=1)
    arrays, aps = {}, {}
    for name, v in {**_layout(inputs), **_constants()}.items():
        arrays["in_" + name] = v
        aps[name] = nc.dram_tensor("in_" + name, v.shape, mybir.dt.from_np(v.dtype), kind="ExternalInput").ap()
    out = nc.dram_tensor("out_x", (P, C, B, T), F32, kind="ExternalOutput").ap()
    conditioned_stack(nc, aps, out)
    r = _run(nc, [arrays], core_ids=[0])
    return np.ascontiguousarray(r.results[0]["out_x"].transpose(2, 3, 1, 0)).reshape(B, T, D)
```

```python
from contextlib import ExitStack

import numpy as np
import concourse.bass as bass
from concourse import mybir

F32 = mybir.dt.float32
F32R = mybir.dt.float32r
I32 = mybir.dt.int32
ALU = mybir.AluOpType
ACT = mybir.ActivationFunctionType
AX_X = mybir.AxisListType.X

P = 128
B, T, D = 4, 512, 512
C = D // P
TT = T // P
HID = 2048
HC = 256
NCH = HID // HC
EXP, LAT, FFN = 8, 64, 256
ET = EXP * FFN // P
NAMES = ("pe", "act", "dve", "pool")


class Step:

    n = {}

    def pe(self, k, e, b, at): pass
    def act(self, k, e, b, at): pass
    def dve(self, k, e, b, at): pass
    def pool(self, k, e, b, at): pass


def start_wait(k, e, at, *names, but={}):
    for name in names:
        n = at[name] - but.get(name, 0)
        if n > 0:
            e.wait_ge(k.done[name], n)


class Norm(Step):

    def __init__(s, src, A, Bias, eps, rms=False, func=None, pair=None, extra=None, early=True):
        s.early = early
        s.src, s.A, s.Bias, s.eps, s.rms, s.pair, s.extra = src, A, Bias, eps, rms, pair, extra
        s.func = func or ACT.Identity
        s.m = 0 if rms else 1
        s.n = {"pe": 1 + s.m, "dve": s.m * C + 1 + C + (C if pair else 0),
               "act": C + 1 + s.m * C + (C if pair else 0) + (C if extra else 0)}

    def late(s, b, name):
        if s.pair and b > 0:
            ends = C + (C if s.extra else 0)
            return {"pe": {"act": ends, "dve": C}, "act": {"dve": C}, "dve": {"act": ends - C}}[name]
        if s.early and name != "dve":
            return {"dve": C - 1}
        return {}

    def centred(s, k, b, c):
        return s.src(b, c) if s.rms else k.hN[:, c, :]

    def pe(s, k, e, b, at):
        start_wait(k, e, at, "act", "dve", "pool", but=s.late(b, "pe"))
        if not s.rms:
            for c in range(C):
                mm = e.matmul(k.bank(0), k.ones[:], s.src(b, c), start=c == 0, stop=c == C - 1)
            mm.then_inc(k.done["pe"], 1)
        if not (s.pair and b > 0):
            start_wait(k, e, at, "dve")
        for c in range(C):
            e.wait_ge(k.done["act"], at["act"] + c + 1)
            mm = e.matmul(k.bank(1), k.ones[:], k.t1[:, c, :], start=c == 0, stop=c == C - 1)
        mm.then_inc(k.done["pe"], 1)

    def dve(s, k, e, b, at):
        start_wait(k, e, at, "act", "dve", "pe", "pool", but=s.late(b, "dve"))
        n = s.m * C
        if not s.rms:
            e.wait_ge(k.done["pe"], at["pe"] + 1)
            for c in range(C):
                e.tensor_tensor(k.hN[:, c, :], s.src(b, c), k.bank(0), ALU.subtract)\
                    .then_inc(k.done["dve"], 1)
        e.wait_ge(k.done["act"], at["act"] + C + 1)
        e.reciprocal(k.rstd, k.sd).then_inc(k.done["dve"], 1)
        e.wait_ge(k.done["dve"], at["dve"] + n + 1)
        for c in range(C):
            e.scalar_tensor_tensor(out=k.hN[:, c, :], in0=s.centred(k, b, c), scalar=s.A(b, c),
                                   in1=k.rstd, op0=ALU.mult, op1=ALU.mult)\
                .then_inc(k.done["dve"], 1)
        if s.pair:
            for c in range(C):
                e.wait_ge(k.done["act"], at["act"] + C + 1 + s.m * C + c + 1)
                high = s.pair[0](b, c).bitcast(F32)
                e.tensor_tensor(s.pair[1](b, c), k.hN[:, c, :], high, ALU.subtract)\
                    .then_inc(k.done["dve"], 1)

    def act(s, k, e, b, at):
        start_wait(k, e, at, "act", "dve", "pe", "pool", but=s.late(b, "act"))
        for c in range(C):
            if not s.rms:
                e.wait_ge(k.done["dve"], at["dve"] + c + 1)
            e.activation(k.t1[:, c, :], s.centred(k, b, c), ACT.Square).then_inc(k.done["act"], 1)
        e.wait_ge(k.done["pe"], at["pe"] + s.n["pe"])
        e.activation(k.sd, k.bank(1), ACT.Sqrt, bias=s.eps, scale=1.0)\
            .then_inc(k.done["act"], 1)
        if not s.rms:
            for c in range(C):
                e.wait_ge(k.done["dve"], at["dve"] + C + 1 + c + 1)
                e.activation(k.hN[:, c, :], k.hN[:, c, :], s.func, bias=s.Bias(b, c), scale=1.0)\
                    .then_inc(k.done["act"], 1)
        if s.pair:
            for c in range(C):
                if s.rms:
                    e.wait_ge(k.done["dve"], at["dve"] + 1 + c + 1)
                else:
                    e.wait_ge(k.done["act"], at["act"] + C + 1 + c + 1)
                e.activation(s.pair[0](b, c), k.hN[:, c, :], ACT.Copy).then_inc(k.done["act"], 1)
        if s.extra is not None:
            e.wait_ge(k.done["dve"], at["dve"] + s.m * C + 1 + C)
            for c in range(C):
                e.activation(s.src(b, c), s.src(b, c), ACT.Identity, bias=s.extra(b, c), scale=1.0)\
                    .then_inc(k.done["act"], 1)


class Linear(Step):

    def __init__(s, groups, mats, put_act, put_dve, width=T, only=None, load=None, ready=None):
        s.groups, s.mats, s.put_act, s.put_dve = groups, mats, put_act, put_dve
        s.widths = width if isinstance(width, list) else [width] * groups
        s.only = only if isinstance(only, list) else [only] * groups
        s.load, s.ready = load, ready
        to_act = [s.by(g) == "act" for g in range(groups)]
        s.n = {"pe": groups, "act": sum(to_act), "dve": groups - sum(to_act)}

    def by(s, g):
        return s.only[g] or ("act" if g % 2 == 0 else "dve")

    def count(s, g):
        return sum(s.by(i) == s.by(g) for i in range(g + 1))

    def pe(s, k, e, b, at):
        if s.ready:
            start_wait(k, e, at, "act", "dve", "pool", but={s.ready[0]: s.ready[1] + C - 1})
        else:
            start_wait(k, e, at, "act", "dve", "pool")
        if s.load is not None:
            e.wait_ge(*s.load)
        for g in range(s.groups):
            if g >= 4:
                f = g - 4
                e.wait_ge(k.done[s.by(f)], at[s.by(f)] + s.count(f))
            mats = s.mats(b, g)
            for i, (lhsT, rhs) in enumerate(mats):
                if s.ready and g == 0:
                    e.wait_ge(k.done[s.ready[0]], at[s.ready[0]] - s.ready[1] - (C - 1 - i))
                mm = e.matmul(k.bank(g % 4)[:, 0:s.widths[g]], lhsT, rhs,
                              start=i == 0, stop=i == len(mats) - 1)
            mm.then_inc(k.done["pe"], 1)

    def act(s, k, e, b, at):
        if s.n["act"]:
            start_wait(k, e, at, "act", "dve", "pe", "pool")
        for g in range(s.groups):
            if s.by(g) == "act":
                e.wait_ge(k.done["pe"], at["pe"] + g + 1)
                s.put_act(e, b, g, k.bank(g % 4)[:, 0:s.widths[g]]).then_inc(k.done["act"], 1)

    def dve(s, k, e, b, at):
        if s.n["dve"]:
            start_wait(k, e, at, "act", "dve", "pe", "pool")
        for g in range(s.groups):
            if s.by(g) == "dve":
                e.wait_ge(k.done["pe"], at["pe"] + g + 1)
                s.put_dve(e, b, g, k.bank(g % 4)[:, 0:s.widths[g]]).then_inc(k.done["dve"], 1)


def joined(*parts, only=None, load=None, ready=None):
    where = [(p, g) for p in parts for g in range(p.groups)]

    def pick(name):
        def at_group(*args):
            *first, g = args[:2] if name == "mats" else args[:3]
            p, own = where[g]
            call = {"mats": p.mats, "act": p.put_act, "dve": p.put_dve}[name]
            return call(*first, own, *args[len(first) + 1:])
        return at_group
    return Linear(len(where), pick("mats"), pick("act"), pick("dve"), [p.widths[g] for p, g in where],
                  only=only, load=load, ready=ready)


class Angles(Step):

    def __init__(s, beside):
        s.beside = beside

    n = {"dve": 14, "act": 2}
    C1 = 6.28125
    C2 = float(np.float32(2 * np.pi - 6.28125))
    C3 = float(2 * np.pi - 6.28125 - float(np.float32(2 * np.pi - 6.28125)))
    MAGIC = 12582912.0
    TOP = 3.1415925

    def dve(s, k, e, b, at):
        start_wait(k, e, {n: at[n] - s.beside.n.get(n, 0) for n in at}, "act", "dve", "pe", "pool")
        done = [0]

        def inc(ins):
            done[0] += 1
            ins.then_inc(k.done["dve"], 1)
            e.wait_ge(k.done["dve"], at["dve"] + done[0])

        e.wait_ge(k.l_pos, 16)
        ang, kk, r = k.Pb[:, 0, :], k.Pb[:, 1, :], k.scratch[:, 2, :]
        inc(e.tensor_copy(kk, k.pos[:, bass.ds(b, 1), :].rearrange("p o t -> p (o t)")))
        inc(e.tensor_scalar(ang, kk, k.freq[:, 0:1], None, ALU.mult))
        for src, parts, out in ((ang, (s.C1, s.C2, s.C3), k.sint), (r, (s.C1, s.C2), k.cost)):
            inc(e.tensor_scalar(kk, src, 1 / (2 * np.pi), s.MAGIC, ALU.mult, ALU.add))
            inc(e.tensor_scalar(kk, kk, s.MAGIC, None, ALU.subtract))
            for part in parts:
                inc(e.scalar_tensor_tensor(out=r, in0=kk, scalar=-part, in1=src, op0=ALU.mult, op1=ALU.add))
                src = r
            inc(e.tensor_scalar(out, r, s.TOP, -s.TOP, ALU.min, ALU.max))
            if out is k.sint:
                inc(e.tensor_scalar(r, r, float(np.pi / 2), None, ALU.add))
        assert done[0] == s.n["dve"], done

    def act(s, k, e, b, at):
        start_wait(k, e, at, "act", "dve", "pe", "pool")
        e.wait_ge(k.done["dve"], at["dve"] + s.n["dve"])
        e.activation(k.sinr[:], k.sint, ACT.Sin).then_inc(k.done["act"], 1)
        e.activation(k.cosr[:], k.cost, ACT.Sin).then_inc(k.done["act"], 1)


class Ordered(Step):

    def number(s, orders):
        s.orders = orders
        s.i = {op: (name, n + 1) for name, order in orders.items() for n, op in enumerate(order)}
        s.n = {name: len(order) for name, order in orders.items()}

    def wait(s, k, e, at, kind, index):
        name, n = s.i[(kind, index)]
        e.wait_ge(k.done[name], at[name] + n)


class SplitTiles(Ordered):

    def high(s, k, e, at, name):
        src, high, _ = s.parts[name]
        return e.activation(high, src, ACT.Copy)

    def low(s, k, e, at, name):
        src, high, low = s.parts[name]
        s.wait(k, e, at, "high", name)
        return e.tensor_tensor(low, src, high.bitcast(F32), ALU.subtract)


class Rope(SplitTiles):

    def __init__(s, tiles, values, perm, cos, sin):
        s.perm, s.cos, s.sin = perm, cos, sin
        s.parts = {g: tile for g, tile in enumerate(tiles)}
        s.parts.update({("v", j): tile for j, tile in enumerate(values)})
        n = s.count = len(tiles)
        act, dve = [("high", ("v", j)) for j in range(len(values))], []
        for g in range(n + 2):
            if g < n:
                dve.append(("mult", g))
            if g < len(values):
                dve.append(("low", ("v", g)))
            if 1 <= g <= n:
                dve.append(("add", g - 1))
                act.append(("high", g - 1))
            if g >= 2:
                dve.append(("low", g - 2))
        s.number({"pe": [("perm", g) for g in range(n)], "pool": [("cos", g) for g in range(n)],
                  "act": act, "dve": dve})

    def pe(s, k, e, b, at):
        start_wait(k, e, at, "act", "dve", "pool")
        for g in range(s.count):
            if g >= 4:
                s.wait(k, e, at, "mult", g - 4)
            e.matmul(k.bank(g % 4), s.perm, s.parts[g][0], start=True, stop=True).then_inc(k.done["pe"], 1)

    def pool(s, k, e, b, at):
        start_wait(k, e, at, "act", "dve", "pe", "pool")
        for g in range(s.count):
            z = s.parts[g][0]
            s.wait(k, e, at, "perm", g)
            e.tensor_tensor(z, z, s.cos, ALU.mult).then_inc(k.done["pool"], 1)

    def act(s, k, e, b, at):
        start_wait(k, e, at, "act", "dve", "pe", "pool")
        for _, name in s.orders["act"]:
            if name in range(s.count):
                s.wait(k, e, at, "add", name)
            s.high(k, e, at, name).then_inc(k.done["act"], 1)

    def dve(s, k, e, b, at):
        start_wait(k, e, at, "act", "dve", "pe", "pool")
        for kind, g in s.orders["dve"]:
            if kind == "mult":
                s.wait(k, e, at, "perm", g)
                if g >= 4:
                    s.wait(k, e, at, "add", g - 4)
                ins = e.tensor_tensor(k.ropet[:, g % 4, :], k.bank(g % 4), s.sin, ALU.mult)
            elif kind == "add":
                s.wait(k, e, at, "mult", g)
                s.wait(k, e, at, "cos", g)
                z = s.parts[g][0]
                ins = e.tensor_tensor(z, z, k.ropet[:, g % 4, :], ALU.add)
            else:
                ins = s.low(k, e, at, g)
            ins.then_inc(k.done["dve"], 1)


class QKNorm(SplitTiles):

    def __init__(s, tiles, values):
        s.parts = {divmod(g, C): tile for g, tile in enumerate(tiles)}
        s.parts.update({("v", j): tile for j, tile in enumerate(values)})
        pe, act, dve = [], [], [("low", ("v", j)) for j in range(TT)]
        for w in range(2):
            act += [("square", (w, c)) for c in range(C)]
            if w == 0:
                act += [("high", ("v", j)) for j in range(TT)]
            act.append(("root", w))
            pe += [("sum", w)]
            dve += [("guard", w), ("inverse", w)]
        for w in range(2):
            pe += [("spread", (w, c)) for c in range(C)]
            act += [("high", (w, c)) for c in range(C)]
            for c in range(C):
                dve.append(("scale", (w, c)))
                if c or w:
                    dve.append(("low", (w, c - 1) if c else (0, C - 1)))
        dve.append(("low", (1, C - 1)))
        s.scaled = [(w, c) for w in range(2) for c in range(C)]
        s.number({"pe": pe, "act": act, "dve": dve})

    def pe(s, k, e, b, at):
        start_wait(k, e, at, "act", "dve", "pool")
        for kind, index in s.orders["pe"]:
            if kind == "sum":
                for c in range(C):
                    s.wait(k, e, at, "square", (index, c))
                    mm = e.matmul(k.bank(index), k.strip[:, 4 * (C - 1 - c):4 * (C - 1 - c) + P],
                                  (k.scratch, k.hN)[index][:, c, :], start=c == 0, stop=c == C - 1)
            else:
                w, c = index
                s.wait(k, e, at, "inverse", w)
                if w:
                    s.wait(k, e, at, "scale", (0, c))
                mm = e.matmul(k.bank(2 + c), k.sinr[:, c * P:(c + 1) * P], k.Pb[:, w, :], start=True, stop=True)
            mm.then_inc(k.done["pe"], 1)

    def act(s, k, e, b, at):
        start_wait(k, e, at, "act", "dve", "pe", "pool")
        for kind, index in s.orders["act"]:
            if kind == "square":
                w, c = index
                ins = e.activation((k.scratch, k.hN)[w][:, c, :], k.R[:, w, c, :], ACT.Square)
            elif kind == "high":
                if index in s.scaled:
                    s.wait(k, e, at, "scale", index)
                ins = s.high(k, e, at, index)
            else:
                s.wait(k, e, at, "sum", index)
                ins = e.activation(k.Pb[:, index, :], k.bank(index), ACT.Sqrt)
            ins.then_inc(k.done["act"], 1)

    def dve(s, k, e, b, at):
        start_wait(k, e, at, "act", "dve", "pe", "pool")
        for kind, index in s.orders["dve"]:
            if kind == "guard":
                s.wait(k, e, at, "root", index)
                ins = e.tensor_scalar(k.Pb[:, index, :], k.Pb[:, index, :], 1e-12, None, ALU.max)
            elif kind == "inverse":
                s.wait(k, e, at, "guard", index)
                ins = e.reciprocal(k.Pb[:, index, :], k.Pb[:, index, :])
            elif kind == "low":
                ins = s.low(k, e, at, index)
            else:
                w, c = index
                s.wait(k, e, at, "spread", index)
                z = k.R[:, w, c, :]
                ins = e.scalar_tensor_tensor(out=z, in0=z, scalar=1.0 if w else k.smul[:, c:c + 1],
                                             in1=k.bank(2 + c), op0=ALU.mult, op1=ALU.mult)
            ins.then_inc(k.done["dve"], 1)


def three(wh, wl, xh, xl):
    return [(wh, xh), (wh, xl), (wl, xh)]


class Attention(Ordered):

    PARTS = 3

    def __init__(s, H, khead, vhead, bias_loaded, tiles_of, V, Vz):
        s.V, s.Vz = V, Vz
        s.H, s.khead, s.vhead, s.bias_loaded, s.tiles_of = H, khead, vhead, bias_loaded, tiles_of
        s.biased = bias_loaded is not None
        s.dv = D // H
        s.per = H // C
        s.U = TT * H
        pe, act, dve = [], [], []
        pool = [("pad q", (0, p)) for p in range(2)]
        for h in range(H):
            pool += [("pad q", (h + 1, p)) for p in range(2) if h + 1 < H]
            pool += [("pad v", (h, p)) for p in range(2)]
        last = s.U - 1
        for t in range(s.U + 12):
            if t == 0:
                pe.append(("scores", 0))
            if t < last:
                pe.append(("scores", t + 1))
            if t - 1 in range(s.U):
                dve.append(("recip", t - 1))
            if t <= last:
                dve.append(("max", t))
                act.append(("exp", t))
            if t - 2 in range(s.U):
                dve.append(("low", t - 2))
            if t - 1 in range(s.U):
                dve.append(("high", t - 1))
            if t - 2 in range(s.U):
                pe.append(("turn high", t - 2))
                act.append(("copy high", t - 2))
            if t - 3 in range(s.U):
                pe.append(("turn low", t - 3))
                act.append(("copy low", t - 3))
            h, part = divmod(t - 7, TT)
            if h in range(H) and part < s.PARTS:
                pe.append(("values", (h, part)))
                if h % s.per == s.per - 1 and part == s.PARTS - 1:
                    act.append(("outcopy", h // s.per))
        s.number({"pe": pe, "act": act, "dve": dve, "pool": pool})

    def S(s, k, u):
        return k.bank((0, 1, 7)[u % 3])

    def width(s, u):
        return P * s.tiles_of(u % TT)

    def turned(s, k, u, p):
        return k.bank(2 + 2 * (u % 2) + p)[:, 0:s.width(u)]

    def pool(s, k, e, b, at):
        start_wait(k, e, at, "act", "dve", "pe", "pool")
        for kind, (h, p) in s.orders["pool"]:
            if kind == "pad q":
                if h >= 2:
                    s.wait(k, e, at, "scores", (h - 2) * TT + TT - 1)
                ins = e.tensor_tensor(k.Qz[p][:, h % 2, :], k.Q[p][:, h // s.per, :].bitcast(F32),
                                      k.heads[s.per][:, h % s.per:h % s.per + 1].to_broadcast([P, T]), ALU.mult)
            else:
                if h >= 2:
                    s.wait(k, e, at, "values", (h - 2, s.PARTS - 1))
                v = s.V[p][:, :, s.vhead(h) * s.dv:(s.vhead(h) + 1) * s.dv].bitcast(F32)
                shape = [P, TT, s.per, s.dv]
                ins = e.tensor_tensor(s.Vz[p][:, h % 2].rearrange("p j (a d) -> p j a d", a=s.per),
                                      v.unsqueeze(2).to_broadcast(shape),
                                      k.places[s.per][:, h % s.per].unsqueeze(1).unsqueeze(3).to_broadcast(shape),
                                      ALU.mult)
            ins.then_inc(k.done["pool"], 1)

    def pe(s, k, e, b, at):
        start_wait(k, e, at, "act", "dve", "pool")
        for kind, u in s.orders["pe"]:
            if kind != "values":
                h, i = divmod(u, TT)
                n = s.tiles_of(i)
            if kind == "scores":
                s.wait(k, e, at, "pad q", (h, 1))
                if u >= 3:
                    s.wait(k, e, at, "max" if s.biased else "exp", u - 3)
                w = P * max(n, 2)
                mats = three(*[k.Qz[p][:, h % 2, i * P:(i + 1) * P] for p in range(2)],
                             *[k.K[p][:, s.khead(h), 0:w] for p in range(2)])
                for m, (lhsT, rhs) in enumerate(mats):
                    mm = e.matmul(s.S(k, u)[:, 0:w], lhsT, rhs, start=m == 0, stop=m == 2)
            elif kind.startswith("turn"):
                p = int(kind == "turn low")
                s.wait(k, e, at, ("high", "low")[p], u)
                if u >= 2:
                    s.wait(k, e, at, ("copy high", "copy low")[p], u - 2)
                for j in range(n):
                    mm = e.transpose(s.turned(k, u, p)[:, j * P:(j + 1) * P].bitcast(F32R),
                                     k.Pr[p][:, u % 2, j * P:(j + 1) * P], k.identr[:])
            else:
                h, part = u
                if part == 0:
                    s.wait(k, e, at, "pad v", (h, 1))
                    s.wait(k, e, at, "copy low", h * TT + TT - 1)
                    if h % s.per == 0 and h >= s.per:
                        s.wait(k, e, at, "outcopy", h // s.per - 1)
                mats = []
                for j in range(TT):
                    first = min(q for q in range(TT) if s.tiles_of(q) > j) * P
                    mats += [(v, pt, first) for v, pt in
                             three(*[s.Vz[p][:, h % 2, j, :] for p in range(2)],
                                   *[k.PT[p][:, h % 2, j, first:T] for p in range(2)])]
                each = len(mats) // s.PARTS
                for m in range(part * each, (part + 1) * each):
                    lhsT, rhs, first = mats[m]
                    mm = e.matmul(k.bank(6)[:, first:T], lhsT, rhs,
                                  start=h % s.per == 0 and m == 0,
                                  stop=h % s.per == s.per - 1 and m == len(mats) - 1)
            mm.then_inc(k.done["pe"], 1)

    def dve(s, k, e, b, at):
        start_wait(k, e, at, "act", "dve", "pe", "pool")
        for kind, u in s.orders["dve"]:
            src = k.hN[:, u % C, 0:s.width(u)]
            high = k.Pr[0][:, u % 2, 0:s.width(u)]
            rsum = k.rsum[:, u:u + 1]
            if kind == "max":
                s.wait(k, e, at, "scores", u)
                if s.biased:
                    if u >= C:
                        s.wait(k, e, at, "low", u - C)
                    e.wait_ge(s.bias_loaded, 16)
                    ins = e.tensor_tensor_reduce(src, s.S(k, u)[:, 0:s.width(u)], k.bias[:, u % TT, 0:s.width(u)],
                                                 -1.0, 3.0e38, ALU.add, ALU.min, k.nmax[:, u:u + 1])
                else:
                    ins = e.tensor_reduce(k.nmax[:, u:u + 1], s.S(k, u)[:, 0:s.width(u)], AX_X, ALU.max, negate=True)
            elif kind == "recip":
                s.wait(k, e, at, "exp", u)
                ins = e.reciprocal(rsum, k.sums[:, u:u + 1])
            elif kind == "high":
                s.wait(k, e, at, "recip", u)
                if u >= 2:
                    s.wait(k, e, at, "turn high", u - 2)
                ins = e.tensor_scalar(high, src, rsum, None, ALU.mult)
            else:
                s.wait(k, e, at, "high", u)
                if u >= 2:
                    s.wait(k, e, at, "turn low", u - 2)
                ins = e.scalar_tensor_tensor(out=k.Pr[1][:, u % 2, 0:s.width(u)], in0=src, scalar=rsum,
                                             in1=high.bitcast(F32), op0=ALU.mult, op1=ALU.subtract)
            ins.then_inc(k.done["dve"], 1)

    def act(s, k, e, b, at):
        start_wait(k, e, at, "act", "dve", "pe", "pool")
        for kind, u in s.orders["act"]:
            h, i = divmod(u, TT)
            if kind == "exp":
                s.wait(k, e, at, "max", u)
                dst = k.hN[:, u % C, 0:s.width(u)]
                if not s.biased and u >= C:
                    s.wait(k, e, at, "low", u - C)
                ins = e.activation(dst, dst if s.biased else s.S(k, u)[:, 0:s.width(u)], ACT.Exp, bias=k.nmax[:, u:u + 1],
                                   scale=-1.0 if s.biased else 1.0, accum_out=k.sums[:, u:u + 1])
            elif kind.startswith("copy"):
                p = int(kind == "copy low")
                s.wait(k, e, at, ("turn high", "turn low")[p], u)
                if h >= 2:
                    s.wait(k, e, at, "values", (h - 2, s.PARTS - 1))
                ins = e.activation(k.PT[p][:, h % 2, 0:s.tiles_of(i), i * P:(i + 1) * P],
                                   s.turned(k, u, p).rearrange("p (j q) -> p j q", q=P), ACT.Copy)
            else:
                s.wait(k, e, at, "values", ((u + 1) * s.per - 1, s.PARTS - 1))
                ins = e.activation(k.t1[:, u, :], k.bank(6), ACT.Copy)
            ins.then_inc(k.done["act"], 1)


class Mlp(Ordered):

    def __init__(s, gated, pieces, loaded, hbias=None, gamma=None):
        s.gated, s.pieces, s.loaded, s.hbias, s.gamma = gated, pieces, loaded, hbias, gamma
        s.S = NCH * B
        s.ups = 2 if gated else 1
        pe, act, dve = [], [], []
        for p in range(len(pieces)):
            dve += [("high", p), ("low", p)]
        for st in range(s.S + 1):
            if st < s.S:
                pe += [("up", (st, t, w)) for t in range(2) for w in range(s.ups)]
                for t in range(2):
                    act.append(("act", (st, t)))
                    if gated:
                        dve.append(("gate", (st, t)))
                    act.append(("hidden high", (st, t)))
                    dve.append(("hidden low", (st, t)))
                j, b = divmod(st, B)
                if j + 1 < NCH and b in (1, 2):
                    for p in range(len(pieces)):
                        if b == 1 + p % 2:
                            dve += [("high", (j + 1) * len(pieces) + p), ("low", (j + 1) * len(pieces) + p)]
            if st >= 1:
                pe += [("down", (st - 1, m)) for m in range(C)]
                dve += [("add", (st - 1, m)) for m in range(C)]
        s.number({"pe": pe, "act": act, "dve": dve})

    def split_free(s, k, e, at, n):
        j = n // len(s.pieces)
        if j >= 2:
            s.wait(k, e, at, "down", ((j - 1) * B - 1, C - 1))

    def pe(s, k, e, b, at):
        start_wait(k, e, at, "act", "dve", "pool")
        for kind, index in s.orders["pe"]:
            if kind == "up":
                st, t, w = index
                j, q = divmod(st, B)
                if q == 0 and t == 0 and w == 0:
                    s.wait(k, e, at, "low", (j + 1) * len(s.pieces) - 1)
                if st >= 1:
                    s.wait(k, e, at, "gate" if s.gated else "act", (st - 1, t))
                    if not s.gated:
                        s.wait(k, e, at, "hidden high", (st - 1, t))
                mats = [m for c in range(C) for m in
                        three(*[s.up(v, j % 2, c, w, t) for v in range(2)], k.HH(q, c), k.HL(q, c))]
                for i, (lhsT, rhs) in enumerate(mats):
                    mm = e.matmul(k.bank(s.ups * t + w), lhsT, rhs, start=i == 0, stop=i == len(mats) - 1)
                mm.then_inc(k.done["pe"], 1)
            else:
                st, m = index
                j = st // B
                if m == 0:
                    s.wait(k, e, at, "hidden low", (st, 1))
                if st >= 1:
                    s.wait(k, e, at, "add", (st - 1, m))
                mats = [mt for t in range(2) for mt in
                        three(*[s.down(v, j % 2, t, m) for v in range(2)],
                              k.hidH[:, st % 2, t, :], k.hidL[:, st % 2, t, :])]
                for i, (lhsT, rhs) in enumerate(mats):
                    mm = e.matmul(k.bank(4 + m), lhsT, rhs, start=i == 0, stop=i == len(mats) - 1)
                mm.then_inc(k.done["pe"], 1)

    def act(s, k, e, b, at):
        start_wait(k, e, at, "act", "dve", "pe", "pool")
        for kind, (st, t) in s.orders["act"]:
            if kind == "act":
                s.wait(k, e, at, "up", (st, t, 0))
                if st >= 2:
                    s.wait(k, e, at, "hidden low", (st - 2, t))
                if s.gated:
                    if st >= 1:
                        s.wait(k, e, at, "gate", (st - 1, t))
                    ins = e.activation(k.t1[:, t, :], k.bank(2 * t), ACT.Silu)
                else:
                    ins = e.activation(k.hN[:, 2 * (st % 2) + t, :], k.bank(t), ACT.Gelu_apprx_tanh,
                                       bias=s.hbias[:, 2 * (st // B) + t:2 * (st // B) + t + 1], scale=1.0)
            else:
                s.wait(k, e, at, "gate" if s.gated else "act", (st, t))
                if st >= 2:
                    s.wait(k, e, at, "down", (st - 2, C - 1))
                ins = e.activation(k.hidH[:, st % 2, t, :], k.hN[:, 2 * (st % 2) + t, :], ACT.Copy)
            ins.then_inc(k.done["act"], 1)

    def dve(s, k, e, b, at):
        start_wait(k, e, at, "act", "dve", "pe", "pool")
        for kind, index in s.orders["dve"]:
            if kind == "high":
                sem, value = s.loaded(index)
                e.wait_ge(sem, value)
                s.split_free(k, e, at, index)
                j, p = divmod(index, len(s.pieces))
                o, w = s.pieces[p]
                ins = e.tensor_copy(k.Wsplit[0][:, j % 2, o:o + w], k.staged(index, w))
            elif kind == "low":
                s.wait(k, e, at, "high", index)
                j, p = divmod(index, len(s.pieces))
                o, w = s.pieces[p]
                ins = e.tensor_tensor(k.Wsplit[1][:, j % 2, o:o + w], k.staged(index, w),
                                      k.Wsplit[0][:, j % 2, o:o + w].bitcast(F32), ALU.subtract)
            elif kind == "gate":
                st, t = index
                s.wait(k, e, at, "act", index)
                s.wait(k, e, at, "up", (st, t, 1))
                if st >= 2:
                    s.wait(k, e, at, "hidden high", (st - 2, t))
                ins = e.tensor_tensor(k.hN[:, 2 * (st % 2) + t, :], k.t1[:, t, :], k.bank(2 * t + 1), ALU.mult)
            elif kind == "hidden low":
                st, t = index
                s.wait(k, e, at, "hidden high", index)
                if st >= 2:
                    s.wait(k, e, at, "down", (st - 2, C - 1))
                ins = e.tensor_tensor(k.hidL[:, st % 2, t, :], k.hN[:, 2 * (st % 2) + t, :],
                                      k.hidH[:, st % 2, t, :].bitcast(F32), ALU.subtract)
            else:
                st, m = index
                q = st % B
                s.wait(k, e, at, "down", index)
                if st >= B:
                    s.wait(k, e, at, "add", (st - B, m))
                ins = e.scalar_tensor_tensor(out=k.xs(q, m), in0=k.bank(4 + m),
                                             scalar=1.0 if s.gamma is None else s.gamma(q, m),
                                             in1=k.xs(q, m), op0=ALU.mult, op1=ALU.add)
            ins.then_inc(k.done["dve"], 1)


class Kit:
    pass


def conditioned_stack(nc, a, out):
    ctx = ExitStack()
    with ctx:
        def sb(name, shape, dt=F32):
            return ctx.enter_context(nc.sbuf_tensor("sb_" + name, shape, dt))

        def sem(name):
            return ctx.enter_context(nc.semaphore(name))

        k = Kit()
        psum = ctx.enter_context(nc.psum_tensor("banks", [P, 8, 512], F32))
        k.bank = lambda i: psum[:, i, :]
        x = sb("x", [P, C, B, T])
        k.hN = sb("hN", [P, C, T])
        k.t1 = sb("t1", [P, C, T])
        k.Pb = sb("Pb", [P, 2, T])
        k.sd, k.rstd = k.Pb[:, 0, :], k.Pb[:, 1, :]
        k.cosr = sb("cos", [P, T])
        k.sinr = sb("sin", [P, T])
        k.ident = sb("ident", [P, P])
        k.ones = sb("ones", [P, P])
        perm = sb("perm", [P, 2, P])
        k.heads = {2: sb("heads2", [P, 2])[:], 4: sb("heads4", [P, 4])[:]}
        k.places = {n: sb(f"places{n}", [P, n, n])[:] for n in (2, 4)}
        k.identr = sb("identr", [P, P], F32R)
        k.strip = sb("strip", [P, P + 4 * (C - 1)])
        k.freq = sb("freq", [P, 1])
        k.nmax = sb("nmax", [P, 64])
        k.sums = sb("sums", [P, 64])
        k.rsum = sb("rsum", [P, 64])
        k.smul = sb("smul", [P, C])
        cond = sb("cond", [P, 2, C, B])
        ADA = 48
        mod = sb("mod", [P, ADA, B])
        modb = sb("modb", [P, ADA])
        cols = sb("cols", [P, 80])
        eps5 = sb("eps5", [P, 1])
        eps6 = sb("eps6", [P, 1])
        comb = sb("comb", [P, 6, C, B])
        def over(scope, name, shape, dt=F32):
            return scope.enter_context(nc.sbuf_tensor("sb_" + name, shape, dt))

        with ExitStack() as inner:
            hide = over(inner, "experts", [P, ET, T])
        with ExitStack() as attention_scope:
            with ExitStack() as inner:
                k.Pr = [over(inner, f"Pr{i}", [P, 2, T], F32R) for i in range(2)]
                k.Qz = [over(inner, f"Qz{i}", [P, 2, T], F32R) for i in range(2)]
            k.R = over(attention_scope, "R", [P, 2, C, T])
            k.V = [over(attention_scope, f"V{i}", [P, TT, D], F32R) for i in range(2)]
            k.Q = [over(attention_scope, f"Q{i}", [P, C, T], F32R) for i in range(2)]
            k.K = [over(attention_scope, f"K{i}", [P, C, T], F32R) for i in range(2)]
            with ExitStack() as inner:
                over(inner, "W_used", [P, 8192])
                Vz2 = [over(inner, f"Vz{i}", [P, 2, TT, P], F32R) for i in range(2)]
            W = over(attention_scope, "W", [P, 10240])
            k.bias = over(attention_scope, "bias", [P, TT, T])
            with ExitStack() as inner:
                k.scratch = over(inner, "scratch", [P, 4, T])
            k.PT = [over(attention_scope, f"PT{i}", [P, 2, TT, T], F32R) for i in range(2)]
        with ExitStack() as scope:
            Hs = [over(scope, f"H{i}", [P, C, B, T], F32R) for i in range(2)]
            k.Wsplit = [over(scope, f"Ws{i}", [P, 2, 3072], F32R) for i in range(2)]
            k.hidH = over(scope, "hidH", [P, 2, 2, T], F32R)
            k.hidL = over(scope, "hidL", [P, 2, 2, T], F32R)
            k.WM = over(scope, "WM", [P, 2, 2048])
        Vflat = [v[:].rearrange("p j d -> p (j d)") for v in k.V]
        narrow = [v[:, 0:TT * P].rearrange("p (j d) -> p j d", j=TT) for v in Vflat]
        Vz = [v[:, TT * P:3 * TT * P].rearrange("p (s j d) -> p s j d", s=2, j=TT) for v in Vflat]
        W0, W1 = W[:, 0:8192], W[:, 5248:10240]
        k.HH = lambda b, c: Hs[0][:, c, b, :]
        k.HL = lambda b, c: Hs[1][:, c, b, :]
        k.staged = lambda n, w: k.WM[:, n % 2, 0:w]
        k.cost, k.sint = k.scratch[:, 0, :], k.scratch[:, 1, :]
        vbias = k.cosr[:]
        k.pos = k.bias[:, :, :].bitcast(I32)
        k.ropet = k.scratch[:, :, :]

        k.done = {n: sem(n + "_done") for n in NAMES}
        l_x, l_const, l_cond = sem("l_x"), sem("l_const"), sem("l_cond")
        l_w = [sem(f"l_w{i}") for i in range(4)]
        l_down3 = sem("l_down3")
        l_bias = [sem(f"l_bias{i}") for i in range(2)]
        k.l_pos = sem("l_pos")
        l_vb = sem("l_vb")
        l_m = [sem(f"l_m{i}") for i in range(2)]
        s_zero = sem("s_zero")
        s_out = sem("s_out")

        one = lambda b: bass.ds(b, 1)
        k.xs = lambda b, c: x[:, c, one(b), :].rearrange("p o t -> p (o t)")
        modc = lambda tile: (lambda b, c: mod[:, tile + c, one(b)])
        combc = lambda i: (lambda b, c: comb[:, i, c, one(b)])
        hN = lambda b, c: k.hN[:, c, :]
        R = lambda i, c: k.R[:, i, c, :]

        COLS = [("L1_cond_ln1_w", 4), ("L1_cond_ln2_w", 4), ("L2_cond_q_bias", 4), ("L2_cond_bproj", 4),
                ("L2_cond_bfc1", 16), ("L2_cond_bfc2", 4), ("L3_cond_b1", 16), ("L3_cond_b2", 4),
                ("L3_cond_ln_g", 4), ("L3_cond_ln_b", 4), ("L3_cond_out_b", 4)]
        col, o = {}, 0
        for name, n in COLS:
            col[name] = cols[:, o:o + n]
            o += n
        MODB = [("L0_cond_b_ada", 0, 8), ("L2_cond_bada", 16, 24), ("L3_cond_emb_b", 40, 8)]

        def view(w, base, width, n=C):
            return w[:, base:base + n * width].rearrange("p (c m) -> p c m", c=n)

        wq0, wkd, wo0 = view(W0, 0, D), view(W0, 2048, P), view(W0, 2560, D)
        wku, wvu = W0[:, 4608:5120], W0[:, 5120:5248]
        wq1, wk1, wv1, wo1 = view(W1, 0, D), view(W1, 2048, P), view(W1, 2560, 64), view(W1, 2816, D)
        wqkv2, wo2 = view(W0, 0, 3 * D), view(W0, 6144, D)
        w1e, w2e = view(W, 0, P, ET), view(W, 2048, P, ET)
        wout3 = view(W, 4096, D)

        def rows(name):
            return a[name].rearrange("(c p) m -> p c m", p=P)

        def copies(dst, scale=lambda g: 1.0, bias=None):
            def put_act(e, b, g, bank):
                if bias is None:
                    return e.activation(dst(b, g), bank, ACT.Copy, scale=scale(g))
                return e.activation(dst(b, g), bank, ACT.Identity, bias=bias(g), scale=scale(g))

            def put_dve(e, b, g, bank):
                return e.tensor_scalar(dst(b, g), bank, scale(g), None if bias is None else bias(g), ALU.mult,
                                       ALU.bypass if bias is None else ALU.add)
            return put_act, put_dve

        def residual(bias=None, gamma=None):
            def put_dve(e, b, g, bank):
                if gamma is not None:
                    return e.scalar_tensor_tensor(out=k.xs(b, g), in0=bank, scalar=gamma(b, g),
                                                  in1=k.xs(b, g), op0=ALU.mult, op1=ALU.add)
                return e.scalar_tensor_tensor(out=k.xs(b, g), in0=bank, scalar=0.0 if bias is None else bias(g),
                                              in1=k.xs(b, g), op0=ALU.add, op1=ALU.add)
            return None, put_dve

        def dense(w, src):
            return lambda b, g: [(w[:, c, g * P:(g + 1) * P], src(c)) for c in range(C)]

        hsrc = lambda c: k.hN[:, c, :]
        asrc = lambda c: k.t1[:, c, :]

        ADA_BLOCKS = ADA * P // D

        class Ada(Ordered):

            def __init__(s):
                pe, act = [], [("silu", 0)]
                for j in range(ADA_BLOCKS + 1):
                    if j < ADA_BLOCKS:
                        pe.append(("block", j))
                        act.append(("row", j))
                    if j >= 1:
                        pe.append(("turn", j - 1))
                act.append(("scales", 0))
                s.number({"pe": pe, "act": act, "dve": [("eps", 0), ("eps", 1)]})

            def pe(s, k, e, b, at):
                e.wait_ge(l_cond, 16)
                for kind, j in s.orders["pe"]:
                    if kind == "block":
                        if j == 4:
                            s.wait(k, e, at, "silu", 0)
                        if j >= 2:
                            s.wait(k, e, at, "row", j - 2)
                        e.wait_ge(l_m[j % 2], 16 * (j // 2 + 1))
                        w = k.WM[:, j % 2, 0:C * D].rearrange("p (c m) -> p c m", c=C)
                        for c in range(C):
                            mm = e.matmul(k.bank(1 + j % 2)[0:B, :], cond[:, int(j >= 4), c, :], w[:, c, :],
                                          start=c == 0, stop=c == C - 1)
                    else:
                        if j == 0:
                            e.wait_ge(l_const, 16 * n_const)
                        s.wait(k, e, at, "row", j)
                        for t in range(4):
                            mm = e.transpose(k.bank(0)[:, B * (4 * j + t):B * (4 * j + t + 1)],
                                             k.hN[0:B, j % C, t * P:(t + 1) * P], k.ident[0:B, 0:B])
                    mm.then_inc(k.done["pe"], 1)

            def act(s, k, e, b, at):
                e.wait_ge(l_cond, 16)
                for kind, j in s.orders["act"]:
                    if kind == "silu":
                        ins = e.activation(cond[:, 1, :, :], cond[:, 0, :, :], ACT.Silu)
                    elif kind == "row":
                        s.wait(k, e, at, "block", j)
                        if j >= C:
                            s.wait(k, e, at, "turn", j - C)
                        ins = e.activation(k.hN[0:B, j % C, :], k.bank(1 + j % 2)[0:B, :], ACT.Copy)
                    else:
                        e.wait_ge(l_const, 16 * n_const)
                        ins = e.activation(k.smul[:], k.smul[:], ACT.Exp)
                    ins.then_inc(k.done["act"], 1)

            def dve(s, k, e, b, at):
                e.memset(eps5[:], 1e-5).then_inc(k.done["dve"], 1)
                e.memset(eps6[:], 1e-6).then_inc(k.done["dve"], 1)

        ada = Ada()

        class Mods(Step):
            n = {"dve": 14}

            def dve(s, k, e, b, at):
                done = [0]

                def inc(ins):
                    done[0] += 1
                    ins.then_inc(k.done["dve"], 1)
                    e.wait_ge(k.done["dve"], at["dve"] + done[0])

                def wide(ap):
                    return ap.unsqueeze(2).to_broadcast([P, C, B])

                start_wait(k, e, at, "pe", "dve", "act")
                e.wait_ge(l_const, 16 * n_const)
                inc(e.tensor_copy(k.identr[:], k.ident[:]))
                inc(e.tensor_copy(mod[:].rearrange("p t b -> p (t b)"), k.bank(0)[:, 0:ADA * B]))
                inc(e.tensor_tensor(mod[:], mod[:], modb[:].unsqueeze(2).to_broadcast([P, ADA, B]), ALU.add))
                for t0, n in ((0, 4), (8, 8), (24, 8), (40, 4)):
                    m = mod[:, t0:t0 + n, :]
                    inc(e.tensor_scalar(m, m, 1.0, None, ALU.add))
                inc(e.tensor_tensor(comb[:, 0], mod[:, 8:12, :], wide(col["L1_cond_ln1_w"]), ALU.mult))
                inc(e.tensor_tensor(comb[:, 1], mod[:, 12:16, :], wide(col["L1_cond_ln2_w"]), ALU.mult))
                inc(e.tensor_tensor(comb[:, 2], mod[:, 20:24, :], wide(col["L2_cond_bfc2"]), ALU.mult))
                inc(e.tensor_tensor(comb[:, 5], mod[:, 16:20, :], wide(col["L2_cond_bproj"]), ALU.mult))
                inc(e.tensor_tensor(comb[:, 3], mod[:, 40:44, :], wide(col["L3_cond_ln_g"]), ALU.mult))
                inc(e.tensor_tensor(comb[:, 4], mod[:, 40:44, :], wide(col["L3_cond_ln_b"]), ALU.mult))
                inc(e.tensor_tensor(comb[:, 4], comb[:, 4], mod[:, 44:48, :], ALU.add))
                assert done[0] == s.n["dve"], done

        split_q = [(R(0, c), k.Q[0][:, c], k.Q[1][:, c]) for c in range(C)]
        split_k = [(R(1, c), k.K[0][:, c], k.K[1][:, c]) for c in range(C)]

        def v_at(layer, j):
            return {0: k.t1[:, 1, j * P:(j + 1) * P], 1: k.R[:, 1, 1, j * 64:(j + 1) * 64], 2: k.t1[:, j, :]}[layer]

        def split_v(layer):
            V, width = ((narrow, P), (narrow, 64), (k.V, D))[layer]
            return [(v_at(layer, j), V[0][:, j, 0:width], V[1][:, j, 0:width]) for j in range(TT)]

        put_v = lambda layer: copies(lambda b, g: v_at(layer, g))

        all_tiles = lambda i: TT
        latent = k.t1[:, 0, :]
        inv_root = float(1 / np.sqrt(np.float32(32)))

        layer0 = [
            Norm(k.xs, modc(0), modc(4), eps5[:, 0:1]),
            joined(Linear(1, lambda b, g: [(wkd[:, c, :], hsrc(c)) for c in range(C)],
                          *copies(lambda b, g: latent)),
                   Linear(C, dense(wq0, hsrc), *copies(lambda b, g: R(0, g), lambda g: inv_root)),
                   load=(l_w[0], 80), ready=("act", 0)),
            joined(Linear(TT, lambda b, g: [(latent[:, g * P:(g + 1) * P], wvu)], *put_v(0), width=P),
                   Linear(C, lambda b, g: [(wku[:, g * P:(g + 1) * P], latent)], *copies(lambda b, g: R(1, g)))),
            Rope(split_q + split_k, split_v(0), perm[:, 0, :], k.cosr[:], k.sinr[:]),
            Attention(16, lambda h: h // 4, lambda h: h // 4, l_bias[0], lambda i: i + 1, narrow, Vz),
            Linear(C, dense(wo0, asrc), *residual(), only="dve"),
        ]

        projections1 = joined(
            Linear(TT, lambda b, g: [(k.hN[:, c, g * P:(g + 1) * P], wv1[:, c, :]) for c in range(C)],
                   *put_v(1), width=64),
            Linear(C, dense(wq1, hsrc), *copies(lambda b, g: R(0, g), lambda g: 0.125)),
            Linear(1, lambda b, g: [(wk1[:, c, :], hsrc(c)) for c in range(C)], *copies(lambda b, g: R(1, 0))),
            only="act", load=(l_w[1], 64), ready=("dve", 0))
        layer1a = [
            Norm(k.xs, combc(0), None, eps6[:, 0:1], rms=True),
            projections1,
            Angles(beside=projections1),
            Rope(split_q + split_k[:1], split_v(1), perm[:, 1, :], k.cosr[:], k.sinr[:]),
            Attention(8, lambda h: 0, lambda h: 0, None, all_tiles, narrow, Vz),
            Linear(C, dense(wo1, asrc), *residual(), only="dve"),
        ]
        norm1b = [Norm(k.xs, combc(1), None, eps6[:, 0:1], rms=True, pair=(k.HH, k.HL))]

        def put_v2(e, b, g, bank):
            if b == 0 and g == 0:
                e.wait_ge(l_vb, 32)
            return e.tensor_tensor(v_at(2, g), bank, vbias, ALU.add)

        layer2a = [
            Norm(k.xs, modc(24), modc(32), eps6[:, 0:1], extra=combc(5)),
            joined(Linear(TT, lambda b, g: [(k.hN[:, c, g * P:(g + 1) * P], wqkv2[:, c, 2 * D:3 * D])
                                            for c in range(C)], None, put_v2),
                   Linear(C, dense(wqkv2, hsrc), *copies(lambda b, g: R(0, g),
                                                         bias=lambda g: col["L2_cond_q_bias"][:, g:g + 1])),
                   Linear(C, lambda b, g: dense(wqkv2, hsrc)(b, g + C), *copies(lambda b, g: R(1, g))),
                   only=["dve"] * TT + ["act"] * 2 * C, load=(l_w[2], 32), ready=("act", C)),
            QKNorm(split_q + split_k, split_v(2)),
            Attention(16, lambda h: h // 4, lambda h: h, l_bias[1], all_tiles, k.V, Vz2),
            Linear(C, dense(wo2, asrc), *residual(gamma=modc(16)), only="dve"),
        ]
        norm2b = [Norm(k.xs, modc(28), modc(36), eps6[:, 0:1], pair=(k.HH, k.HL), extra=combc(2))]

        gelu_bias = col["L3_cond_b1"]

        def gelu_put(e, b, g, bank):
            return e.activation(hide[:, g, :], bank, ACT.Gelu, bias=gelu_bias[:, g:g + 1], scale=1.0)

        layer3 = [
            Linear(ET, lambda b, g: [(w1e[:, g, :], k.xs(b, g // 4))], gelu_put, None, only="act",
                   load=(l_w[3], 16 * 8)),
            Linear(C, lambda b, g: [(w2e[:, 4 * g + i, :], hide[:, 4 * g + i, :]) for i in range(4)],
                   *copies(hN, bias=lambda g: col["L3_cond_b2"][:, g:g + 1]), load=(l_down3, 16 * 9)),
            Norm(hN, combc(3), combc(4), eps5[:, 0:1], func=ACT.Silu, early=False),
            Linear(C, dense(wout3, hsrc), *residual(lambda g: col["L3_cond_out_b"][:, g:g + 1]), only="dve",
                   ready=("act", 0)),
        ]

        l_m_at, seen = {1: [], 2: []}, [16 * 6, 16 * 6]
        for layer, loads in ((1, [2, 1] * NCH), (2, [2] * NCH)):
            for n, m in enumerate(loads):
                seen[n % 2] += 16 * m
                l_m_at[layer].append(seen[n % 2])

        def up(layer_ups):
            return lambda v, slot, c, w, t: k.Wsplit[v][:, slot, (c * layer_ups + w) * HC + t * P:
                                                        (c * layer_ups + w) * HC + (t + 1) * P]

        def down(base):
            return lambda v, slot, t, m: k.Wsplit[v][:, slot, base + t * D + m * P:base + t * D + (m + 1) * P]

        phases = [([ada, Mods()], False), (layer0, True), (layer1a, True), (norm1b, True)]
        mlp1 = Mlp(True, [(0, 2 * C * HC), (2 * C * HC, 2 * D)], loaded=lambda n: (l_m[n % 2], l_m_at[1][n]))
        mlp2 = Mlp(False, [(0, 2 * C * HC)], loaded=lambda n: (l_m[n % 2], l_m_at[2][n]),
                   hbias=col["L2_cond_bfc1"], gamma=modc(20))
        mlp1.up, mlp1.down = up(2), down(2 * C * HC)
        mlp2.up, mlp2.down = up(1), down(C * HC)
        phases.append(([mlp1], False))
        phases += [(layer2a, True), (norm2b, True)]
        phases.append(([mlp2], False))
        phases.append((layer3, True))

        starts, total = [], dict.fromkeys(NAMES, 0)
        for stages, looped in phases:
            starts.append(dict(total))
            for n in NAMES:
                total[n] += (B if looped else 1) * sum(st.n.get(n, 0) for st in stages)
        starts.append(dict(total))
        L1P, M1P, L2P, M2P, L3P = 2, 4, 5, 7, 8

        PICK = {"pe": lambda st: st.pe, "act": lambda st: st.act, "dve": lambda st: st.dve,
                "pool": lambda st: st.pool}

        n_const = 11 + len(COLS) + len(MODB) + 1

        def wait_all(e, p):
            for name in NAMES:
                if starts[p][name]:
                    e.wait_ge(k.done[name], starts[p][name])

        def engine(e, name, first, last):
            for (stages, looped), start in list(zip(phases, starts))[first:last]:
                if not any(st.n.get(name, 0) or st.n == {} for st in stages):
                    continue
                per = {n: sum(st.n.get(n, 0) for st in stages) for n in NAMES}

                def body(b):
                    at = {n: start[n] + (b * per[n] if looped else 0) for n in NAMES}
                    for st in stages:
                        PICK[name](st)(k, e, b, at)
                        at = {n: at[n] + st.n.get(n, 0) for n in NAMES}
                if looped:
                    for b in range(B):
                        body(b)
                else:
                    body(0)

        block = ctx.enter_context(nc.Block())

        @block.sync
        def _(e):
            e.dma_start(cond[:, 0, :, :], a["condT"].rearrange("(c p) b -> p c b", p=P)).then_inc(l_cond, 16)
            blocks = [("L0_cond_W_ada", 2), ("L1_cond_ln1_tw", 1), ("L1_cond_ln2_tw", 1), ("L2_cond_Wada", 6),
                      ("L3_cond_emb_W", 2)]
            n = 0
            for name, count in blocks:
                for j in range(count):
                    if n >= 2:
                        e.wait_ge(k.done["pe"], ada.i[("block", n - 2)][1])
                    e.dma_start(k.WM[:, n % 2, 0:C * D].rearrange("p (c m) -> p c m", c=C),
                                rows(name)[:, :, j * D:(j + 1) * D]).then_inc(l_m[n % 2], 16)
                    n += 1
                    if n == 1:
                        for c in range(C):
                            e.dma_start(x[:, c, :, :], a["x"][c * P:(c + 1) * P]).then_inc(l_x, 16)

            def wait_phase(p):
                for name in NAMES:
                    if starts[p][name]:
                        e.wait_ge(k.done[name], starts[p][name])

            def slot_free(stage, phase, n):
                name, i = stage.i[("low", n - 2)]
                e.wait_ge(k.done[name], starts[phase][name] + i)

            for j in range(NCH):
                if j == 0:
                    wait_phase(L1P + 1)
                else:
                    slot_free(mlp1, M1P, 2 * j)
                wup = k.WM[:, 0, :].rearrange("p (c w m) -> p c w m", c=C, w=2)
                for w, name in enumerate(("L1_cond_Wg", "L1_cond_Wu")):
                    e.dma_start(wup[:, :, w, :], rows(name)[:, :, j * HC:(j + 1) * HC]).then_inc(l_m[0], 16)
                if j:
                    slot_free(mlp1, M1P, 2 * j + 1)
                e.dma_start(k.WM[:, 1, 0:2 * D].rearrange("p (t m) -> p t m", t=2),
                            rows("L1_cond_Wd")[:, 2 * j:2 * j + 2, :]).then_inc(l_m[1], 16)
            for j in range(NCH):
                if j < 2:
                    wait_phase(M2P - 1)
                else:
                    slot_free(mlp2, M2P, j)
                e.dma_start(k.WM[:, j % 2, 0:C * HC].rearrange("p (c m) -> p c m", c=C),
                            rows("L2_cond_Wfc1")[:, :, j * HC:(j + 1) * HC]).then_inc(l_m[j % 2], 16)
                e.dma_start(k.WM[:, j % 2, C * HC:C * HC + 2 * D].rearrange("p (t m) -> p t m", t=2),
                            rows("L2_cond_Wfc2")[:, 2 * j:2 * j + 2, :]).then_inc(l_m[j % 2], 16)
            wait_phase(L3P)
            e.wait_ge(s_zero, 2)
            for half in range(2):
                src1 = a["L3_cond_W1"].rearrange("(q h) l (t f) -> h l q t f", h=2, t=2)[half]
                dst1 = w1e[64 * half:64 * half + 64].rearrange("l (q h t) f -> l q h t f", h=2, t=2)[:, :, half]
                for q in range(4):
                    e.dma_start(dst1[:, q], src1[:, q]).then_inc(l_w[3], 16)
            per = sum(st.n.get("dve", 0) for st in layer3)
            for b in range(B):
                e.wait_ge(k.done["dve"], starts[L3P]["dve"] + (b + 1) * per)
                e.dma_start(out[:, :, b, :], x[:, :, b, :]).then_inc(s_out, 16)
            e.wait_ge(s_out, 16 * B)

        @block.gpsimd
        def _(e):
            e.dma_start(k.ident[:], a["ident"]).then_inc(l_const, 16)
            e.dma_start(k.ones[:], a["ones"]).then_inc(l_const, 16)
            e.dma_start(k.strip[:], a["strip"]).then_inc(l_const, 16)
            e.dma_start(perm[:], a["perm"].rearrange("w p m -> p w m")).then_inc(l_const, 16)
            e.dma_start(k.cosr[:], a["cos0"]).then_inc(l_const, 16)
            e.dma_start(k.sinr[:], a["sin0"]).then_inc(l_const, 16)
            e.dma_start(k.freq[:], a["freq"]).then_inc(l_const, 16)
            e.dma_start(k.heads[2], a["heads2"]).then_inc(l_const, 16)
            e.dma_start(k.heads[4], a["heads4"]).then_inc(l_const, 16)
            for n in (2, 4):
                e.dma_start(k.places[n], a[f"places{n}"]).then_inc(l_const, 16)
            for name, _ in COLS:
                e.dma_start(col[name], a[name]).then_inc(l_const, 16)
            e.dma_start(k.smul[:], a["L2_cond_scale_mul_log"]).then_inc(l_const, 16)
            e.memset(modb[:], 0.0).then_inc(s_zero, 1)
            e.wait_ge(s_zero, 1)
            for name, t0, n in MODB:
                e.dma_start(modb[:, t0:t0 + n], a[name]).then_inc(l_const, 16)
            e.dma_start(k.bias[:], a["mask0"].rearrange("(i p) t -> p i t", p=P)).then_inc(l_bias[0], 16)
            for dst, name in ((wq0, "L0_cond_Wq"), (wkd, "L0_cond_Wkd"), (wo0, "L0_cond_Wo")):
                e.dma_start(dst, rows(name)).then_inc(l_w[0], 16)
            e.dma_start(wku, a["L0_cond_Wku"]).then_inc(l_w[0], 16)
            e.dma_start(wvu, a["L0_cond_Wvu"]).then_inc(l_w[0], 16)
            for dst, name in ((wq1, "L1_cond_Wq"), (wk1, "L1_cond_Wk"), (wv1, "L1_cond_Wv"), (wo1, "L1_cond_Wo")):
                e.dma_start(dst, rows(name)).then_inc(l_w[1], 16)
            engine(e, "pool", 0, L1P)
            wait_all(e, L1P)
            e.dma_start(k.pos, a["pos"].rearrange("b t -> (b t)").partition_broadcast(P)
                        .rearrange("p (b t) -> p b t", b=B)).then_inc(k.l_pos, 16)
            engine(e, "pool", L1P, L2P)
            wait_all(e, L2P)
            e.dma_start(wqkv2, rows("L2_cond_Wqkv")).then_inc(l_w[2], 16)
            e.dma_start(wo2, rows("L2_cond_Wproj")).then_inc(l_w[2], 16)
            e.dma_start(k.bias[:], a["mask"].rearrange("(i p) t -> p i t", p=P)).then_inc(l_bias[1], 16)
            e.dma_start(vbias, a["L2_cond_v_bias"].rearrange("o d -> (o d)").partition_broadcast(P))\
                .then_inc(l_vb, 16)
            e.dma_start(k.sinr[:], a["spread"]).then_inc(l_vb, 16)
            engine(e, "pool", L2P, L3P)
            wait_all(e, L3P)
            e.memset(W[:, 0:2048], 0.0).then_inc(s_zero, 1)
            e.memset(W[:, 2048:4096], 0.0).then_inc(s_zero, 1)
            e.wait_ge(s_zero, 3)
            for half in range(2):
                src2 = a["L3_cond_W2"].rearrange("(q h) (t p) l -> h p q t l", h=2, t=2)[half]
                dst2 = w2e.rearrange("p (q h t) l -> p q h t l", h=2, t=2)[:, :, half, :,
                                                                          64 * half:64 * half + 64]
                for q in range(4):
                    e.dma_start(dst2[:, q], src2[:, q]).then_inc(l_down3, 16)
            e.dma_start(wout3, rows("L3_cond_out_W")).then_inc(l_down3, 16)
            engine(e, "pool", L3P, len(phases))

        @block.tensor
        def _(e):
            engine(e, "pe", 0, 1)
            e.wait_ge(l_x, 16 * C)
            e.wait_ge(l_const, 16 * n_const)
            engine(e, "pe", 1, len(phases))

        @block.vector
        def _(e):
            engine(e, "dve", 0, 1)
            e.wait_ge(l_x, 16 * C)
            engine(e, "dve", 1, len(phases))

        @block.scalar
        def _(e):
            engine(e, "act", 0, 1)
            e.wait_ge(l_x, 16 * C)
            engine(e, "act", 1, len(phases))


def _layout(inputs):
    g = {n: np.asarray(v) for n, v in inputs.items()}
    T_ = lambda w: np.ascontiguousarray(w.T)
    column = lambda v: np.ascontiguousarray(v.reshape(-1, P).T)
    o = {"x": np.ascontiguousarray(g["x"].transpose(2, 0, 1)), "condT": T_(g["cond_2048"]),
         "pos": g["pos_BxS"], "mask": np.ascontiguousarray(g["mask_1x1xSxS_ff0"][0, 0])}
    for n in ("L0_cond_W_ada", "L0_cond_Wq", "L0_cond_Wkd", "L0_cond_Wvu", "L0_cond_Wo", "L1_cond_ln1_tw",
              "L1_cond_ln2_tw", "L1_cond_Wq", "L1_cond_Wv", "L1_cond_Wo", "L1_cond_Wg", "L1_cond_Wu",
              "L1_cond_Wd", "L2_cond_Wqkv", "L2_cond_Wproj", "L2_cond_Wada", "L2_cond_Wfc1", "L2_cond_Wfc2"):
        o[n] = T_(g[n])
    o["L0_cond_Wku"] = T_(np.repeat(g["L0_cond_Wku"].reshape(4, 1, 32, P), 4, axis=1).reshape(D, P))
    o["L1_cond_Wk"] = T_(np.concatenate([g["L1_cond_Wk"]] * 2))
    for n in ("L3_cond_emb_W", "L3_cond_W1", "L3_cond_W2", "L3_cond_out_W"):
        o[n] = g[n]
    for n in ("L1_cond_ln1_w", "L1_cond_ln2_w", "L2_cond_q_bias", "L2_cond_bproj", "L2_cond_bfc1",
              "L2_cond_bfc2", "L3_cond_b1", "L3_cond_b2", "L3_cond_ln_g", "L3_cond_ln_b", "L3_cond_out_b",
              "L0_cond_b_ada", "L2_cond_bada", "L3_cond_emb_b"):
        o[n] = column(g[n])
    o["L2_cond_v_bias"] = g["L2_cond_v_bias"].reshape(1, D)
    o["L2_cond_scale_mul_log"] = column(np.repeat(g["L2_cond_scale_mul_log"].reshape(16), 32))
    return {n: np.ascontiguousarray(v) for n, v in o.items()}


def _constants():
    f = np.float32
    eye = np.eye(P, dtype=f)
    o = {"ident": eye, "ones": np.full((P, P), 1 / D, f)}
    o["strip"] = np.zeros((P, P + 4 * (C - 1)), f)
    o["strip"][:, 4 * (C - 1):4 * C] = np.kron(np.eye(4), np.ones((32, 1)))
    o["spread"] = np.zeros((P, T), f)
    o["spread"][:16] = np.kron(np.eye(16), np.ones((1, 32)))
    o["perm"] = np.stack([np.kron(np.eye(P // d), np.roll(np.eye(d), d // 2, axis=0)).astype(f)
                          for d in (32, 64)])
    row = np.arange(P)
    f32 = (1.0 / f(10000.0) ** (np.arange(0, 32, 2, dtype=f) / f(32))).astype(f)
    ang = (np.arange(T, dtype=f)[None, :] * f32[row % 16][:, None]).astype(f)
    sgn = np.where(row % 32 < 16, -1, 1).astype(f)[:, None]
    o["cos0"], o["sin0"] = np.cos(ang), np.sin(ang) * sgn
    f64 = (1.0 / f(10000.0) ** (np.arange(0, 64, 2, dtype=f) / f(64))).astype(f)
    o["freq"] = (f64[row % 32] * np.where(row % 64 < 32, -1, 1))[:, None]
    o["heads2"], o["heads4"] = np.kron(np.eye(2), np.ones((64, 1))), np.kron(np.eye(4), np.ones((32, 1)))
    for n in (2, 4):
        o[f"places{n}"] = np.broadcast_to(np.eye(n), (P, n, n))
    i = np.arange(T)
    hidden = (np.abs(i[None] - i[:, None]) > 64) & ~(i % 64 == 0)[None] | (i[None] // P > i[:, None] // P)
    o["mask0"] = np.where(hidden, f(-1e30), f(0))
    return {n: np.ascontiguousarray(v, dtype=f) for n, v in o.items()}


def kernel(**inputs):
    import concourse.bacc as _bacc
    from concourse.bass_utils import run_bass_kernel_spmd as _run

    nc = _bacc.Bacc("TRN2", target_bir_lowering=False, num_devices=1)
    arrays, aps = {}, {}
    for name, v in {**_layout(inputs), **_constants()}.items():
        arrays["in_" + name] = v
        aps[name] = nc.dram_tensor("in_" + name, v.shape, mybir.dt.from_np(v.dtype), kind="ExternalInput").ap()
    out = nc.dram_tensor("out_x", (P, C, B, T), F32, kind="ExternalOutput").ap()
    conditioned_stack(nc, aps, out)
    r = _run(nc, [arrays], core_ids=[0])
    return np.ascontiguousarray(r.results[0]["out_x"].transpose(2, 3, 1, 0)).reshape(B, T, D)
```
